# Optimizing a Trainium2 kernel written in Bass

```python
import numpy as np
import jax
import jax.numpy as jnp

def _softmax(x, axis=-1):
    return jax.nn.softmax(x, axis=axis)

def _gelu(x):
    return jax.nn.gelu(x, approximate=True)

def _silu(x):
    return jax.nn.silu(x)

def _sigmoid(x):
    return jax.nn.sigmoid(x)

def _layernorm(x, axis=-1, eps=1e-05):
    m = jnp.mean(x, axis=axis, keepdims=True)
    v = jnp.var(x, axis=axis, keepdims=True)
    return (x - m) / jnp.sqrt(v + eps)

def _scatter_add(tgt, idx, src, axis=0):
    return tgt.at[idx].add(src)

def _segment_sum(src, seg, n):
    return jax.ops.segment_sum(src, seg, n)
kernel_name = 'mk_seq_postln_d1_jaxref_r8_c46e59'

def setup_inputs(seed: int=0):
    np.random.seed(seed)
    _w = jnp.asarray

    def _L0_attn_setup():
        import jax, jax.numpy as jnp
        import numpy as np
        B, T, C, H = (2, 128, 128, 16)
        D = C // H
        EPS = 1e-06
        key = jax.random.key(seed)
        k1, k2, k3, k4, k5 = jax.random.split(key, 5)
        s = 0.02
        return {'x': jax.random.normal(k1, (B, T, C), dtype=jnp.float32), 'w_qkv': jax.random.normal(k2, (3 * C, C), dtype=jnp.float32) * s, 'b_qkv': jax.random.normal(k3, (3 * C,), dtype=jnp.float32) * s, 'w_out': jax.random.normal(k4, (C, C), dtype=jnp.float32) * s, 'b_out': jax.random.normal(k5, (C,), dtype=jnp.float32) * s}
    _L0_attn_in = _L0_attn_setup()

    def _L0_ffn_setup():
        import jax, jax.numpy as jnp
        import numpy as np
        B, S, H, F, E, K = (4, 256, 128, 448, 8, 2)
        CAP_FACTOR = 1.25

        def _moe_forward(hidden_states, gate_w, w1, w2, w3):
            b, s, h = hidden_states.shape
            dtype = hidden_states.dtype
            x = hidden_states.reshape(-1, h)
            router_logits = x @ gate_w.T
            expert_weights = jax.nn.softmax(router_logits.astype(jnp.float32), axis=1)
            _, selected_experts = jax.lax.top_k(expert_weights, K)
            top_k_idx = selected_experts.reshape(b, s, K)
            probs = expert_weights.reshape(b, s, E)
            capacity = int(s * K / E * CAP_FACTOR)
            expert_mask = jax.nn.one_hot(top_k_idx, E, dtype=jnp.int32)
            mask_fused = expert_mask.reshape(b, s * K, E)
            count_fused = jnp.cumsum(mask_fused, axis=1)
            count = count_fused.reshape(b, s, K, E)
            trunc_mask = expert_mask * (count <= capacity).astype(jnp.int32)
            combined_mask = trunc_mask.sum(axis=2)
            masked_probs = probs * combined_mask
            pos_fused = mask_fused * count_fused
            pos = pos_fused.reshape(b, s, K, E)
            combined_pos = pos.sum(axis=2) * combined_mask
            pos_in_cap = jax.nn.one_hot(combined_pos, capacity + 1, dtype=jnp.int32)
            combine_mask = masked_probs[..., None] * pos_in_cap
            combine_mask = combine_mask[..., 1:].astype(dtype)
            dispatch_mask = (combine_mask != 0).astype(dtype)
            dispatch = jnp.einsum('bsm,bsec->ebcm', hidden_states, dispatch_mask)
            h1 = jnp.einsum('ebcm,emh->ebch', dispatch, w1)
            h3 = jnp.einsum('ebcm,emh->ebch', dispatch, w3)
            expert_out = jnp.einsum('ebch,ehm->ebcm', jax.nn.silu(h1) * h3, w2)
            final = jnp.einsum('ebcm,bsec->bsm', expert_out, combine_mask)
            return final
        key = jax.random.key(seed)
        k1, k2, k3, k4, k5 = jax.random.split(key, 5)
        s_h = 1.0 / np.sqrt(H)
        s_f = 1.0 / np.sqrt(F)
        return {'hidden_states': jax.random.normal(k1, (B, S, H), dtype=jnp.float32), 'gate_w': jax.random.normal(k2, (E, H), dtype=jnp.float32) * s_h, 'w1': jax.random.normal(k3, (E, H, F), dtype=jnp.float32) * s_h, 'w2': jax.random.normal(k4, (E, F, H), dtype=jnp.float32) * s_f, 'w3': jax.random.normal(k5, (E, H, F), dtype=jnp.float32) * s_h}
    _L0_ffn_in = _L0_ffn_setup()
    _d = {'L0_attn_x': _L0_attn_in['x'], 'L0_attn_w_qkv': _L0_attn_in['w_qkv'], 'L0_attn_b_qkv': _L0_attn_in['b_qkv'], 'L0_attn_w_out': _L0_attn_in['w_out'], 'L0_attn_b_out': _L0_attn_in['b_out'], 'L0_ffn_gate_w': _L0_ffn_in['gate_w'], 'L0_ffn_w1': _L0_ffn_in['w1'], 'L0_ffn_w2': _L0_ffn_in['w2'], 'L0_ffn_w3': _L0_ffn_in['w3']}
    _x0 = _d['L0_attn_x']
    _d['L0_attn_x'] = jax.random.normal(jax.random.fold_in(jax.random.key(seed), 1), (32, 256, 128), dtype=_x0.dtype)
    del _x0
    return _d

def reference(L0_attn_x, L0_attn_w_qkv, L0_attn_b_qkv, L0_attn_w_out, L0_attn_b_out, L0_ffn_gate_w, L0_ffn_w1, L0_ffn_w2, L0_ffn_w3):

    def _L0_attn_ref(x, w_qkv, b_qkv, w_out, b_out):
        import jax, jax.numpy as jnp
        import numpy as np
        B, T, C, H = (2, 128, 128, 16)
        D = C // H
        EPS = 1e-06
        b, t, c = x.shape
        qkv = x @ w_qkv.T + b_qkv
        q, k, v = jnp.split(qkv, 3, axis=-1)

        def to_heads(u):
            return u.reshape(b, t, H, D).transpose(0, 2, 1, 3).astype(jnp.float32)
        q, k, v = (to_heads(q), to_heads(k), to_heads(v))
        q_prime = jax.nn.elu(q) + 1.0
        k_prime = jax.nn.elu(k) + 1.0
        kv_cumsum = jnp.cumsum(jnp.einsum('bhtd,bhte->bhtde', k_prime, v), axis=2)
        context = jnp.einsum('bhtd,bhtde->bhte', q_prime, kv_cumsum)
        norm = jnp.einsum('bhtd,bhtd->bht', q_prime, jnp.cumsum(k_prime, axis=2))
        out = context / (norm[..., None] + EPS)
        out = out.astype(x.dtype).transpose(0, 2, 1, 3).reshape(b, t, c)
        return out @ w_out.T + b_out

    def _L0_ffn_ref(hidden_states, gate_w, w1, w2, w3):
        import jax, jax.numpy as jnp
        import numpy as np
        B, S, H, F, E, K = (4, 256, 128, 448, 8, 2)
        CAP_FACTOR = 1.25

        def _moe_forward(hidden_states, gate_w, w1, w2, w3):
            b, s, h = hidden_states.shape
            dtype = hidden_states.dtype
            x = hidden_states.reshape(-1, h)
            router_logits = x @ gate_w.T
            expert_weights = jax.nn.softmax(router_logits.astype(jnp.float32), axis=1)
            _, selected_experts = jax.lax.top_k(expert_weights, K)
            top_k_idx = selected_experts.reshape(b, s, K)
            probs = expert_weights.reshape(b, s, E)
            capacity = int(s * K / E * CAP_FACTOR)
            expert_mask = jax.nn.one_hot(top_k_idx, E, dtype=jnp.int32)
            mask_fused = expert_mask.reshape(b, s * K, E)
            count_fused = jnp.cumsum(mask_fused, axis=1)
            count = count_fused.reshape(b, s, K, E)
            trunc_mask = expert_mask * (count <= capacity).astype(jnp.int32)
            combined_mask = trunc_mask.sum(axis=2)
            masked_probs = probs * combined_mask
            pos_fused = mask_fused * count_fused
            pos = pos_fused.reshape(b, s, K, E)
            combined_pos = pos.sum(axis=2) * combined_mask
            pos_in_cap = jax.nn.one_hot(combined_pos, capacity + 1, dtype=jnp.int32)
            combine_mask = masked_probs[..., None] * pos_in_cap
            combine_mask = combine_mask[..., 1:].astype(dtype)
            dispatch_mask = (combine_mask != 0).astype(dtype)
            dispatch = jnp.einsum('bsm,bsec->ebcm', hidden_states, dispatch_mask)
            h1 = jnp.einsum('ebcm,emh->ebch', dispatch, w1)
            h3 = jnp.einsum('ebcm,emh->ebch', dispatch, w3)
            expert_out = jnp.einsum('ebch,ehm->ebcm', jax.nn.silu(h1) * h3, w2)
            final = jnp.einsum('ebcm,bsec->bsm', expert_out, combine_mask)
            return final
        return _moe_forward(hidden_states, gate_w, w1, w2, w3)
    x = L0_attn_x
    x = _layernorm(x + _L0_attn_ref(x, L0_attn_w_qkv, L0_attn_b_qkv, L0_attn_w_out, L0_attn_b_out), axis=-1)
    x = _layernorm(x + _L0_ffn_ref(x, L0_ffn_gate_w, L0_ffn_w1, L0_ffn_w2, L0_ffn_w3), axis=-1)
    return x

_drawn_inputs = setup_inputs


def setup_inputs(seed=0):
    import zlib

    import numpy as np

    out = dict(_drawn_inputs(seed))
    spreads = {}
    factors = {'L0_attn_w_qkv': 4.124, 'L0_attn_b_qkv': 4.602, 'L0_attn_w_out': 3.632}
    for name, (base, spread) in spreads.items():
        noise = np.random.default_rng([zlib.crc32(name.encode()), seed]).standard_normal(out[name].shape)
        drawn = base * np.exp(spread * noise) if base else spread * noise
        out[name] = jnp.asarray(drawn.astype(out[name].dtype))
    for name, factor in factors.items():
        out[name] = (out[name] * factor).astype(out[name].dtype)
    return out
```

```python
def build(nc, x, xt_in, wqkv, bqkv, wout, bout, gate, w1, w2, w3, acc, slot_rows, out):
    from contextlib import ExitStack

    import concourse.bass as bass
    from concourse import mybir

    fp32 = mybir.dt.float32
    bf16 = mybir.dt.bfloat16
    u32 = mybir.dt.uint32
    ACT = mybir.ActivationFunctionType
    ALU = mybir.AluOpType

    TOK, C = x.shape
    P = 128
    T = 256
    B = TOK // T
    H = 16
    DH = C // H
    DV = DH + 1
    J = 4
    R = H // J
    E, _, F = w1.shape
    K_TOP = 2
    CAP = int(T * K_TOP / E * 1.25)
    SLOTS = B * CAP
    FK = 4
    FT = F - 3 * P
    CH = 512
    NCH = SLOTS // CH
    SUB = CH // P
    NT = SLOTS // P
    NAUX = 3 * E + 2
    HALF = E // 2 * CAP
    EPS_ATT = 1e-6
    EPS_LN = 1e-5
    ROWS_C = 8
    NC_CH = TOK // (P * ROWS_C)

    XT = ["qkv0", "qkv1", "tr0", "tr1"]
    XA = ["xhi", "ex0", "v0", "ex1", "v1", "T0", "T1"]
    XV = ["xlo", "mn0", "f0", "mn1", "f1"]
    XP = ["qh0", "kh0", "ql0", "kl0", "vh", "vl", "qh1", "kh1", "ql1", "kl1"]
    YT = ["state", "sc00", "sc01", "sc02", "sc03", "sc10", "sc11", "ctx0", "sc12", "ct0", "sc13", "proj0",
          "ctx1", "ct1", "proj1"]
    YV = ["s32", "am00", "am02", "am10", "den0", "rec0", "cn0", "am12", "res0", "bn0", "ag0",
          "den1", "rec1", "cn1", "res1", "bn1", "ag1", "ve", "x10", "x11"]
    YA = ["cp01", "cp03", "cp11", "cT0", "cp13", "cT1"]
    YP = ["shi", "slo", "am01", "am03", "am11", "am13", "rstd"]
    ZT = ["x1t", "rt", "pos", "d0", "d1", "d2", "d3", "d4", "d5"]
    ZA = ["x1T", "el0", "el1", "xh0", "xh1"]
    ZV = ["mx0", "mx1", "nm", "rs", "pr", "tp0", "tp1", "ti0", "ti1", "tif", "m0", "m1", "M",
          "val", "dpa", "dp", "D0", "D1", "xl0", "xl1", "ax0", "ax1"]
    ZP = ["x1h", "x1l", "ph", "r1", "pm", "pl"]

    def n(b, steps, step):
        return b * len(steps) + (steps.index(step) + 1)

    def prev(b, steps, step):
        return b * len(steps) + (steps.index(step) + 1 - len(steps))

    def prev2(b, steps, step):
        return b * len(steps) + (steps.index(step) + 1 - 2 * len(steps))

    ctx = ExitStack()
    with ctx:
        def sb(name, shape, dt=fp32):
            return ctx.enter_context(nc.sbuf_tensor(name, shape, dt))

        def sem(name):
            return ctx.enter_context(nc.semaphore(name))

        ident = sb("ident", [P, P])
        identb = sb("identb", [P, P], bf16)
        tri = sb("tri", [P, P])
        trib = sb("trib", [P, P], bf16)
        onesb = sb("onesb", [P, P], bf16)
        head_mask = sb("head_mask", [P, J, R, DV])
        iota_c = sb("iota_c", [P, CAP], bf16)
        iota_e = sb("iota_e", [P, E])
        aux_mask = sb("aux_mask", [32, E, CAP])
        sel = sb("sel", [32, 3], bf16)
        half_pow = sb("half_pow", [P, ROWS_C])
        slot_base = sb("slot_base", [P, NT])
        spare_row = sb("spare_row", [P, NT])
        zrow = sb("zrow", [P, C])
        wq32 = sb("wq32", [P, 3 * C])
        wqh = sb("wqh", [P, 3 * C], bf16)
        wql = sb("wql", [P, 3 * C], bf16)
        wo32 = sb("wo32", [P, C])
        gt32 = sb("gt32", [P, E])
        bias32 = sb("bias32", [96, 4 * C])
        bias_h = sb("bias_h", [96, 4 * C], bf16)
        bias_m = sb("bias_m", [96, 4 * C], bf16)
        bias3 = sb("bias3", [96, 4 * C], bf16)
        xT32 = sb("xT32", [P, T])
        x32 = sb("x32", [P, 2, 2, C])
        xh = sb("xh", [P, T], bf16)
        xl = sb("xl", [P, T], bf16)
        mn = sb("mn", [P, 2, 2 * C])
        ex = sb("ex", [P, 2, 2 * C])
        feat = sb("feat", [P, 2, 2 * C])
        stack = sb("stack", [P, 2, 2, 2, C, 2, 2], bf16)
        qkT = sb("qkT", [P, 2, 2, 2, J, P], bf16)
        v32 = sb("v32", [P, 2, 2, H, DV])
        vh = sb("vh", [P, 2, H, DV], bf16)
        vl = sb("vl", [P, 2, H, DV], bf16)
        s32 = sb("s32", [P, J, R * DV])
        sh = sb("sh", [P, J, R * DV], bf16)
        sl = sb("sl", [P, J, R * DV], bf16)
        raw = sb("raw", [P, 2, J * P])
        am = sb("am", [P, 2, R, J, P])
        den = sb("den", [P, 2, H])
        rec = sb("rec", [P, 2, H])
        cn = sb("cn", [P, 2, C])
        cT = sb("cT", [P, 2, P])
        r32 = sb("r32", [P, 2, C])
        bn = sb("bn", [P, 2, 6])
        mv = sb("mv", [P, 2, 2])
        ve = sb("ve", [P, 2])
        rstd = sb("rstd", [P, 2])
        x1 = sb("x1", [P, 2, 2, C])
        x1h = sb("x1h", [P, 2, C], bf16)
        x1l = sb("x1l", [P, 2, C], bf16)
        x1T = sb("x1T", [P, 2, P])
        mx = sb("mx", [P, 2, 8])
        nm = sb("nm", [P, 2])
        el = sb("el", [P, 2, E])
        es = sb("es", [P, 2])
        rs = sb("rs", [P, 2])
        pr = sb("pr", [P, 2, E])
        tp = sb("tp", [P, 2, 8])
        ti = sb("ti", [P, 2, 8], u32)
        tif = sb("tif", [P, 2, K_TOP])
        m0 = sb("m0", [P, 2, E])
        m1 = sb("m1", [P, 2, E])
        mb = sb("mb", [P, 2, E], bf16)
        val = sb("val", [P, 2, E])
        dpa = sb("dpa", [P, 2, E])
        dp = sb("dp", [P, 2, E], bf16)
        onehot = sb("onehot", [P, 2, E, CAP], bf16)
        aux = sb("aux", [P, 2, NAUX], bf16)
        pres = sb("pres", [P, 2, E])
        rows_out = sb("rows_out", [NAUX, E, CAP], bf16)
        xdh = sb("xdh", [P, E, SLOTS], bf16)
        xdl = sb("xdl", [P, E, SLOTS], bf16)
        wst = sb("wst", [P, 2 * F + FK * C])
        wh = sb("wh", [P, 2, 2 * F + FK * C], bf16)
        wl = sb("wl", [P, 2, 2 * F + FK * C], bf16)
        rows_in = sb("rows_in", [NAUX, 2, SLOTS], bf16)
        idx_a = sb("idx_a", [P, NT])
        idx = sb("idx", [P, 2, NT], u32)
        prob = sb("prob", [P, 2, NT])
        sil = sb("sil", [P, 2, CH])
        gh = sb("gh", [P, 2, FK, CH], bf16)
        g32 = am[:, 0, :, :, :].rearrange("p r j t -> p r (j t)")
        gl = am[:, 1, :, :, :].rearrange("p r j t -> p (r j t)").bitcast(bf16)\
            .rearrange("p (q k s) -> p q k s", q=2, k=FK)
        eo = sb("eo", [P, 2, SUB, C])
        cx = am[:, :, :, :, :].rearrange("p h r j t -> p h (r j t)")
        cst = sb("cst", [P, 2, ROWS_C, 6])
        cmv = sb("cmv", [P, 2, ROWS_C, 2])
        cve = sb("cve", [P, 2, ROWS_C])
        crs = sb("crs", [P, 2, ROWS_C])

        bank = [ctx.enter_context(nc.psum_tensor(f"bank{i}", [P, 512], fp32)) for i in range(8)]
        p_qkv = bank[0]
        p_tr = bank[2][:, :].bitcast(bf16).rearrange("p (s t) -> p s t", s=8)
        p_sc = [bank[3], bank[4]]
        p_ctx = bank[5][:, 0:H * DV]
        p_y = bank[6]
        p_z = [bank[7], bank[1]]

        const_ready = sem("const_ready")
        wa_loaded = sem("wa_loaded")
        setup_v = sem("setup_v")
        setup_p = sem("setup_p")
        passed_v = sem("passed_v")
        passed_p = sem("passed_p")
        passed_s = sem("passed_s")
        xt_loaded = sem("xt_loaded")
        x_loaded = sem("x_loaded")
        xt, xa, xv, xp = (sem(s) for s in ("xt", "xa", "xv", "xp"))
        yt, ya, yv, yp = (sem(s) for s in ("yt", "ya", "yv", "yp"))
        zt, za, zv, zp = (sem(s) for s in ("zt", "za", "zv", "zp"))
        acc_stored = sem("acc_stored")
        spare_stored = sem("spare_stored")
        rows_stored = sem("rows_stored")
        w_loaded = sem("w_loaded")
        rows_loaded = sem("rows_loaded")
        w_split_h = sem("w_split_h")
        w_split_l = sem("w_split_l")
        info_t = sem("info_t")
        info_v = sem("info_v")
        up_t = sem("up_t")
        silu_a = sem("silu_a")
        gate_v = sem("gate_v")
        gh_a = sem("gh_a")
        gl_p = sem("gl_p")
        down_t = sem("down_t")
        eo_v = sem("eo_v")
        added = [sem("added0"), sem("added1")]
        c_loaded = [sem("c_loaded0"), sem("c_loaded1")]
        c_v = sem("c_v")
        c_p = sem("c_p")
        c_stored = [sem("c_stored0"), sem("c_stored1")]

        NSETV = 13
        block = ctx.enter_context(nc.Block())

        def slots_a(engine, slot):
            slot(0, 0, True, False)
            slot(1, 1, True, True)
            with engine.Fori(0, B // 2 - 2) as i:
                slot(i * 2 + 2, 0, True, True)
                slot(i * 2 + 3, 1, True, True)
            slot(B - 2, 0, True, True)
            slot(B - 1, 1, False, True)
            slot(B, 0, False, True, False)

        @block.sync
        def _(sp):
            sp.dma_start(wq32[:, :], wqkv).then_inc(wa_loaded, 16)
            sp.dma_start(wo32[:, :], wout).then_inc(wa_loaded, 16)
            sp.dma_start(gt32[:, :], gate).then_inc(wa_loaded, 16)
            for row in (0, 32, 64):
                sp.dma_start(bias32[row:row + 1, 0:3 * C], bqkv).then_inc(wa_loaded, 16)
                sp.dma_start(bias32[row:row + 1, 3 * C:4 * C], bout).then_inc(wa_loaded, 16)

            def load(b, par, first=False):
                if not first:
                    sp.wait_ge(xt_loaded, b * 16)
                    sp.wait_ge(xa, prev(b, XA, "xhi"))
                    sp.wait_ge(xv, prev(b, XV, "xlo"))
                sp.dma_start(xT32[:, :], xt_in[:, bass.ds(b * T, T)]).then_inc(xt_loaded, 16)
                if not first:
                    sp.wait_ge(x_loaded, b * 16)
                sp.dma_start(x32[:, par, :, :], x[bass.ds(b * T, T), :].rearrange("(h p) c -> p h c", h=2))\
                    .then_inc(x_loaded, 16)

            load(0, 0, True)

            def slot(b, par, do_x, do_z, do_y=True):
                if do_x:
                    if do_z:
                        sp.wait_ge(yv, prev(b, YV, "res1"))
                    load(b + 1, 1 - par)
                if do_z:
                    bz = b - 1
                    sp.wait_ge(zv, n(bz, ZV, "ax1"))
                    sp.sem_inc(passed_s, 1)
                    if not isinstance(bz, int) or bz > 0:
                        sp.wait_ge(rows_stored, bz * 16)
                    sp.dma_start(slot_rows[:, :, bass.ds(bz * CAP, CAP)].rearrange("e a c -> a e c"),
                                 rows_out[:, :, :]).then_inc(rows_stored, 16)
                if do_y:
                    sp.wait_ge(yv, n(b, YV, "x11"))
                    sp.dma_start(acc[bass.ds(b * T, T), :].rearrange("(h p) c -> p h c", h=2),
                                 x1[:, par, :, :]).then_inc(acc_stored, 16)

            slots_a(sp, slot)

            def load_expert(e, par, first=False):
                if not first:
                    sp.wait_ge(w_split_l, e)
                    sp.wait_ge(w_split_h, e)
                for col, src, lo, hi in ((0, w1, 0, 3 * P), (3 * P, w3, 0, 3 * P), (6 * P, w3, 3 * P, F),
                                         (6 * P + FT, w1, 3 * P, F)):
                    s = src[bass.ds(e, 1), :, lo:hi].rearrange("o m f -> m (o f)")
                    sp.dma_start(wst[:, col:col + hi - lo], s).then_inc(w_loaded, 16)
                s = w2[bass.ds(e, 1), 0:3 * P, :].rearrange("o (k p) m -> p (o k) m", p=P)
                sp.dma_start(wst[:, 2 * F:2 * F + 3 * C].rearrange("p (k m) -> p k m", k=3), s)\
                    .then_inc(w_loaded, 16)
                s = w2[bass.ds(e, 1), 3 * P:F, :].rearrange("o f m -> f (o m)")
                sp.dma_start(wst[0:FT, 2 * F + 3 * C:], s).then_inc(w_loaded, 16)

            def load_rows(e, par):
                sp.dma_start(rows_in[:, par, :], slot_rows[bass.ds(e, 1), :, :].rearrange("o a s -> a (o s)"))\
                    .then_inc(rows_loaded, 16)

            sp.wait_ge(setup_p, 1)
            load_expert(0, 0, True)
            sp.wait_ge(rows_stored, 16 * B)
            load_rows(0, 0)

            def next_expert(e, par, last=False):
                load_expert(e + 1, 1 - par)
                sp.wait_ge(rows_loaded, e * 16 + 16)
                sp.wait_ge(info_t, e)
                load_rows(e + 1, 1 - par)

            with sp.Fori(0, E // 2 - 1) as i:
                next_expert(i * 2, 0)
                next_expert(i * 2 + 1, 1)
            next_expert(E - 2, 0)

            for q in range(2):
                sp.wait_ge(added[q], E * NCH // 2 * SUB * 16)
            sp.wait_ge(spare_stored, 16 * NT)

            def rows_of(t, k):
                return t[bass.ds(k * P * ROWS_C, P * ROWS_C), :].rearrange("(p r) c -> p (r c)", p=P)

            def load_c(k, par):
                sp.dma_start(cx[:, par, 0:ROWS_C * C], rows_of(acc, k)).then_inc(c_loaded[par], 16)

            load_c(0, 0)
            load_c(1, 1)

            def store_c(i, par, more):
                k = i * 2 + par
                sp.wait_ge(c_v, k * 5 + 5)
                sp.dma_start(rows_of(out, k), cx[:, par, ROWS_C * C:2 * ROWS_C * C]).then_inc(c_stored[par], 16)
                if more:
                    load_c(k + 2, par)

            with sp.Fori(0, NC_CH // 2 - 1) as i:
                store_c(i, 0, True)
                store_c(i, 1, True)
            store_c(NC_CH // 2 - 1, 0, False)
            store_c(NC_CH // 2 - 1, 1, False)
            sp.wait_ge(acc_stored, 16 * B)
            for q in range(2):
                sp.wait_ge(c_stored[q], NC_CH // 2 * 16)

        @block.gpsimd
        def _(pool):
            g = nc.gpsimd
            made = [0]

            def link(ins):
                made[0] += 1
                ins.then_inc(const_ready, 1)
                pool.wait_ge(const_ready, made[0])

            link(g.memset(ident[:, :], 0.0))
            link(g.affine_select(out=ident[:, :], in_=ident[:, :], compare_op=ALU.not_equal, fill=1.0, base=0,
                                 pattern=[[-1, P]], channel_multiplier=1))
            link(g.tensor_copy(identb[:, :], ident[:, :]))
            link(g.memset(tri[:, :], 1.0))
            link(g.affine_select(out=tri[:, :], in_=tri[:, :], compare_op=ALU.is_ge, fill=0.0, base=0,
                                 pattern=[[1, P]], channel_multiplier=-1))
            link(g.tensor_copy(trib[:, :], tri[:, :]))
            link(g.memset(onesb[:, :], 1.0))
            link(g.memset(head_mask[:, :, :, :], 1.0))
            link(g.affine_select(out=head_mask[:, :, :, :], in_=head_mask[:, :, :, :], compare_op=ALU.is_ge,
                                 fill=0.0, base=0, pattern=[[0, J], [-32, R], [0, DV]], channel_multiplier=1))
            link(g.affine_select(out=head_mask[:, :, :, :], in_=head_mask[:, :, :, :], compare_op=ALU.is_ge,
                                 fill=0.0, base=31, pattern=[[0, J], [32, R], [0, DV]], channel_multiplier=-1))
            link(g.iota(iota_c[:, :], [[1, CAP]], base=0, channel_multiplier=0,
                        allow_small_or_imprecise_dtypes=True))
            link(g.iota(iota_e[:, :], [[1, E]], base=0, channel_multiplier=0,
                        allow_small_or_imprecise_dtypes=True))
            link(g.memset(aux_mask[:, :, :], 0.0))
            for part in range(3):
                link(g.affine_select(out=aux_mask[:, :, :], in_=aux_mask[:, :, :], compare_op=ALU.not_equal,
                                     fill=1.0, base=-part * E, pattern=[[-1, E], [0, CAP]],
                                     channel_multiplier=1))
            link(g.affine_select(out=aux_mask[:, :, :], in_=aux_mask[:, :, :], compare_op=ALU.is_ge,
                                 fill=1.0, base=3 * E - 1, pattern=[[0, E], [0, CAP]], channel_multiplier=-1))
            link(g.memset(sel[:, :], 0.0))
            link(g.affine_select(out=sel[:, 0:2], in_=sel[:, 0:2], compare_op=ALU.not_equal, fill=1.0,
                                 base=-3 * E, pattern=[[-1, 2]], channel_multiplier=1))
            link(g.affine_select(out=sel[:, 2:3], in_=sel[:, 2:3], compare_op=ALU.is_ge, fill=1.0,
                                 base=-3 * E, pattern=[[0, 1]], channel_multiplier=1))
            link(g.memset(aux[:, :, 3 * E + 1:3 * E + 2], 1.0))
            link(g.iota(aux[:, :, 3 * E:3 * E + 1], [[P, 2], [0, 1]], base=0, channel_multiplier=1,
                        allow_small_or_imprecise_dtypes=True))
            link(g.iota(spare_row[:, :], [[P, NT]], base=TOK, channel_multiplier=1,
                        allow_small_or_imprecise_dtypes=True))
            link(g.memset(v32[:, :, :, :, :], 1.0))
            link(g.memset(zrow[:, :], 0.0))
            link(g.memset(wst[:, :], 0.0))
            link(g.memset(slot_base[:, :], 0.0))
            for b in range(1, B):
                t0, t1 = max(0, (b * CAP) // P), NT
                v = slot_base[:, t0:t1]
                link(g.affine_select(out=v, in_=v, compare_op=ALU.is_ge, fill=float(T * b),
                                     base=b * CAP - 1 - P * t0, pattern=[[-P, t1 - t0]], channel_multiplier=-1))
            for s in range(NT):
                pool.dma_start(acc[TOK + s * P:TOK + (s + 1) * P, :], zrow[:, :]).then_inc(spare_stored, 16)
            g.memset(half_pow[:, :], -0.5).then_inc(setup_p, 1)

            def slot(b, par, do_x, do_z, do_y=True):
                early = isinstance(b, int) and b == 0
                o = 1 - par
                bx, bz = b + 1, b - 1
                if do_z:
                    pool.wait_ge(yv, n(bz, YV, "x11"))
                    if not (isinstance(bz, int) and bz == 0):
                        pool.wait_ge(zt, prev(bz, ZT, "d3"))
                    pool.sem_inc(passed_p, 1)
                    g.tensor_copy(x1h[:, :, :], x1[:, o, :, :]).then_inc(zp, 1)
                    pool.wait_ge(zp, n(bz, ZP, "x1h"))
                    g.tensor_tensor(x1l[:, :, :], x1[:, o, :, :], x1h[:, :, :], ALU.subtract).then_inc(zp, 1)
                if do_y:
                    pool.wait_ge(yv, n(b, YV, "s32"))
                    if not early:
                        pool.wait_ge(yt, prev(b, YT, "ctx1"))
                    pool.sem_inc(passed_p, 1)
                    g.tensor_copy(sh[:, :, :], s32[:, :, :]).then_inc(yp, 1)
                    pool.wait_ge(yp, n(b, YP, "shi"))
                    g.tensor_tensor(sl[:, :, :], s32[:, :, :], sh[:, :, :], ALU.subtract).then_inc(yp, 1)

                def stacks(bx, h):
                    pool.wait_ge(xv, n(bx, XV, f"f{h}"))
                    if not (isinstance(bx, int) and bx < 2):
                        pool.wait_ge(xt, prev2(bx, XT, f"tr{h}"))
                        pool.wait_ge(yt, prev2(bx, YT, "state"))
                    pool.sem_inc(passed_p, 1)
                    q, k = feat[:, h, 0:C], feat[:, h, C:2 * C]
                    sq, sk = stack[:, ox, h, 0, :, :, :], stack[:, ox, h, 1, :, :, :]
                    q2 = q.rearrange("p (c o) -> p c o", o=1).to_broadcast([P, C, 2])
                    k2 = k.rearrange("p (c o) -> p c o", o=1).to_broadcast([P, C, 2])
                    g.tensor_copy(sq[:, :, :, 0], q2).then_inc(xp, 1)
                    g.tensor_copy(sk[:, :, 0, :], k2).then_inc(xp, 1)
                    pool.wait_ge(xp, n(bx, XP, f"kh{h}"))
                    g.tensor_tensor(sq[:, :, :, 1], q2, sq[:, :, :, 0], ALU.subtract).then_inc(xp, 1)
                    g.tensor_tensor(sk[:, :, 1, :], k2, sk[:, :, 0, :], ALU.subtract).then_inc(xp, 1)

                ox = o

                def mask_a(h, r):
                    pool.wait_ge(ya, n(b, YA, f"cp{h}{r}"))
                    if not early:
                        pool.wait_ge(yt, prev(b, YT, f"ctx{h}"))
                    m = tri[:, :].rearrange("p (o t) -> p o t", o=1).to_broadcast([P, J, P])
                    g.tensor_tensor(am[:, h, r, :, :], raw[:, r // 2, :].rearrange("p (j t) -> p j t", j=J), m,
                                    ALU.mult).then_inc(yp, 1)

                if do_x:
                    stacks(bx, 0)
                if do_y:
                    mask_a(0, 1)
                    mask_a(0, 3)
                if do_x:
                    pool.wait_ge(xa, n(bx, XA, "v0"))
                    pool.sem_inc(passed_p, 1)
                    g.tensor_copy(vh[:, ox, :, :], v32[:, ox, 0, :, :]).then_inc(xp, 1)
                    pool.wait_ge(xp, n(bx, XP, "vh"))
                    g.tensor_tensor(vl[:, ox, :, :], v32[:, ox, 0, :, :], vh[:, ox, :, :], ALU.subtract)\
                        .then_inc(xp, 1)
                    stacks(bx, 1)
                if do_z:
                    pool.wait_ge(zv, n(bz, ZV, "pr"))
                    if not (isinstance(bz, int) and bz == 0):
                        pool.wait_ge(zt, prev(bz, ZT, "d5"))
                    pool.sem_inc(passed_p, 1)
                    g.tensor_copy(aux[:, :, 0:E], pr[:, :, :]).then_inc(zp, 1)
                    pool.wait_ge(zp, n(bz, ZP, "ph"))
                    g.tensor_tensor(pres[:, :, :], pr[:, :, :], aux[:, :, 0:E], ALU.subtract).then_inc(zp, 1)
                    pool.wait_ge(zp, n(bz, ZP, "r1"))
                    pool.sem_inc(passed_p, 1)
                    g.tensor_copy(aux[:, :, E:2 * E], pres[:, :, :]).then_inc(zp, 1)
                    pool.wait_ge(zp, n(bz, ZP, "pm"))
                    g.tensor_tensor(aux[:, :, 2 * E:3 * E], pres[:, :, :], aux[:, :, E:2 * E], ALU.subtract)\
                        .then_inc(zp, 1)
                if do_y:
                    mask_a(1, 1)
                    mask_a(1, 3)
                    pool.wait_ge(yv, n(b, YV, "ve"))
                    g.tensor_tensor(rstd[:, :], ve[:, :], half_pow[:, 0:2], ALU.pow).then_inc(yp, 1)

            def first_x():
                for h in range(2):
                    pool.wait_ge(xv, n(0, XV, f"f{h}"))
                    if h == 1:
                        pool.wait_ge(xa, n(0, XA, "v0"))
                        g.tensor_copy(vh[:, 0, :, :], v32[:, 0, 0, :, :]).then_inc(xp, 1)
                        pool.wait_ge(xp, n(0, XP, "vh"))
                        g.tensor_tensor(vl[:, 0, :, :], v32[:, 0, 0, :, :], vh[:, 0, :, :], ALU.subtract)\
                            .then_inc(xp, 1)
                    q, k = feat[:, h, 0:C], feat[:, h, C:2 * C]
                    sq, sk = stack[:, 0, h, 0, :, :, :], stack[:, 0, h, 1, :, :, :]
                    q2 = q.rearrange("p (c o) -> p c o", o=1).to_broadcast([P, C, 2])
                    k2 = k.rearrange("p (c o) -> p c o", o=1).to_broadcast([P, C, 2])
                    g.tensor_copy(sq[:, :, :, 0], q2).then_inc(xp, 1)
                    g.tensor_copy(sk[:, :, 0, :], k2).then_inc(xp, 1)
                    pool.wait_ge(xp, n(0, XP, f"kh{h}"))
                    g.tensor_tensor(sq[:, :, :, 1], q2, sq[:, :, :, 0], ALU.subtract).then_inc(xp, 1)
                    g.tensor_tensor(sk[:, :, 1, :], k2, sk[:, :, 0, :], ALU.subtract).then_inc(xp, 1)

            first_x()
            slots_a(pool, slot)

            def split_weights(e, par):
                pool.wait_ge(w_loaded, e * 96 + 96)
                if not (isinstance(e, int) and e < 2):
                    pool.wait_ge(down_t, e * NCH - NCH)
                pool.sem_inc(passed_p, 1)
                g.tensor_copy(wh[:, par, :], wst[:, :]).then_inc(w_split_h, 1)
                pool.wait_ge(w_split_h, e + 1)
                g.tensor_tensor(wl[:, par, :], wst[:, :], wh[:, par, :], ALU.subtract).then_inc(w_split_l, 1)

            def low_part(nb, cpar, first):
                for k in range(FK):
                    rows = P if k < 3 else FT
                    pool.wait_ge(gh_a, nb * FK + (k + 1))
                    if not first:
                        pool.wait_ge(down_t, nb - 1)
                    g.tensor_tensor(gl[0:rows, cpar, k, :], g32[0:rows, k, :], gh[0:rows, cpar, k, :],
                                    ALU.subtract).then_inc(gl_p, 1)

            def add_rows(nb, c, par, cpar):
                pool.wait_ge(eo_v, nb + 1)
                pool.sem_inc(passed_p, 1)
                for s in range(SUB):
                    g.indirect_dma_start(
                        out=acc, out_offset=bass.IndirectOffsetOnAxis(
                            ap=idx[:, par, c * SUB + s:c * SUB + s + 1], axis=0),
                        in_=eo[:, cpar, s, :], in_offset=None, compute_op=ALU.add).then_inc(added[cpar], 16)

            split_weights(0, 0)
            pool.wait_ge(acc_stored, 16 * B)
            pool.wait_ge(spare_stored, 16 * NT)

            def experts(i, first, last):
                for q in range(2 * NCH):
                    par, c, cpar = q // NCH, q % NCH, q % 2
                    nb = i * (2 * NCH) + q
                    low_part(nb, cpar, first and q < 2)
                    if c == 1 and not (last and par == 1):
                        split_weights(i * 2 + par + 1, 1 - par)
                    if q > 0:
                        pq = q - 1
                        if pq % NCH == 0 and not (first and pq == 0):
                            e = i * 2 + pq // NCH
                            pool.wait_ge(added[0], (i * NCH + (NCH // 2 + 1 if pq else 0)) * SUB * 16)
                            pool.wait_ge(added[1], (i * NCH + (NCH // 2 if pq else 0)) * SUB * 16)
                        add_rows(nb - 1, pq % NCH, pq // NCH, pq % 2)
                add_rows(i * (2 * NCH) + 2 * NCH - 1, NCH - 1, 1, 1)

            experts(0, True, False)
            with pool.Fori(1, E // 2 - 1) as i:
                experts(i, False, False)
            experts(E // 2 - 1, False, True)

            def chunk_c(k, par):
                pool.wait_ge(c_v, k * 5 + 3)
                g.tensor_tensor(crs[:, par, :], cve[:, par, :], half_pow[:, :], ALU.pow).then_inc(c_p, 1)

            with pool.Fori(0, NC_CH // 2) as i:
                chunk_c(i * 2, 0)
                chunk_c(i * 2 + 1, 1)

        @block.vector
        def _(dve):
            v = nc.vector
            dve.wait_ge(wa_loaded, 9 * 16)
            dve.wait_ge(setup_p, 1)
            made = [0]

            def link(ins):
                made[0] += 1
                ins.then_inc(setup_v, 1)
                dve.wait_ge(setup_v, made[0])

            link(v.tensor_copy(wqh[:, :], wq32[:, :]))
            link(v.tensor_tensor(wql[:, :], wq32[:, :], wqh[:, :], ALU.subtract))
            link(v.memset(bias3[:, :], 0.0))
            for row in (0, 32, 64):
                link(v.tensor_copy(bias_h[row:row + 1, :], bias32[row:row + 1, :]))
            link(v.tensor_copy(bias3[0:1, :], bias_h[0:1, :]))
            for row in (32, 64):
                link(v.tensor_tensor(bias32[row:row + 1, :], bias32[row:row + 1, :], bias_h[row:row + 1, :],
                                     ALU.subtract))
                link(v.tensor_copy(bias_m[row:row + 1, :], bias32[row:row + 1, :]))
            link(v.tensor_copy(bias3[32:33, :], bias_m[32:33, :]))
            link(v.tensor_tensor(bias3[64:65, :], bias32[64:65, :], bias_m[64:65, :], ALU.subtract))
            assert made[0] == NSETV

            def xlo(b, first=False):
                dve.wait_ge(xa, n(b, XA, "xhi"))
                if not first:
                    dve.wait_ge(xt, prev(b, XT, "qkv1"))
                v.tensor_tensor(xl[:, :], xT32[:, :], xh[:, :], ALU.subtract).then_inc(xv, 1)

            def mins(b, h, first=False):
                dve.wait_ge(xt, n(b, XT, f"qkv{h}"))
                if not first:
                    dve.wait_ge(xa, prev(b, XA, f"ex{h}"))
                v.tensor_scalar(mn[:, h, :], p_qkv[:, 0:2 * C], 0.0, None, ALU.min).then_inc(xv, 1)

            def feats(b, h, first=False):
                dve.wait_ge(xa, n(b, XA, f"ex{h}"))
                if not first:
                    dve.wait_ge(xp, prev(b, XP, f"kl{h}"))
                v.scalar_tensor_tensor(out=feat[:, h, :], in0=p_qkv[:, 0:2 * C], scalar=0.0, in1=ex[:, h, :],
                                       op0=ALU.max, op1=ALU.add).then_inc(xv, 1)

            xlo(0, True)
            for h in range(2):
                mins(0, h, True)
                feats(0, h, True)

            def slot(b, par, do_x, do_z, do_y=True):
                early = isinstance(b, int) and b == 0
                o = 1 - par
                bx, bz = b + 1, b - 1
                zfirst = isinstance(bz, int) and bz == 0

                def mask_v(h, r):
                    dve.wait_ge(yt, n(b, YT, f"sc{h}{r}"))
                    if not early:
                        dve.wait_ge(yt, prev(b, YT, f"ctx{h}"))
                    m = tri[:, :].rearrange("p (o t) -> p o t", o=1).to_broadcast([P, J, P])
                    v.tensor_tensor(am[:, h, r, :, :], p_sc[r % 2][:, :].rearrange("p (j t) -> p j t", j=J), m,
                                    ALU.mult).then_inc(yv, 1)

                def normalize(h):
                    dve.wait_ge(yt, n(b, YT, f"ctx{h}"))
                    if not early:
                        dve.wait_ge(yv, prev(b, YV, f"cn{h}"))
                    c3 = p_ctx.rearrange("p (h e) -> p h e", e=DV)
                    v.tensor_scalar(den[:, h, :], c3[:, :, DH], EPS_ATT, None, ALU.add).then_inc(yv, 1)
                    dve.wait_ge(yv, n(b, YV, f"den{h}"))
                    v.reciprocal(rec[:, h, :], den[:, h, :]).then_inc(yv, 1)
                    dve.wait_ge(yv, n(b, YV, f"rec{h}"))
                    if not early:
                        dve.wait_ge(yt, prev(b, YT, f"ct{h}"))
                    v.tensor_tensor(cn[:, h, :].rearrange("p (h e) -> p h e", e=DH), c3[:, :, 0:DH],
                                    rec[:, h, :].rearrange("p (h o) -> p h o", o=1).to_broadcast([P, H, DH]),
                                    ALU.mult).then_inc(yv, 1)

                def residual(h):
                    dve.wait_ge(yt, n(b, YT, f"proj{h}"))
                    dve.wait_ge(x_loaded, b * 16 + 16)
                    if not early:
                        dve.wait_ge(yv, prev(b, YV, "x11"))
                    v.tensor_tensor(r32[:, h, :], p_y[:, 0:C], x32[:, par, h, :], ALU.add).then_inc(yv, 1)
                    dve.wait_ge(yv, n(b, YV, f"res{h}"))
                    v.bn_stats(bn[:, h, :], r32[:, h, :]).then_inc(yv, 1)
                    dve.wait_ge(yv, n(b, YV, f"bn{h}"))
                    dve.sem_inc(passed_v, 1)
                    v.bn_aggr(mv[:, h, :], bn[:, h, :]).then_inc(yv, 1)

                lg = p_z[0][:, 0:2 * E].rearrange("p (h e) -> p h e", h=2)
                if do_x:
                    xlo(bx)
                    mins(bx, 0)
                if do_y:
                    dve.wait_ge(yt, n(b, YT, "state"))
                    if not early:
                        dve.wait_ge(yp, prev(b, YP, "slo"))
                    v.tensor_tensor(s32[:, :, :], p_y[:, 0:H * DV].rearrange("p (j q) -> p j q", j=J),
                                    head_mask[:, :, :, :].rearrange("p j r e -> p j (r e)"), ALU.mult)\
                        .then_inc(yv, 1)
                if do_x:
                    feats(bx, 0)
                if do_y:
                    mask_v(0, 0)
                if do_z:
                    dve.wait_ge(zt, n(bz, ZT, "rt"))
                    if not zfirst:
                        dve.wait_ge(zv, prev(bz, ZV, "nm"))
                    for h in range(2):
                        dve.sem_inc(passed_v, 1)
                        v.max(mx[:, h, :], lg[:, h, :]).then_inc(zv, 1)
                    dve.wait_ge(zv, n(bz, ZV, "mx1"))
                    if not zfirst:
                        dve.wait_ge(za, prev(bz, ZA, "el1"))
                    v.tensor_scalar(nm[:, :], mx[:, :, 0], -1.0, None, ALU.mult).then_inc(zv, 1)
                if do_x:
                    mins(bx, 1)
                    feats(bx, 1)
                if do_y:
                    mask_v(0, 2)
                if do_z:
                    dve.wait_ge(za, n(bz, ZA, "el1"))
                    v.reciprocal(rs[:, :], es[:, :]).then_inc(zv, 1)
                    dve.wait_ge(zv, n(bz, ZV, "rs"))
                    if not zfirst:
                        dve.wait_ge(zp, prev(bz, ZP, "r1"))
                    v.tensor_tensor(pr[:, :, :], el[:, :, :],
                                    rs[:, :].rearrange("p (h o) -> p h o", o=1).to_broadcast([P, 2, E]),
                                    ALU.mult).then_inc(zv, 1)
                    dve.wait_ge(zv, n(bz, ZV, "pr"))
                    for h in range(2):
                        dve.sem_inc(passed_v, 1)
                        v.max(tp[:, h, :], pr[:, h, :]).then_inc(zv, 1)
                    dve.wait_ge(zv, n(bz, ZV, "tp1"))
                    for h in range(2):
                        dve.sem_inc(passed_v, 1)
                        v.max_index(ti[:, h, :], tp[:, h, :], pr[:, h, :]).then_inc(zv, 1)
                    dve.wait_ge(zv, n(bz, ZV, "ti1"))
                    v.tensor_copy(tif[:, :, :], ti[:, :, 0:K_TOP]).then_inc(zv, 1)
                    dve.wait_ge(zv, n(bz, ZV, "tif"))
                    ie = iota_e[:, :].rearrange("p (o e) -> p o e", o=1).to_broadcast([P, 2, E])
                    for k, m in ((0, m0), (1, m1)):
                        v.tensor_tensor(m[:, :, :], ie, tif[:, :, k:k + 1].to_broadcast([P, 2, E]),
                                        ALU.is_equal).then_inc(zv, 1)
                    dve.wait_ge(zv, n(bz, ZV, "m1"))
                    if not zfirst:
                        dve.wait_ge(zt, prev(bz, ZT, "pos"))
                    v.tensor_tensor(mb[:, :, :], m0[:, :, :], m1[:, :, :], ALU.add).then_inc(zv, 1)
                if do_y:
                    mask_v(1, 0)
                    normalize(0)
                if do_z:
                    pos = p_z[0][:, 32:32 + 2 * E].rearrange("p (h e) -> p h e", h=2)
                    dve.wait_ge(zt, n(bz, ZT, "pos"))
                    v.scalar_tensor_tensor(out=val[:, :, :], in0=pos, scalar=CAP + 0.5, in1=mb[:, :, :],
                                           op0=ALU.is_le, op1=ALU.mult).then_inc(zv, 1)
                    dve.wait_ge(zv, n(bz, ZV, "val"))
                    v.tensor_tensor(dpa[:, :, :], pos, val[:, :, :], ALU.mult).then_inc(zv, 1)
                    dve.wait_ge(zv, n(bz, ZV, "dpa"))
                    v.tensor_scalar(dp[:, :, :], dpa[:, :, :], -1.0, None, ALU.add).then_inc(zv, 1)
                    dve.wait_ge(zv, n(bz, ZV, "dp"))
                    if not zfirst:
                        dve.wait_ge(zt, prev(bz, ZT, "d5"))
                    for h in range(2):
                        v.tensor_tensor(onehot[:, h, :, :],
                                        iota_c[:, :].rearrange("p (o c) -> p o c", o=1).to_broadcast([P, E, CAP]),
                                        dp[:, h, :].rearrange("p (e o) -> p e o", o=1).to_broadcast([P, E, CAP]),
                                        ALU.is_equal).then_inc(zv, 1)
                if do_y:
                    mask_v(1, 2)
                    residual(0)
                    normalize(1)

                def low_slots(q):
                    dve.wait_ge(zt, n(bz, ZT, f"d{2 + q}"))
                    v.tensor_copy(xdl[:, 4 * q:4 * q + 4, bass.ds(bz * CAP, CAP)],
                                  p_z[q][:, 0:HALF].rearrange("p (e c) -> p e c", c=CAP)).then_inc(zv, 1)

                def slot_info(q):
                    dve.wait_ge(zt, n(bz, ZT, f"d{4 + q}"))
                    if not zfirst:
                        dve.wait_ge(rows_stored, bz * 16)
                    v.tensor_tensor(rows_out[:, 4 * q:4 * q + 4, :],
                                    p_z[q][0:NAUX, 0:HALF].rearrange("p (e c) -> p e c", c=CAP),
                                    aux_mask[0:NAUX, 4 * q:4 * q + 4, :], ALU.mult).then_inc(zv, 1)

                if do_z:
                    low_slots(0)
                    low_slots(1)
                    slot_info(0)
                if do_y:
                    residual(1)
                    dve.wait_ge(yv, n(b, YV, "ag1"))
                    if not early:
                        dve.wait_ge(yp, prev(b, YP, "rstd"))
                    v.tensor_scalar(ve[:, :], mv[:, :, 1], EPS_LN, None, ALU.add).then_inc(yv, 1)
                    dve.wait_ge(yp, n(b, YP, "rstd"))
                    if not (isinstance(b, int) and b < 2):
                        dve.wait_ge(acc_stored, b * 16 - 16)
                        dve.wait_ge(zp, prev2(b, ZP, "x1l"))
                        dve.wait_ge(zt, prev2(b, ZT, "x1t"))
                    for h in range(2):
                        v.tensor_scalar(x1[:, par, h, :], r32[:, h, :], mv[:, h, 0:1], rstd[:, h:h + 1],
                                        ALU.subtract, ALU.mult).then_inc(yv, 1)
                if do_z:
                    slot_info(1)

            slots_a(dve, slot)

            def info(e, par):
                dve.wait_ge(info_t, e + 1)
                p3 = p_y[:, 0:3 * NT].rearrange("p (t q) -> p t q", q=3)
                v.tensor_tensor(idx_a[:, :], p3[:, :, 0], slot_base[:, :], ALU.add).then_inc(info_v, 1)
                dve.wait_ge(info_v, e * 5 + 1)
                v.tensor_tensor(idx_a[:, :], idx_a[:, :], spare_row[:, :], ALU.subtract).then_inc(info_v, 1)
                dve.wait_ge(info_v, e * 5 + 2)
                v.tensor_tensor(idx_a[:, :], p3[:, :, 1], idx_a[:, :], ALU.mult).then_inc(info_v, 1)
                dve.wait_ge(info_v, e * 5 + 3)
                v.tensor_tensor(idx[:, par, :], idx_a[:, :], spare_row[:, :], ALU.add).then_inc(info_v, 1)
                v.tensor_copy(prob[:, par, :], p3[:, :, 2]).then_inc(info_v, 1)

            def gate_chunk(nb, first):
                for k in range(FK):
                    rows = P if k < 3 else FT
                    dve.wait_ge(silu_a, nb * FK + (k + 1))
                    if not first:
                        dve.wait_ge(gl_p, nb * FK + (k + 1 - FK))
                    h3 = bank[2 * (k % 2) + 1][:, :] if k < 3 else bank[2][0:FT, :]
                    v.tensor_tensor(g32[0:rows, k, :], sil[0:rows, k % 2, :], h3, ALU.mult).then_inc(gate_v, 1)

            def scale_rows(nb, e, c, par, cpar, nadds):
                dve.wait_ge(down_t, nb + 1)
                if nadds is not None:
                    dve.wait_ge(added[cpar], nadds)
                dve.wait_ge(info_v, e * 5 + 5)
                v.tensor_tensor(eo[:, cpar, :, :], bank[4 + cpar][:, :].rearrange("p (s m) -> p s m", s=SUB),
                                prob[:, par, c * SUB:(c + 1) * SUB].rearrange("p (s o) -> p s o", o=1)
                                .to_broadcast([P, SUB, C]), ALU.mult).then_inc(eo_v, 1)

            def experts(i, first):
                for q in range(2 * NCH):
                    par, c, cpar = q // NCH, q % NCH, q % 2
                    nb = i * (2 * NCH) + q
                    gate_chunk(nb, first and q == 0)
                    if c == 0:
                        if not first:
                            back = (0, 0) if par else (NCH // 2, NCH // 2 + 1)
                            dve.wait_ge(added[0], (i * NCH - back[0]) * SUB * 16)
                            dve.wait_ge(added[1], (i * NCH - back[1]) * SUB * 16)
                        info(i * 2 + par, par)
                    if q > 0:
                        pq = q - 1
                        cnt = None if first and pq < 2 else (i * NCH + pq // 2) * SUB * 16
                        scale_rows(nb - 1, i * 2 + pq // NCH, pq % NCH, pq // NCH, pq % 2, cnt)
                scale_rows(i * (2 * NCH) + 2 * NCH - 1, i * 2 + 1, NCH - 1, 1, 1, (i * NCH + (2 * NCH - 1) // 2) * SUB * 16)

            experts(0, True)
            with dve.Fori(1, E // 2) as i:
                experts(i, False)

            def chunk_c(k, par, i, first):
                dve.wait_ge(c_loaded[par], i * 16 + 16)
                for r in range(ROWS_C):
                    ins = v.bn_stats(cst[:, par, r, :], cx[:, par, r * C:(r + 1) * C])
                ins.then_inc(c_v, 1)
                dve.wait_ge(c_v, k * 5 + 1)
                for r in range(ROWS_C):
                    dve.sem_inc(passed_v, 1)
                    ins = v.bn_aggr(cmv[:, par, r, :], cst[:, par, r, :])
                ins.then_inc(c_v, 1)
                dve.wait_ge(c_v, k * 5 + 2)
                v.tensor_scalar(cve[:, par, :], cmv[:, par, :, 1], EPS_LN, None, ALU.add).then_inc(c_v, 1)
                dve.wait_ge(c_p, k + 1)
                if not first:
                    dve.wait_ge(c_stored[par], i * 16)
                for r in range(ROWS_C):
                    ins = v.tensor_scalar(cx[:, par, (ROWS_C + r) * C:(ROWS_C + r + 1) * C],
                                          cx[:, par, r * C:(r + 1) * C], cmv[:, par, r, 0:1],
                                          crs[:, par, r:r + 1], ALU.subtract, ALU.mult)
                    if r == ROWS_C // 2 - 1:
                        ins.then_inc(c_v, 1)
                ins.then_inc(c_v, 1)

            chunk_c(0, 0, 0, True)
            chunk_c(1, 1, 0, True)
            with dve.Fori(1, NC_CH // 2) as i:
                chunk_c(i * 2, 0, i, False)
                chunk_c(i * 2 + 1, 1, i, False)

        @block.scalar
        def _(act):
            a = nc.scalar

            def xhi(b, first=False):
                act.wait_ge(xt_loaded, b * 16 + 16)
                if not first:
                    act.wait_ge(xt, prev(b, XT, "qkv1"))
                    act.wait_ge(xv, prev(b, XV, "xlo"))
                a.activation(xh[:, :], xT32[:, :], ACT.Copy).then_inc(xa, 1)

            def exps(b, h, par, first=False):
                act.wait_ge(xv, n(b, XV, f"mn{h}"))
                if not first:
                    act.wait_ge(xv, prev(b, XV, f"f{h}"))
                a.activation(ex[:, h, :], mn[:, h, :], ACT.Exp).then_inc(xa, 1)
                act.wait_ge(xv, n(b, XV, f"f{h}"))
                if not (isinstance(b, int) and b < 2):
                    act.wait_ge(yt, prev2(b, YT, f"ctx{h}"))
                    act.wait_ge(xp, prev2(b, XP, "vl"))
                a.activation(v32[:, par, h, :, 0:DH],
                             p_qkv[:, 2 * C:3 * C].rearrange("p (h e) -> p h e", e=DH), ACT.Copy).then_inc(xa, 1)

            def evac_t(b, h, par):
                act.wait_ge(xt, n(b, XT, f"tr{h}"))
                if not (isinstance(b, int) and b < 2):
                    act.wait_ge(yt, prev2(b, YT, "ctx1"))
                a.activation(qkT[:, par, h, :, :, :].rearrange("p q j t -> p (q j) t"), p_tr, ACT.Copy)\
                    .then_inc(xa, 1)

            act.wait_ge(setup_p, 1)
            xhi(0, True)
            exps(0, 0, 0, True)
            exps(0, 1, 0, True)
            evac_t(0, 0, 0)
            evac_t(0, 1, 0)

            def slot(b, par, do_x, do_z, do_y=True):
                early = isinstance(b, int) and b == 0
                o = 1 - par
                bx, bz = b + 1, b - 1
                zfirst = isinstance(bz, int) and bz == 0

                def copy_sc(h, r, last):
                    act.wait_ge(yt, n(b, YT, f"sc{h}{r}"))
                    if last is not None:
                        act.wait_ge(yp, last)
                    a.activation(raw[:, r // 2, :], p_sc[r % 2][:, :], ACT.Copy).then_inc(ya, 1)

                def evac_c(h):
                    act.wait_ge(yt, n(b, YT, f"ct{h}"))
                    if not early:
                        act.wait_ge(yt, prev(b, YT, f"proj{h}"))
                    a.activation(cT[:, h, :], p_y[:, 0:P], ACT.Copy).then_inc(ya, 1)

                if do_x:
                    xhi(bx)
                if do_z:
                    act.wait_ge(zt, n(bz, ZT, "x1t"))
                    if not zfirst:
                        act.wait_ge(zt, prev(bz, ZT, "rt"))
                    a.activation(x1T[:, :, :].rearrange("p h t -> p (h t)"), p_z[0][:, 0:2 * P], ACT.Copy)\
                        .then_inc(za, 1)
                if do_x:
                    exps(bx, 0, o)
                if do_y:
                    copy_sc(0, 1, None if early else prev(b, YP, "am11"))
                if do_z:
                    act.wait_ge(zv, n(bz, ZV, "nm"))
                    if not zfirst:
                        act.wait_ge(zv, prev(bz, ZV, "pr"))
                    for h in range(2):
                        a.activation(el[:, h, :], p_z[0][:, h * E:(h + 1) * E], ACT.Exp, bias=nm[:, h:h + 1],
                                     accum_out=es[:, h:h + 1]).then_inc(za, 1)
                if do_x:
                    exps(bx, 1, o)
                if do_y:
                    copy_sc(0, 3, None if early else prev(b, YP, "am13"))
                if do_x:
                    evac_t(bx, 0, o)
                if do_y:
                    copy_sc(1, 1, n(b, YP, "am01"))
                    evac_c(0)
                if do_x:
                    evac_t(bx, 1, o)
                if do_y:
                    copy_sc(1, 3, n(b, YP, "am03"))
                if do_z:
                    for q in range(2):
                        act.wait_ge(zt, n(bz, ZT, f"d{q}"))
                        a.activation(xdh[:, 4 * q:4 * q + 4, bass.ds(bz * CAP, CAP)],
                                     p_z[q][:, 0:HALF].rearrange("p (e c) -> p e c", c=CAP), ACT.Copy)\
                            .then_inc(za, 1)
                if do_y:
                    evac_c(1)

            slots_a(act, slot)

            def chunk(nb, cpar, first):
                def high(k):
                    rows = P if k < 3 else FT
                    act.wait_ge(gate_v, nb * FK + (k + 1))
                    a.activation(gh[0:rows, cpar, k, :], g32[0:rows, k, :], ACT.Copy).then_inc(gh_a, 1)

                for k in range(FK):
                    rows = P if k < 3 else FT
                    act.wait_ge(up_t, nb * FK + (k + 1))
                    if not (first and k < 2):
                        act.wait_ge(gate_v, nb * FK + (k - 1))
                    h1 = bank[2 * (k % 2)][:, :] if k < 3 else bank[2][FT:P, :]
                    a.activation(sil[0:rows, k % 2, :], h1, ACT.Silu).then_inc(silu_a, 1)
                    if k == 0 and not (isinstance(nb, int) and nb < 2):
                        act.wait_ge(down_t, nb - 1)
                    if k > 0:
                        high(k - 1)
                high(FK - 1)

            for nb in range(2 * NCH):
                chunk(nb, nb % 2, nb == 0)
            with act.Fori(1, E // 2) as i:
                for q in range(2 * NCH):
                    chunk(i * (2 * NCH) + q, q % 2, False)

        @block.tensor
        def _(pe):
            t = nc.tensor

            def qkv(b, h, first=False):
                if h == 0:
                    pe.wait_ge(xv, n(b, XV, "xlo"))
                    pe.wait_ge(xa, n(b, XA, "xhi"))
                if not (first and h == 0):
                    if h:
                        pe.wait_ge(xv, n(b, XV, "f0"))
                        pe.wait_ge(xa, n(b, XA, "v0"))
                    else:
                        pe.wait_ge(xv, prev(b, XV, "f1"))
                        pe.wait_ge(xa, prev(b, XA, "v1"))
                sl_ = slice(h * P, (h + 1) * P)
                o_ = p_qkv[:, 0:3 * C]
                t.matmul(o_, xh[:, sl_], wqh[:, :], start=True, stop=False)
                t.matmul(o_, xh[:, sl_], wql[:, :], start=False, stop=False)
                t.matmul(o_, xl[:, sl_], wqh[:, :], start=False, stop=False)
                t.matmul(o_, onesb[0:96, :], bias3[:, 0:3 * C], start=False, stop=True).then_inc(xt, 1)

            def transposes(b, h, par, first=False):
                pe.wait_ge(xp, n(b, XP, f"kl{h}"))
                if not (first and h == 0):
                    pe.wait_ge(xa, n(b, XA, "T0") if h else prev(b, XA, "T1"))
                for qk in range(2):
                    for j in range(J):
                        src = stack[:, par, h, qk, 32 * j:32 * j + 32, :, :].rearrange("p c a d -> p (c a d)")
                        ins = t.transpose(p_tr[:, qk * J + j, :], src, identb[:, :])
                ins.then_inc(xt, 1)

            pe.wait_ge(setup_p, 1)
            pe.wait_ge(setup_v, NSETV)
            qkv(0, 0, True)
            qkv(0, 1, True)
            transposes(0, 0, 0, True)
            transposes(0, 1, 0, True)

            def slot(b, par, do_x, do_z, do_y=True):
                early = isinstance(b, int) and b == 0
                o = 1 - par
                bx, bz = b + 1, b - 1
                zfirst = isinstance(bz, int) and bz == 0

                def scores(h, r, wait_v, wait_p):
                    if h == 0 and r == 0:
                        pe.wait_ge(xa, n(b, XA, "T0"))
                    if h == 1 and r == 0:
                        pe.wait_ge(xa, n(b, XA, "T1"))
                    if wait_v is not None:
                        pe.wait_ge(yv if r % 2 == 0 else ya, wait_v)
                    for j in range(J):
                        ins = t.matmul(p_sc[r % 2][:, j * P:(j + 1) * P], qkT[32 * r:32 * r + 32, par, h, 1, j, :],
                                       qkT[32 * r:32 * r + 32, par, h, 0, j, :], start=True, stop=True)
                    ins.then_inc(yt, 1)

                def context(h):
                    pe.wait_ge(yv, n(b, YV, f"am{h}2"))
                    pe.wait_ge(yp, n(b, YP, f"am{h}3"))
                    pe.wait_ge(xa, n(b, XA, f"v{h}"))
                    if h:
                        pe.wait_ge(yv, n(b, YV, "cn0"))
                        pe.wait_ge(yp, n(b, YP, "slo"))
                    elif not early:
                        pe.wait_ge(yv, prev(b, YV, "cn1"))
                    first = True
                    for j in range(J):
                        for r in range(R):
                            hd = j * R + r
                            ins = t.matmul(p_ctx[:, hd * DV:(hd + 1) * DV], am[:, h, r, j, :],
                                           v32[:, par, h, hd, :], start=first, stop=(h == 0),
                                           skip_group_check=True)
                            first = False
                    if h:
                        for part, s in ((0, sh), (1, sl)):
                            for j in range(J):
                                ins = t.matmul(p_ctx[:, j * R * DV:(j + 1) * R * DV], qkT[:, par, 1, 0, j, :],
                                               s[:, j, :], start=False, stop=(part == 1), skip_group_check=True)
                    ins.then_inc(yt, 1)

                def ctx_t(h):
                    pe.wait_ge(yv, n(b, YV, f"cn{h}"))
                    if h:
                        pe.wait_ge(yv, n(b, YV, "res0"))
                    else:
                        pe.wait_ge(yv, n(b, YV, "s32"))
                    t.transpose(p_y[:, 0:P], cn[:, h, :], ident[:, :]).then_inc(yt, 1)

                def proj(h):
                    pe.wait_ge(ya, n(b, YA, f"cT{h}"))
                    t.matmul(p_y[:, 0:C], cT[:, h, :], wo32[:, :], start=True, stop=False)
                    t.matmul(p_y[:, 0:C], onesb[0:96, :], bias3[:, 3 * C:4 * C], start=False, stop=True)\
                        .then_inc(yt, 1)

                def dispatch(i):
                    part, q = i // 2, i % 2
                    if i == 0:
                        pe.wait_ge(zv, n(bz, ZV, "D1"))
                        pe.wait_ge(zp, n(bz, ZP, "x1l"))
                    if i == 1 and not zfirst:
                        pe.wait_ge(zv, prev(bz, ZV, "ax1"))
                    if part == 1:
                        pe.wait_ge(za, n(bz, ZA, f"xh{q}"))
                    if part == 2:
                        pe.wait_ge(zv, n(bz, ZV, f"xl{q}"))
                        pe.wait_ge(zp, n(bz, ZP, "pl"))
                    m = C if part < 2 else NAUX
                    src = (x1h, x1l, aux)[part]
                    for h in range(2):
                        ins = t.matmul(p_z[q][0:m, 0:HALF], src[:, h, :],
                                       onehot[:, h, 4 * q:4 * q + 4, :].rearrange("p e c -> p (e c)"),
                                       start=(h == 0), stop=(h == 1))
                    ins.then_inc(zt, 1)

                if do_x:
                    qkv(bx, 0)
                if do_z:
                    pe.wait_ge(yv, n(bz, YV, "x11"))
                    if not zfirst:
                        pe.wait_ge(zv, prev(bz, ZV, "ax0"))
                    for h in range(2):
                        ins = t.transpose(p_z[0][:, h * P:(h + 1) * P], x1[:, o, h, :], ident[:, :])
                    ins.then_inc(zt, 1)
                if do_y:
                    pe.wait_ge(xp, n(b, XP, "vl"))
                    if not early:
                        pe.wait_ge(yv, prev(b, YV, "res1"))
                    for j in range(J):
                        for part, vv in ((0, vh), (1, vl)):
                            ins = t.matmul(
                                p_y[:, j * R * DV:(j + 1) * R * DV],
                                stack[:, par, 0, 1, 32 * j:32 * j + 32, :, :].rearrange("p c a d -> p (c a d)"),
                                vv[:, par, j * R:(j + 1) * R, :].rearrange("p r e -> p (r e)"),
                                start=(part == 0), stop=(part == 1))
                    ins.then_inc(yt, 1)
                    scores(0, 0, None if early else prev(b, YV, "am12"), None)
                    scores(0, 1, None if early else prev(b, YA, "cp13"), None)
                if do_z:
                    pe.wait_ge(za, n(bz, ZA, "x1T"))
                    for h in range(2):
                        ins = t.matmul(p_z[0][:, h * E:(h + 1) * E], x1T[:, h, :], gt32[:, :],
                                       start=True, stop=True)
                    ins.then_inc(zt, 1)
                if do_x:
                    qkv(bx, 1)
                if do_y:
                    scores(0, 2, n(b, YV, "am00"), None)
                    scores(0, 3, n(b, YA, "cp01"), None)
                if do_x:
                    transposes(bx, 0, o)
                if do_y:
                    scores(1, 0, n(b, YV, "am02"), None)
                    scores(1, 1, n(b, YA, "cp03"), None)
                if do_z:
                    pe.wait_ge(zv, n(bz, ZV, "M"))
                    po = p_z[0][:, 32:32 + 2 * E]
                    t.matmul(po[:, 0:E], trib[:, :], mb[:, 0, :], start=True, stop=True)
                    t.matmul(po[:, E:2 * E], onesb[:, :], mb[:, 0, :], start=True, stop=False)
                    t.matmul(po[:, E:2 * E], trib[:, :], mb[:, 1, :], start=False, stop=True).then_inc(zt, 1)
                if do_y:
                    context(0)
                    scores(1, 2, n(b, YV, "am10"), None)
                    ctx_t(0)
                if do_x:
                    transposes(bx, 1, o)
                if do_y:
                    scores(1, 3, n(b, YA, "cp11"), None)
                    proj(0)
                if do_z:
                    dispatch(0)
                    dispatch(1)
                if do_y:
                    context(1)
                if do_z:
                    dispatch(2)
                if do_y:
                    ctx_t(1)
                if do_z:
                    dispatch(3)
                    dispatch(4)
                if do_y:
                    proj(1)
                if do_z:
                    dispatch(5)

            slots_a(pe, slot)

            pe.wait_ge(za, n(B - 1, ZA, "xh1"))
            pe.wait_ge(zv, n(B - 1, ZV, "ax1"))
            pe.wait_ge(yv, n(B - 1, YV, "x11"))

            def info(e, par, first):
                pe.wait_ge(rows_loaded, e * 16 + 16)
                if not first:
                    pe.wait_ge(info_v, e * 5)
                for s in range(NT):
                    ins = t.matmul(p_y[:, 3 * s:3 * s + 3], rows_in[:, par, s * P:(s + 1) * P], sel[0:NAUX, :],
                                   start=True, stop=True)
                ins.then_inc(info_t, 1)

            def up(e, nb, par, c, first):
                for k in range(FK):
                    pair = ((2 * (k % 2), k * P), (2 * (k % 2) + 1, (3 + k) * P)) if k < 3 else ((2, 6 * P),)
                    if not (first and k < 2):
                        pe.wait_ge(gate_v, nb * FK + (k - 1))
                    for bk, w0 in pair:
                        o_ = bank[bk][:, :]
                        xs = bass.ds(c * CH, CH)
                        rh = xdh[:, bass.ds(e, 1), xs].rearrange("p o s -> p (o s)")
                        rl = xdl[:, bass.ds(e, 1), xs].rearrange("p o s -> p (o s)")
                        t.matmul(o_, wh[:, par, w0:w0 + P], rh, start=True, stop=False)
                        t.matmul(o_, wh[:, par, w0:w0 + P], rl, start=False, stop=False)
                        ins = t.matmul(o_, wl[:, par, w0:w0 + P], rh, start=False, stop=True)
                    ins.then_inc(up_t, 1)

            def down(nb, par, cpar, first):
                pe.wait_ge(gl_p, nb * FK + FK)
                if not first:
                    pe.wait_ge(eo_v, nb - 1)
                for s in range(SUB):
                    o_ = bank[4 + cpar][:, s * C:(s + 1) * C]
                    ss = slice(s * P, (s + 1) * P)
                    for k in range(FK):
                        rows = P if k < 3 else FT
                        w = slice(2 * F + k * C, 2 * F + (k + 1) * C)
                        t.matmul(o_, gh[0:rows, cpar, k, ss], wh[0:rows, par, w], start=(k == 0), stop=False)
                        t.matmul(o_, gh[0:rows, cpar, k, ss], wl[0:rows, par, w], start=False, stop=False)
                        ins = t.matmul(o_, gl[0:rows, cpar, k, ss], wh[0:rows, par, w], start=False,
                                       stop=(k == FK - 1))
                ins.then_inc(down_t, 1)

            def experts(i, first):
                for q in range(2 * NCH):
                    par, c, cpar = q // NCH, q % NCH, q % 2
                    nb = i * (2 * NCH) + q
                    if c == 0:
                        pe.wait_ge(w_split_l, i * 2 + par + 1)
                    up(i * 2 + par, nb, par, c, first and q == 0)
                    if c == 0:
                        info(i * 2 + par, par, first and par == 0)
                    if q > 0:
                        down(nb - 1, (q - 1) // NCH, (q - 1) % 2, first and q - 1 < 2)
                down(i * (2 * NCH) + 2 * NCH - 1, 1, 1, False)

            experts(0, True)
            with pe.Fori(1, E // 2) as i:
                experts(i, False)




def kernel(**inputs):
    import numpy as np

    import concourse.bacc as bacc
    from concourse import mybir
    from concourse.bass_utils import run_bass_kernel_spmd

    fp32 = mybir.dt.float32
    x = np.asarray(inputs["L0_attn_x"])
    nb, t, c = x.shape
    x2 = np.ascontiguousarray(x.reshape(nb * t, c))
    arrays = {
        "x": x2,
        "x_t": np.ascontiguousarray(x2.T),
        "wqkv_t": np.ascontiguousarray(np.asarray(inputs["L0_attn_w_qkv"]).T),
        "bqkv": np.ascontiguousarray(np.asarray(inputs["L0_attn_b_qkv"]).reshape(1, -1)),
        "wout_t": np.ascontiguousarray(np.asarray(inputs["L0_attn_w_out"]).T),
        "bout": np.ascontiguousarray(np.asarray(inputs["L0_attn_b_out"]).reshape(1, -1)),
        "gate_t": np.ascontiguousarray(np.asarray(inputs["L0_ffn_gate_w"]).T),
        "w1": np.ascontiguousarray(np.asarray(inputs["L0_ffn_w1"])),
        "w2": np.ascontiguousarray(np.asarray(inputs["L0_ffn_w2"])),
        "w3": np.ascontiguousarray(np.asarray(inputs["L0_ffn_w3"])),
    }
    nc = bacc.Bacc("TRN2", target_bir_lowering=False, num_devices=1)
    aps = [nc.dram_tensor(k, a.shape, fp32, kind="ExternalInput").ap() for k, a in arrays.items()]
    e = arrays["w1"].shape[0]
    cap = int(t * 2 / e * 1.25)
    acc = nc.dram_tensor("acc", (nb * t + nb * cap, c), fp32, kind="Internal").ap()
    slot_rows = nc.dram_tensor("slot_rows", (e, 3 * e + 2, nb * cap), mybir.dt.bfloat16, kind="Internal").ap()
    out = nc.dram_tensor("out", (nb * t, c), fp32, kind="ExternalOutput").ap()
    build(nc, *aps, acc, slot_rows, out)
    r = run_bass_kernel_spmd(nc, [arrays], core_ids=[0])
    return np.asarray(r.results[0]["out"]).reshape(nb, t, c)
```

```python
def build(nc, x, xt_in, wqkv, bqkv, wout, bout, gate, w1, w2, w3, acc, slot_rows, out):
    from contextlib import ExitStack

    import concourse.bass as bass
    from concourse import mybir

    fp32 = mybir.dt.float32
    bf16 = mybir.dt.bfloat16
    u32 = mybir.dt.uint32
    ACT = mybir.ActivationFunctionType
    ALU = mybir.AluOpType

    TOK, C = x.shape
    P = 128
    T = 256
    B = TOK // T
    H = 16
    DH = C // H
    DV = DH + 1
    J = 4
    R = H // J
    E, _, F = w1.shape
    K_TOP = 2
    CAP = int(T * K_TOP / E * 1.25)
    SLOTS = B * CAP
    FK = 4
    FT = F - 3 * P
    CH = 512
    NCH = SLOTS // CH
    SUB = CH // P
    NT = SLOTS // P
    NAUX = 3 * E + 2
    HALF = E // 2 * CAP
    EPS_ATT = 1e-6
    EPS_LN = 1e-5
    ROWS_C = 8
    NC_CH = TOK // (P * ROWS_C)

    XT = ["qkv0", "qkv1", "tr0", "tr1"]
    XA = ["xhi", "ex0", "v0", "qh0", "kh0", "vh0", "ex1", "v1", "T0", "qh1", "kh1", "vh1", "T1"]
    XV = ["mn0", "f0", "mn1", "f1"]
    XP = ["xlo", "ql0", "kl0", "vl0", "ql1", "kl1", "vl1"]
    YT = ["state", "sc00", "sc01", "sc02", "sc03", "ctx00", "sc10", "ctx01", "sc11", "ctx02", "sc12", "ctx03",
          "sc13", "ctx10", "ctx11", "ctx12", "ctx13", "ctx"]
    YV = ["s32", "am00", "am01", "am02", "lo00", "am03", "am10", "lo02", "am11", "am12", "lo10", "am13", "lo12",
          "den", "rec", "cn"]
    YA = ["shi", "hi00", "hi01", "hi02", "hi03", "hi10", "hi11", "hi12", "hi13"]
    YP = ["slo", "lo01", "lo03", "lo11", "lo13"]
    WT = ["ct", "proj"]
    WA = ["cT"]
    WV = ["res", "bn0", "bn1", "ag0", "ag1", "ve", "x10", "x11"]
    WP = ["rstd"]
    ZT = ["x1t", "rt", "pos", "d0", "d1", "d2", "d3", "d4", "d5"]
    ZA = ["x1h", "x1T", "el0", "el1", "xh0", "xh1", "xl0", "xl1"]
    ZV = ["mx0", "mx1", "nm", "rs", "pr", "tp0", "tp1", "ti0", "ti1", "tif", "m0", "m1", "M",
          "val", "dpa", "dp", "D0", "D1", "ax0", "ax1"]
    ZP = ["x1l", "ph", "r1", "pm", "pl"]

    def n(b, steps, step):
        return b * len(steps) + (steps.index(step) + 1)

    def prev(b, steps, step):
        return b * len(steps) + (steps.index(step) + 1 - len(steps))

    def prev2(b, steps, step):
        return b * len(steps) + (steps.index(step) + 1 - 2 * len(steps))

    ctx = ExitStack()
    with ctx:
        def sb(name, shape, dt=fp32):
            return ctx.enter_context(nc.sbuf_tensor(name, shape, dt))

        def sem(name):
            return ctx.enter_context(nc.semaphore(name))

        ident = sb("ident", [P, P])
        identb = sb("identb", [P, P], bf16)
        tri = sb("tri", [P, P])
        trib = sb("trib", [P, P], bf16)
        onesb = sb("onesb", [P, P], bf16)
        head_mask = sb("head_mask", [P, J, R, DV])
        iota_c = sb("iota_c", [P, CAP], bf16)
        iota_e = sb("iota_e", [P, E])
        aux_mask = sb("aux_mask", [32, E, CAP])
        sel = sb("sel", [32, 3], bf16)
        half_pow = sb("half_pow", [P, ROWS_C])
        slot_base = sb("slot_base", [P, NT])
        spare_row = sb("spare_row", [P, NT])
        zrow = sb("zrow", [P, C])
        wq32 = sb("wq32", [P, 3 * C])
        wqh = sb("wqh", [P, 3 * C], bf16)
        wql = sb("wql", [P, 3 * C], bf16)
        wo32 = sb("wo32", [P, C])
        gt32 = sb("gt32", [P, E])
        bias32 = sb("bias32", [96, 4 * C])
        bias_h = sb("bias_h", [96, 4 * C], bf16)
        bias_m = sb("bias_m", [96, 4 * C], bf16)
        bias3 = sb("bias3", [96, 4 * C], bf16)
        xT32 = sb("xT32", [P, T])
        x32 = sb("x32", [P, 2, 2, C])
        xh = sb("xh", [P, T], bf16)
        xl = sb("xl", [P, T], bf16)
        mn = sb("mn", [P, 2, 2 * C])
        ex = sb("ex", [P, 2, 2 * C])
        feat = sb("feat", [P, 2, 2 * C])
        stack = sb("stack", [P, 2, 2, 2, C, 2, 2], bf16)
        qkT = sb("qkT", [P, 2, 2, 2, J, P], bf16)
        v32 = sb("v32", [P, 2, 2, H, DV])
        vh = sb("vh", [P, 2, 2, H, DV], bf16)
        vl = sb("vl", [P, 2, 2, H, DV], bf16)
        s32 = sb("s32", [P, J, R * DV])
        sh = sb("sh", [P, J, R * DV], bf16)
        sl = sb("sl", [P, J, R * DV], bf16)
        am = sb("am", [P, 2, R, J, P])
        den = sb("den", [P, 2 * H])
        rec = sb("rec", [P, 2 * H])
        cn = sb("cn", [P, 2, C])
        cT = sb("cT", [P, 2, P])
        r32 = sb("r32", [P, 2, C])
        bn = sb("bn", [P, 2, 6])
        mv = sb("mv", [P, 2, 2])
        ve = sb("ve", [P, 2])
        rstd = sb("rstd", [P, 2])
        x1 = sb("x1", [P, 2, 2, C])
        x1h = sb("x1h", [P, 2, C], bf16)
        x1l = sb("x1l", [P, 2, C], bf16)
        x1T = sb("x1T", [P, 2, P])
        mx = sb("mx", [P, 2, 8])
        nm = sb("nm", [P, 2])
        el = sb("el", [P, 2, E])
        es = sb("es", [P, 2])
        rs = sb("rs", [P, 2])
        pr = sb("pr", [P, 2, E])
        tp = sb("tp", [P, 2, 8])
        ti = sb("ti", [P, 2, 8], u32)
        tif = sb("tif", [P, 2, K_TOP])
        m0 = sb("m0", [P, 2, E])
        m1 = sb("m1", [P, 2, E])
        mb = sb("mb", [P, 2, E], bf16)
        val = sb("val", [P, 2, E])
        dpa = sb("dpa", [P, 2, E])
        dp = sb("dp", [P, 2, E], bf16)
        onehot = sb("onehot", [P, 2, E, CAP], bf16)
        aux = sb("aux", [P, 2, NAUX], bf16)
        pres = sb("pres", [P, 2, E])
        rows_out = sb("rows_out", [NAUX, E, CAP], bf16)
        xdh = sb("xdh", [P, E, SLOTS], bf16)
        xdl = sb("xdl", [P, E, SLOTS], bf16)
        wst = sb("wst", [P, 2 * F + FK * C])
        wh = sb("wh", [P, 2, 2 * F + FK * C], bf16)
        wl = sb("wl", [P, 2, 2 * F + FK * C], bf16)
        rows_in = sb("rows_in", [NAUX, 2, SLOTS], bf16)
        idx_a = sb("idx_a", [P, NT])
        idx = sb("idx", [P, 2, NT], u32)
        prob = sb("prob", [P, 2, NT])
        sil = sb("sil", [P, 2, CH])
        gh = sb("gh", [P, 2, FK, CH], bf16)
        am32 = am[:, 0, :, :, :]
        am_hl = am[:, 1, :, :, :].rearrange("p r j t -> p (r j t)").bitcast(bf16)\
            .rearrange("p (q r j t) -> p q r j t", q=2, r=R, j=J)
        g32 = am[:, 0, :, :, :].rearrange("p r j t -> p r (j t)")
        gl = am[:, 1, :, :, :].rearrange("p r j t -> p (r j t)").bitcast(bf16)\
            .rearrange("p (q k s) -> p q k s", q=2, k=FK)
        eo = sb("eo", [P, 2, SUB, C])
        cx = am[:, :, :, :, :].rearrange("p h r j t -> p h (r j t)")
        cst = sb("cst", [P, 2, ROWS_C, 6])
        cmv = sb("cmv", [P, 2, ROWS_C, 2])
        cve = sb("cve", [P, 2, ROWS_C])
        crs = sb("crs", [P, 2, ROWS_C])

        bank = [ctx.enter_context(nc.psum_tensor(f"bank{i}", [P, 512], fp32)) for i in range(8)]
        p_qkv = bank[0]
        p_tr = bank[2][:, :].bitcast(bf16).rearrange("p (s t) -> p s t", s=8)
        p_sc = [bank[3], bank[4]]
        p_ctx = bank[5][:, 0:2 * H * DV].rearrange("p (h q) -> p h q", h=2)
        p_state = bank[5][:, 2 * H * DV:3 * H * DV]
        p_y = bank[6]
        p_z = [bank[7], bank[1]]

        const_ready = sem("const_ready")
        wa_loaded = sem("wa_loaded")
        setup_v = sem("setup_v")
        setup_p = sem("setup_p")
        passed_v = sem("passed_v")
        passed_p = sem("passed_p")
        passed_s = sem("passed_s")
        xt_loaded = sem("xt_loaded")
        x_loaded = sem("x_loaded")
        xt, xa, xv, xp = (sem(s) for s in ("xt", "xa", "xv", "xp"))
        yt, ya, yv, yp = (sem(s) for s in ("yt", "ya", "yv", "yp"))
        wt, wa, wv, wp = (sem(s) for s in ("wt", "wa", "wv", "wp"))
        zt, za, zv, zp = (sem(s) for s in ("zt", "za", "zv", "zp"))
        acc_stored = sem("acc_stored")
        spare_stored = sem("spare_stored")
        zrow_ready = sem("zrow_ready")
        rows_stored = sem("rows_stored")
        w_loaded = sem("w_loaded")
        rows_loaded = sem("rows_loaded")
        w_split_h = sem("w_split_h")
        w_split_l = sem("w_split_l")
        info_t = sem("info_t")
        info_v = sem("info_v")
        up_t = sem("up_t")
        silu_a = sem("silu_a")
        gate_v = sem("gate_v")
        gh_a = sem("gh_a")
        gl_v = sem("gl_v")
        down_t = sem("down_t")
        eo_v = sem("eo_v")
        added = [sem("added0"), sem("added1")]
        c_loaded = [sem("c_loaded0"), sem("c_loaded1")]
        c_v = sem("c_v")
        c_p = sem("c_p")
        c_stored = [sem("c_stored0"), sem("c_stored1")]

        NSETV = 13
        block = ctx.enter_context(nc.Block())

        def since(b, first):
            return not (isinstance(b, int) and b < first)

        def stages(b):
            if not isinstance(b, int):
                return True, True, True, True
            return b + 1 < B, b < B, 1 <= b <= B, 2 <= b <= B + 1

        def slots_a(engine, slot, ahead=1):
            pairs = (B - ahead - 3) // 2
            for b in range(3):
                slot(b, b % 2)
            with engine.Fori(0, pairs) as i:
                slot(i * 2 + 3, 1)
                slot(i * 2 + 4, 0)
            for b in range(3 + 2 * pairs, B + 2):
                slot(b, b % 2)

        @block.sync
        def _(sp):
            sp.dma_start(wq32[:, :], wqkv).then_inc(wa_loaded, 16)
            sp.dma_start(wo32[:, :], wout).then_inc(wa_loaded, 16)
            sp.dma_start(gt32[:, :], gate).then_inc(wa_loaded, 16)
            for row in (0, 32, 64):
                sp.dma_start(bias32[row:row + 1, 0:3 * C], bqkv).then_inc(wa_loaded, 16)
                sp.dma_start(bias32[row:row + 1, 3 * C:4 * C], bout).then_inc(wa_loaded, 16)

            def load_xt(b):
                if since(b, 1):
                    sp.wait_ge(xt_loaded, b * 16)
                    sp.wait_ge(xa, prev(b, XA, "xhi"))
                    sp.wait_ge(xp, prev(b, XP, "xlo"))
                    sp.sem_inc(passed_s, 1)
                sp.dma_start(xT32[:, :], xt_in[:, bass.ds(b * T, T)]).then_inc(xt_loaded, 16)

            load_xt(0)
            load_xt(1)

            def slot(b, par):
                do_x, do_y, do_w, do_z = stages(b)
                bw, bz = b - 1, b - 2
                if since(b, 0) and not (isinstance(b, int) and b + 2 >= B):
                    load_xt(b + 2)
                if do_y:
                    if since(b, 2):
                        sp.wait_ge(wv, prev2(b, WV, "res"))
                        sp.sem_inc(passed_s, 1)
                        sp.wait_ge(x_loaded, b * 16)
                    elif b == 1:
                        sp.wait_ge(x_loaded, 16)
                    sp.sem_inc(passed_s, 1)
                    sp.dma_start(x32[:, par, :, :], x[bass.ds(b * T, T), :].rearrange("(h p) c -> p h c", h=2))\
                        .then_inc(x_loaded, 16)
                if do_w:
                    sp.wait_ge(wv, n(bw, WV, "x11"))
                    sp.sem_inc(passed_s, 1)
                    sp.dma_start(acc[bass.ds(bw * T, T), :].rearrange("(h p) c -> p h c", h=2),
                                 x1[:, 1 - par, :, :]).then_inc(acc_stored, 16)
                if do_z:
                    sp.wait_ge(zv, n(bz, ZV, "ax1"))
                    sp.sem_inc(passed_s, 1)
                    if since(bz, 1):
                        sp.wait_ge(rows_stored, bz * 16)
                    sp.sem_inc(passed_s, 1)
                    sp.dma_start(slot_rows[:, :, bass.ds(bz * CAP, CAP)].rearrange("e a c -> a e c"),
                                 rows_out[:, :, :]).then_inc(rows_stored, 16)

            def load_expert(e, par, first=False):
                if not first:
                    sp.wait_ge(w_split_l, e)
                    sp.wait_ge(w_split_h, e)
                for col, src, lo, hi in ((0, w1, 0, 3 * P), (3 * P, w3, 0, 3 * P), (6 * P, w3, 3 * P, F),
                                         (6 * P + FT, w1, 3 * P, F)):
                    s = src[bass.ds(e, 1), :, lo:hi].rearrange("o m f -> m (o f)")
                    sp.dma_start(wst[:, col:col + hi - lo], s).then_inc(w_loaded, 16)
                s = w2[bass.ds(e, 1), 0:3 * P, :].rearrange("o (k p) m -> p (o k) m", p=P)
                sp.dma_start(wst[:, 2 * F:2 * F + 3 * C].rearrange("p (k m) -> p k m", k=3), s)\
                    .then_inc(w_loaded, 16)
                s = w2[bass.ds(e, 1), 3 * P:F, :].rearrange("o f m -> f (o m)")
                sp.dma_start(wst[0:FT, 2 * F + 3 * C:], s).then_inc(w_loaded, 16)

            sp.wait_ge(zrow_ready, 2)
            sp.dma_start(acc[TOK:TOK + SLOTS, :].rearrange("(s p) c -> p s c", p=P),
                         zrow[:, :].rearrange("p (o c) -> p o c", o=1).to_broadcast([P, NT, C]))\
                .then_inc(spare_stored, 16)
            load_expert(0, 0, True)

            slots_a(sp, slot, ahead=2)


            def load_rows(e, par):
                sp.dma_start(rows_in[:, par, :], slot_rows[bass.ds(e, 1), :, :].rearrange("o a s -> a (o s)"))\
                    .then_inc(rows_loaded, 16)

            sp.wait_ge(rows_stored, 16 * B)
            load_rows(0, 0)

            def next_expert(e, par, last=False):
                load_expert(e + 1, 1 - par)
                sp.wait_ge(rows_loaded, e * 16 + 16)
                sp.wait_ge(info_t, e)
                load_rows(e + 1, 1 - par)

            with sp.Fori(0, E // 2 - 1) as i:
                next_expert(i * 2, 0)
                next_expert(i * 2 + 1, 1)
            next_expert(E - 2, 0)

            for q in range(2):
                sp.wait_ge(added[q], E * NCH // 2 * SUB * 16)
            sp.wait_ge(spare_stored, 16)

            def rows_of(t, k):
                return t[bass.ds(k * P * ROWS_C, P * ROWS_C), :].rearrange("(p r) c -> p (r c)", p=P)

            def load_c(k, par):
                sp.dma_start(cx[:, par, 0:ROWS_C * C], rows_of(acc, k)).then_inc(c_loaded[par], 16)

            load_c(0, 0)
            load_c(1, 1)

            def store_c(i, par, more):
                k = i * 2 + par
                sp.wait_ge(c_v, k * 5 + 5)
                sp.dma_start(rows_of(out, k), cx[:, par, ROWS_C * C:2 * ROWS_C * C]).then_inc(c_stored[par], 16)
                if more:
                    load_c(k + 2, par)

            with sp.Fori(0, NC_CH // 2 - 1) as i:
                store_c(i, 0, True)
                store_c(i, 1, True)
            store_c(NC_CH // 2 - 1, 0, False)
            store_c(NC_CH // 2 - 1, 1, False)
            sp.wait_ge(acc_stored, 16 * B)
            for q in range(2):
                sp.wait_ge(c_stored[q], NC_CH // 2 * 16)

        @block.gpsimd
        def _(pool):
            g = nc.gpsimd
            made = [0]

            def link(ins):
                made[0] += 1
                ins.then_inc(const_ready, 1)
                pool.wait_ge(const_ready, made[0])

            link(g.memset(ident[:, :], 0.0))
            link(g.affine_select(out=ident[:, :], in_=ident[:, :], compare_op=ALU.not_equal, fill=1.0, base=0,
                                 pattern=[[-1, P]], channel_multiplier=1))
            link(g.tensor_copy(identb[:, :], ident[:, :]))
            link(g.memset(tri[:, :], 1.0))
            link(g.affine_select(out=tri[:, :], in_=tri[:, :], compare_op=ALU.is_ge, fill=0.0, base=0,
                                 pattern=[[1, P]], channel_multiplier=-1))
            link(g.tensor_copy(trib[:, :], tri[:, :]))
            link(g.memset(onesb[:, :], 1.0))
            link(g.memset(head_mask[:, :, :, :], 1.0))
            link(g.affine_select(out=head_mask[:, :, :, :], in_=head_mask[:, :, :, :], compare_op=ALU.is_ge,
                                 fill=0.0, base=0, pattern=[[0, J], [-32, R], [0, DV]], channel_multiplier=1))
            link(g.affine_select(out=head_mask[:, :, :, :], in_=head_mask[:, :, :, :], compare_op=ALU.is_ge,
                                 fill=0.0, base=31, pattern=[[0, J], [32, R], [0, DV]], channel_multiplier=-1))
            link(g.iota(iota_c[:, :], [[1, CAP]], base=0, channel_multiplier=0,
                        allow_small_or_imprecise_dtypes=True))
            link(g.iota(iota_e[:, :], [[1, E]], base=0, channel_multiplier=0,
                        allow_small_or_imprecise_dtypes=True))
            link(g.memset(aux_mask[:, :, :], 0.0))
            for part in range(3):
                link(g.affine_select(out=aux_mask[:, :, :], in_=aux_mask[:, :, :], compare_op=ALU.not_equal,
                                     fill=1.0, base=-part * E, pattern=[[-1, E], [0, CAP]],
                                     channel_multiplier=1))
            link(g.affine_select(out=aux_mask[:, :, :], in_=aux_mask[:, :, :], compare_op=ALU.is_ge,
                                 fill=1.0, base=3 * E - 1, pattern=[[0, E], [0, CAP]], channel_multiplier=-1))
            link(g.memset(sel[:, :], 0.0))
            link(g.affine_select(out=sel[:, 0:2], in_=sel[:, 0:2], compare_op=ALU.not_equal, fill=1.0,
                                 base=-3 * E, pattern=[[-1, 2]], channel_multiplier=1))
            link(g.affine_select(out=sel[:, 2:3], in_=sel[:, 2:3], compare_op=ALU.is_ge, fill=1.0,
                                 base=-3 * E, pattern=[[0, 1]], channel_multiplier=1))
            link(g.memset(aux[:, :, 3 * E + 1:3 * E + 2], 1.0))
            link(g.iota(aux[:, :, 3 * E:3 * E + 1], [[P, 2], [0, 1]], base=0, channel_multiplier=1,
                        allow_small_or_imprecise_dtypes=True))
            link(g.iota(spare_row[:, :], [[P, NT]], base=TOK, channel_multiplier=1,
                        allow_small_or_imprecise_dtypes=True))
            link(g.memset(v32[:, :, :, :, :], 1.0))
            g.memset(zrow[:, :], 0.0).then_inc(zrow_ready, 1)
            g.memset(wst[:, :], 0.0).then_inc(zrow_ready, 1)
            g.memset(half_pow[:, :], -0.5).then_inc(setup_p, 1)

            def x_low(b):
                pool.wait_ge(xa, n(b, XA, "xhi"))
                if since(b, 1):
                    pool.wait_ge(xt, prev(b, XT, "qkv1"))
                g.tensor_tensor(xl[:, :], xT32[:, :], xh[:, :], ALU.subtract).then_inc(xp, 1)

            def stack_low(b, h, par):
                q2 = feat[:, h, 0:C].rearrange("p (c o) -> p c o", o=1).to_broadcast([P, C, 2])
                k2 = feat[:, h, C:2 * C].rearrange("p (c o) -> p c o", o=1).to_broadcast([P, C, 2])
                sq, sk = stack[:, par, h, 0, :, :, :], stack[:, par, h, 1, :, :, :]
                if since(b, 2):
                    pool.wait_ge(xt, prev2(b, XT, f"tr{h}"))
                    pool.wait_ge(yt, prev2(b, YT, "state"))
                pool.wait_ge(xa, n(b, XA, f"qh{h}"))
                g.tensor_tensor(sq[:, :, :, 1], q2, sq[:, :, :, 0], ALU.subtract).then_inc(xp, 1)
                pool.wait_ge(xa, n(b, XA, f"kh{h}"))
                g.tensor_tensor(sk[:, :, 1, :], k2, sk[:, :, 0, :], ALU.subtract).then_inc(xp, 1)

            def v_low(b, h, par):
                pool.wait_ge(xa, n(b, XA, f"vh{h}"))
                if since(b, 2):
                    pool.wait_ge(yt, prev2(b, YT, "ctx"))
                g.tensor_tensor(vl[:, par, h, :, :], v32[:, par, h, :, :], vh[:, par, h, :, :], ALU.subtract)\
                    .then_inc(xp, 1)

            def split_weights(e, par):
                pool.wait_ge(w_loaded, e * 96 + 96)
                if not (isinstance(e, int) and e < 2):
                    pool.wait_ge(down_t, e * NCH - NCH)
                pool.sem_inc(passed_p, 1)
                g.tensor_copy(wh[:, par, :], wst[:, :]).then_inc(w_split_h, 1)
                pool.wait_ge(w_split_h, e + 1)
                g.tensor_tensor(wl[:, par, :], wst[:, :], wh[:, par, :], ALU.subtract).then_inc(w_split_l, 1)

            x_low(0)
            stack_low(0, 0, 0)
            v_low(0, 0, 0)
            stack_low(0, 1, 0)
            v_low(0, 1, 0)

            def slot(b, par):
                do_x, do_y, do_w, do_z = stages(b)
                o = 1 - par
                bx, bw, bz = b + 1, b - 1, b - 2
                if do_x:
                    x_low(bx)
                if do_y:
                    pool.wait_ge(ya, n(b, YA, "shi"))
                    if since(b, 1):
                        pool.wait_ge(yt, prev(b, YT, "ctx"))
                    g.tensor_tensor(sl[:, :, :], s32[:, :, :], sh[:, :, :], ALU.subtract).then_inc(yp, 1)
                def scores_low(h, r):
                    if not do_y:
                        return
                    pool.wait_ge(ya, n(b, YA, f"hi{h}{r}"))
                    if h:
                        pool.wait_ge(yt, n(b, YT, f"ctx0{r}"))
                    elif since(b, 1):
                        pool.wait_ge(yt, prev(b, YT, f"ctx1{r}"))
                    g.tensor_tensor(am_hl[:, 1, r, :, :], am32[:, r, :, :], am_hl[:, 0, r, :, :], ALU.subtract)\
                        .then_inc(yp, 1)

                if do_x:
                    stack_low(bx, 0, o)
                scores_low(0, 1)
                if do_x:
                    v_low(bx, 0, o)
                if do_z:
                    pool.wait_ge(za, n(bz, ZA, "x1h"))
                    if since(bz, 1):
                        pool.wait_ge(zt, prev(bz, ZT, "d3"))
                    g.tensor_tensor(x1l[:, :, :], x1[:, par, :, :], x1h[:, :, :], ALU.subtract).then_inc(zp, 1)
                if do_w:
                    pool.wait_ge(wv, n(bw, WV, "ve"))
                    if since(bw, 1):
                        pool.wait_ge(wv, prev(bw, WV, "x11"))
                    g.tensor_tensor(rstd[:, :], ve[:, :], half_pow[:, 0:2], ALU.pow).then_inc(wp, 1)
                scores_low(0, 3)
                if do_z:
                    pool.wait_ge(zv, n(bz, ZV, "pr"))
                    if since(bz, 1):
                        pool.wait_ge(zt, prev(bz, ZT, "d5"))
                    pool.sem_inc(passed_p, 1)
                    g.tensor_copy(aux[:, :, 0:E], pr[:, :, :]).then_inc(zp, 1)
                    pool.wait_ge(zp, n(bz, ZP, "ph"))
                    g.tensor_tensor(pres[:, :, :], pr[:, :, :], aux[:, :, 0:E], ALU.subtract).then_inc(zp, 1)
                    pool.wait_ge(zp, n(bz, ZP, "r1"))
                    pool.sem_inc(passed_p, 1)
                    g.tensor_copy(aux[:, :, E:2 * E], pres[:, :, :]).then_inc(zp, 1)
                    pool.wait_ge(zp, n(bz, ZP, "pm"))
                    g.tensor_tensor(aux[:, :, 2 * E:3 * E], pres[:, :, :], aux[:, :, E:2 * E], ALU.subtract)\
                        .then_inc(zp, 1)
                scores_low(1, 1)
                if do_x:
                    stack_low(bx, 1, o)
                    v_low(bx, 1, o)
                scores_low(1, 3)
                if isinstance(b, int) and b == B - 1:
                    split_weights(0, 0)

            slots_a(pool, slot)

            def add_rows(nb, c, par, cpar):
                pool.wait_ge(eo_v, nb + 1)
                pool.sem_inc(passed_p, 1)
                for s in range(SUB):
                    g.indirect_dma_start(
                        out=acc, out_offset=bass.IndirectOffsetOnAxis(
                            ap=idx[:, par, c * SUB + s:c * SUB + s + 1], axis=0),
                        in_=eo[:, cpar, s, :], in_offset=None, compute_op=ALU.add).then_inc(added[cpar], 16)

            link(g.memset(slot_base[:, :], 0.0))
            for b in range(1, B):
                t0, t1 = max(0, (b * CAP) // P), NT
                v = slot_base[:, t0:t1]
                link(g.affine_select(out=v, in_=v, compare_op=ALU.is_ge, fill=float(T * b),
                                     base=b * CAP - 1 - P * t0, pattern=[[-P, t1 - t0]], channel_multiplier=-1))
            g.memset(crs[:, :, :], 0.0).then_inc(setup_p, 1)
            pool.wait_ge(acc_stored, 16 * B)
            pool.wait_ge(spare_stored, 16)

            def experts(i, first, last):
                for q in range(2 * NCH):
                    par, c = q // NCH, q % NCH
                    nb = i * (2 * NCH) + q
                    if c == 0:
                        if par or not first:
                            pool.wait_ge(added[0], (i * NCH + (NCH // 2 + 1 if par else 0)) * SUB * 16)
                            pool.wait_ge(added[1], (i * NCH + (NCH // 2 if par else 0)) * SUB * 16)
                    add_rows(nb, c, par, q % 2)
                    if c == 0 and not (last and par == 1):
                        split_weights(i * 2 + par + 1, 1 - par)

            experts(0, True, False)
            with pool.Fori(1, E // 2 - 1) as i:
                experts(i, False, False)
            experts(E // 2 - 1, False, True)

            def chunk_c(k, par):
                pool.wait_ge(c_v, k * 5 + 3)
                g.tensor_tensor(crs[:, par, :], cve[:, par, :], half_pow[:, :], ALU.pow).then_inc(c_p, 1)

            with pool.Fori(0, NC_CH // 2) as i:
                chunk_c(i * 2, 0)
                chunk_c(i * 2 + 1, 1)

        @block.vector
        def _(dve):
            v = nc.vector
            dve.wait_ge(wa_loaded, 9 * 16)
            dve.wait_ge(setup_p, 1)
            made = [0]

            def link(ins):
                made[0] += 1
                ins.then_inc(setup_v, 1)
                dve.wait_ge(setup_v, made[0])

            link(v.tensor_copy(wqh[:, :], wq32[:, :]))
            link(v.tensor_tensor(wql[:, :], wq32[:, :], wqh[:, :], ALU.subtract))
            link(v.memset(bias3[:, :], 0.0))
            for row in (0, 32, 64):
                link(v.tensor_copy(bias_h[row:row + 1, :], bias32[row:row + 1, :]))
            link(v.tensor_copy(bias3[0:1, :], bias_h[0:1, :]))
            for row in (32, 64):
                link(v.tensor_tensor(bias32[row:row + 1, :], bias32[row:row + 1, :], bias_h[row:row + 1, :],
                                     ALU.subtract))
                link(v.tensor_copy(bias_m[row:row + 1, :], bias32[row:row + 1, :]))
            link(v.tensor_copy(bias3[32:33, :], bias_m[32:33, :]))
            link(v.tensor_tensor(bias3[64:65, :], bias32[64:65, :], bias_m[64:65, :], ALU.subtract))
            assert made[0] == NSETV

            def mins(b, h):
                dve.wait_ge(xt, n(b, XT, f"qkv{h}"))
                if since(b, 1):
                    dve.wait_ge(xa, prev(b, XA, f"ex{h}"))
                v.tensor_scalar(mn[:, h, :], p_qkv[:, 0:2 * C], 0.0, None, ALU.min).then_inc(xv, 1)

            def feats(b, h):
                dve.wait_ge(xa, n(b, XA, f"ex{h}"))
                if since(b, 1):
                    dve.wait_ge(xp, prev(b, XP, f"kl{h}"))
                v.scalar_tensor_tensor(out=feat[:, h, :], in0=p_qkv[:, 0:2 * C], scalar=0.0, in1=ex[:, h, :],
                                       op0=ALU.max, op1=ALU.add).then_inc(xv, 1)

            for h in range(2):
                mins(0, h)
                feats(0, h)

            def slot(b, par):
                do_x, do_y, do_w, do_z = stages(b)
                o = 1 - par
                bx, bw, bz = b + 1, b - 1, b - 2

                def mask(h, r):
                    if not do_y:
                        return
                    dve.wait_ge(yt, n(b, YT, f"sc{h}{r}"))
                    if h:
                        dve.wait_ge(yp if r % 2 else yv, n(b, YP if r % 2 else YV, f"lo0{r}"))
                    elif since(b, 1):
                        dve.wait_ge(yp if r % 2 else yv, prev(b, YP if r % 2 else YV, f"lo1{r}"))
                    m = tri[:, :].rearrange("p (o t) -> p o t", o=1).to_broadcast([P, J, P])
                    v.tensor_tensor(am32[:, r, :, :], p_sc[r % 2][:, :].rearrange("p (j t) -> p j t", j=J), m,
                                    ALU.mult).then_inc(yv, 1)

                def scores_low(h, r):
                    if not do_y:
                        return
                    dve.wait_ge(ya, n(b, YA, f"hi{h}{r}"))
                    if h:
                        dve.wait_ge(yt, n(b, YT, f"ctx0{r}"))
                    elif since(b, 1):
                        dve.wait_ge(yt, prev(b, YT, f"ctx1{r}"))
                    v.tensor_tensor(am_hl[:, 1, r, :, :], am32[:, r, :, :], am_hl[:, 0, r, :, :], ALU.subtract)\
                        .then_inc(yv, 1)

                def state():
                    dve.wait_ge(yt, n(b, YT, "state"))
                    if since(b, 1):
                        dve.wait_ge(yp, prev(b, YP, "slo"))
                    v.tensor_tensor(s32[:, :, :], p_state.rearrange("p (j q) -> p j q", j=J),
                                    head_mask[:, :, :, :].rearrange("p j r e -> p j (r e)"), ALU.mult)\
                        .then_inc(yv, 1)

                def normalize():
                    c4 = p_ctx.rearrange("p h (g e) -> p (h g) e", e=DV)
                    dve.wait_ge(yt, n(b, YT, "ctx"))
                    if since(b, 1):
                        dve.wait_ge(yv, prev(b, YV, "cn"))
                    v.tensor_scalar(den[:, :], c4[:, :, DH], EPS_ATT, None, ALU.add).then_inc(yv, 1)
                    dve.wait_ge(yv, n(b, YV, "den"))
                    v.reciprocal(rec[:, :], den[:, :]).then_inc(yv, 1)
                    dve.wait_ge(yv, n(b, YV, "rec"))
                    if since(b, 1):
                        dve.wait_ge(wt, prev(b, WT, "ct"))
                    v.tensor_tensor(cn[:, :, :].rearrange("p h (g e) -> p (h g) e", e=DH), c4[:, :, 0:DH],
                                    rec[:, :].rearrange("p (g o) -> p g o", o=1).to_broadcast([P, 2 * H, DH]),
                                    ALU.mult).then_inc(yv, 1)

                def residual():
                    dve.wait_ge(wt, n(bw, WT, "proj"))
                    dve.wait_ge(x_loaded, bw * 16 + 16)
                    if since(bw, 1):
                        dve.wait_ge(wv, prev(bw, WV, "x11"))
                    v.tensor_tensor(r32[:, :, :], p_y[:, 2 * C:4 * C].rearrange("p (h c) -> p h c", h=2),
                                    x32[:, o, :, :], ALU.add).then_inc(wv, 1)

                def statistics():
                    dve.wait_ge(wv, n(bw, WV, "res"))
                    for h in range(2):
                        v.bn_stats(bn[:, h, :], r32[:, h, :]).then_inc(wv, 1)
                    dve.wait_ge(wv, n(bw, WV, "bn1"))
                    for h in range(2):
                        dve.sem_inc(passed_v, 1)
                        v.bn_aggr(mv[:, h, :], bn[:, h, :]).then_inc(wv, 1)

                def variance():
                    dve.wait_ge(wv, n(bw, WV, "ag1"))
                    if since(bw, 1):
                        dve.wait_ge(wp, prev(bw, WP, "rstd"))
                    v.tensor_scalar(ve[:, :], mv[:, :, 1], EPS_LN, None, ALU.add).then_inc(wv, 1)

                def scale():
                    dve.wait_ge(wp, n(bw, WP, "rstd"))
                    if since(bw, 2):
                        dve.wait_ge(acc_stored, bw * 16 - 16)
                        dve.wait_ge(zp, prev2(bw, ZP, "x1l"))
                        dve.wait_ge(zt, prev2(bw, ZT, "x1t"))
                    for h in range(2):
                        v.tensor_scalar(x1[:, o, h, :], r32[:, h, :], mv[:, h, 0:1], rstd[:, h:h + 1],
                                        ALU.subtract, ALU.mult).then_inc(wv, 1)

                lg = p_z[0][:, 0:2 * E].rearrange("p (h e) -> p h e", h=2)
                pos = p_z[0][:, 32:32 + 2 * E].rearrange("p (h e) -> p h e", h=2)

                def logits_max():
                    dve.wait_ge(zt, n(bz, ZT, "rt"))
                    if since(bz, 1):
                        dve.wait_ge(zv, prev(bz, ZV, "nm"))
                    for h in range(2):
                        dve.sem_inc(passed_v, 1)
                        v.max(mx[:, h, :], lg[:, h, :]).then_inc(zv, 1)
                    dve.wait_ge(zv, n(bz, ZV, "mx1"))
                    if since(bz, 1):
                        dve.wait_ge(za, prev(bz, ZA, "el1"))
                    v.tensor_scalar(nm[:, :], mx[:, :, 0], -1.0, None, ALU.mult).then_inc(zv, 1)

                def probabilities():
                    dve.wait_ge(za, n(bz, ZA, "el1"))
                    v.reciprocal(rs[:, :], es[:, :]).then_inc(zv, 1)
                    dve.wait_ge(zv, n(bz, ZV, "rs"))
                    if since(bz, 1):
                        dve.wait_ge(zp, prev(bz, ZP, "r1"))
                    v.tensor_tensor(pr[:, :, :], el[:, :, :],
                                    rs[:, :].rearrange("p (h o) -> p h o", o=1).to_broadcast([P, 2, E]),
                                    ALU.mult).then_inc(zv, 1)

                def top():
                    dve.wait_ge(zv, n(bz, ZV, "pr"))
                    for h in range(2):
                        dve.sem_inc(passed_v, 1)
                        v.max(tp[:, h, :], pr[:, h, :]).then_inc(zv, 1)
                    dve.wait_ge(zv, n(bz, ZV, "tp1"))
                    for h in range(2):
                        dve.sem_inc(passed_v, 1)
                        v.max_index(ti[:, h, :], tp[:, h, :], pr[:, h, :]).then_inc(zv, 1)

                def top_index():
                    dve.wait_ge(zv, n(bz, ZV, "ti1"))
                    v.tensor_copy(tif[:, :, :], ti[:, :, 0:K_TOP]).then_inc(zv, 1)

                def chosen():
                    dve.wait_ge(zv, n(bz, ZV, "tif"))
                    ie = iota_e[:, :].rearrange("p (o e) -> p o e", o=1).to_broadcast([P, 2, E])
                    for k, m in ((0, m0), (1, m1)):
                        v.tensor_tensor(m[:, :, :], ie, tif[:, :, k:k + 1].to_broadcast([P, 2, E]),
                                        ALU.is_equal).then_inc(zv, 1)

                def chosen_both():
                    dve.wait_ge(zv, n(bz, ZV, "m1"))
                    if since(bz, 1):
                        dve.wait_ge(zt, prev(bz, ZT, "pos"))
                    v.tensor_tensor(mb[:, :, :], m0[:, :, :], m1[:, :, :], ALU.add).then_inc(zv, 1)

                def within_capacity():
                    dve.wait_ge(zt, n(bz, ZT, "pos"))
                    v.scalar_tensor_tensor(out=val[:, :, :], in0=pos, scalar=CAP + 0.5, in1=mb[:, :, :],
                                           op0=ALU.is_le, op1=ALU.mult).then_inc(zv, 1)
                    dve.wait_ge(zv, n(bz, ZV, "val"))
                    v.tensor_tensor(dpa[:, :, :], pos, val[:, :, :], ALU.mult).then_inc(zv, 1)

                def slot_number():
                    dve.wait_ge(zv, n(bz, ZV, "dpa"))
                    v.tensor_scalar(dp[:, :, :], dpa[:, :, :], -1.0, None, ALU.add).then_inc(zv, 1)

                def one_hot(h):
                    dve.wait_ge(zv, n(bz, ZV, "dp"))
                    if since(bz, 1):
                        dve.wait_ge(zt, prev(bz, ZT, "d5"))
                    v.tensor_tensor(onehot[:, h, :, :],
                                    iota_c[:, :].rearrange("p (o c) -> p o c", o=1).to_broadcast([P, E, CAP]),
                                    dp[:, h, :].rearrange("p (e o) -> p e o", o=1).to_broadcast([P, E, CAP]),
                                    ALU.is_equal).then_inc(zv, 1)

                def slot_info(q):
                    dve.wait_ge(zt, n(bz, ZT, f"d{4 + q}"))
                    if since(bz, 1):
                        dve.wait_ge(rows_stored, bz * 16)
                    v.tensor_tensor(rows_out[:, 4 * q:4 * q + 4, :],
                                    p_z[q][0:NAUX, 0:HALF].rearrange("p (e c) -> p e c", c=CAP),
                                    aux_mask[0:NAUX, 4 * q:4 * q + 4, :], ALU.mult).then_inc(zv, 1)

                if do_y:
                    state()
                mask(0, 0)
                if do_x:
                    mins(bx, 0)
                mask(0, 1)
                if do_x:
                    feats(bx, 0)
                if do_z:
                    logits_max()
                mask(0, 2)
                if do_w:
                    residual()
                    statistics()
                if do_z:
                    probabilities()
                scores_low(0, 0)
                mask(0, 3)
                if do_w:
                    variance()
                if do_x:
                    mins(bx, 1)
                if do_z:
                    top()
                mask(1, 0)
                if do_x:
                    feats(bx, 1)
                scores_low(0, 2)
                if do_z:
                    top_index()
                if do_w:
                    scale()
                if do_z:
                    chosen()
                mask(1, 1)
                if do_z:
                    chosen_both()
                mask(1, 2)
                if do_z:
                    within_capacity()
                scores_low(1, 0)
                mask(1, 3)
                if do_z:
                    slot_number()
                    one_hot(0)
                scores_low(1, 2)
                if do_z:
                    one_hot(1)
                if do_y:
                    normalize()
                if do_z:
                    slot_info(0)
                    slot_info(1)

            slots_a(dve, slot)

            def info(e, par):
                dve.wait_ge(info_t, e + 1)
                p3 = p_y[:, 0:3 * NT].rearrange("p (t q) -> p t q", q=3)
                v.tensor_tensor(idx_a[:, :], p3[:, :, 0], slot_base[:, :], ALU.add).then_inc(info_v, 1)
                dve.wait_ge(info_v, e * 5 + 1)
                v.tensor_tensor(idx_a[:, :], idx_a[:, :], spare_row[:, :], ALU.subtract).then_inc(info_v, 1)
                dve.wait_ge(info_v, e * 5 + 2)
                v.tensor_tensor(idx_a[:, :], p3[:, :, 1], idx_a[:, :], ALU.mult).then_inc(info_v, 1)
                dve.wait_ge(info_v, e * 5 + 3)
                v.tensor_tensor(idx[:, par, :], idx_a[:, :], spare_row[:, :], ALU.add).then_inc(info_v, 1)
                v.tensor_copy(prob[:, par, :], p3[:, :, 2]).then_inc(info_v, 1)

            def gate_chunk(nb, cpar, first, early):
                for k in range(FK):
                    rows = P if k < 3 else FT
                    dve.wait_ge(silu_a, nb * FK + (k + 1))
                    if not first:
                        dve.wait_ge(gl_v, nb * FK + (k + 1 - FK))
                    h3 = bank[2 * (k % 2) + 1][:, :] if k < 3 else bank[2][0:FT, :]
                    v.tensor_tensor(g32[0:rows, k, :], sil[0:rows, k % 2, :], h3, ALU.mult).then_inc(gate_v, 1)
                    if k:
                        low_part(nb, k - 1, cpar, early)

            def low_part(nb, k, cpar, early):
                rows = P if k < 3 else FT
                dve.wait_ge(gh_a, nb * FK + (k + 1))
                if k == 0 and not early:
                    dve.wait_ge(down_t, nb - 1)
                v.tensor_tensor(gl[0:rows, cpar, k, :], g32[0:rows, k, :], gh[0:rows, cpar, k, :],
                                ALU.subtract).then_inc(gl_v, 1)

            def scale_rows(nb, e, c, par, cpar, nadds):
                dve.wait_ge(down_t, nb + 1)
                if nadds is not None:
                    dve.wait_ge(added[cpar], nadds)
                dve.wait_ge(info_v, e * 5 + 5)
                v.tensor_tensor(eo[:, cpar, :, :], bank[4 + cpar][:, :].rearrange("p (s m) -> p s m", s=SUB),
                                prob[:, par, c * SUB:(c + 1) * SUB].rearrange("p (s o) -> p s o", o=1)
                                .to_broadcast([P, SUB, C]), ALU.mult).then_inc(eo_v, 1)

            def experts(i, first):
                for q in range(2 * NCH):
                    par, c, cpar = q // NCH, q % NCH, q % 2
                    nb = i * (2 * NCH) + q
                    gate_chunk(nb, cpar, first and q == 0, first and q < 2)
                    if c == 0:
                        if first and par == 0:
                            dve.wait_ge(setup_p, 2)
                        if not first:
                            back = (0, 0) if par else (NCH // 2, NCH // 2 + 1)
                            dve.wait_ge(added[0], (i * NCH - back[0]) * SUB * 16)
                            dve.wait_ge(added[1], (i * NCH - back[1]) * SUB * 16)
                        info(i * 2 + par, par)
                    if q or not first:
                        pq = (q - 1) % (2 * NCH)
                        cnt = None if first and pq < 2 else (i * NCH + (q - 1) // 2) * SUB * 16
                        scale_rows(nb - 1, i * 2 + (q - 1) // NCH, pq % NCH, pq // NCH, pq % 2, cnt)
                    low_part(nb, FK - 1, cpar, first and q < 2)

            experts(0, True)
            with dve.Fori(1, E // 2) as i:
                experts(i, False)
            scale_rows(E * NCH - 1, E - 1, NCH - 1, 1, 1, (E // 2 * NCH - 1) * SUB * 16)

            def chunk_c(k, par, i, first):
                dve.wait_ge(c_loaded[par], i * 16 + 16)
                for r in range(ROWS_C):
                    ins = v.bn_stats(cst[:, par, r, :], cx[:, par, r * C:(r + 1) * C])
                ins.then_inc(c_v, 1)
                dve.wait_ge(c_v, k * 5 + 1)
                for r in range(ROWS_C):
                    dve.sem_inc(passed_v, 1)
                    ins = v.bn_aggr(cmv[:, par, r, :], cst[:, par, r, :])
                ins.then_inc(c_v, 1)
                dve.wait_ge(c_v, k * 5 + 2)
                v.tensor_scalar(cve[:, par, :], cmv[:, par, :, 1], EPS_LN, None, ALU.add).then_inc(c_v, 1)
                dve.wait_ge(c_p, k + 1)
                if not first:
                    dve.wait_ge(c_stored[par], i * 16)
                for r in range(ROWS_C):
                    ins = v.tensor_scalar(cx[:, par, (ROWS_C + r) * C:(ROWS_C + r + 1) * C],
                                          cx[:, par, r * C:(r + 1) * C], cmv[:, par, r, 0:1],
                                          crs[:, par, r:r + 1], ALU.subtract, ALU.mult)
                    if r == ROWS_C // 2 - 1:
                        ins.then_inc(c_v, 1)
                ins.then_inc(c_v, 1)

            chunk_c(0, 0, 0, True)
            chunk_c(1, 1, 0, True)
            with dve.Fori(1, NC_CH // 2) as i:
                chunk_c(i * 2, 0, i, False)
                chunk_c(i * 2 + 1, 1, i, False)

        @block.scalar
        def _(act):
            a = nc.scalar

            def x_high(b):
                act.wait_ge(xt_loaded, b * 16 + 16)
                if since(b, 1):
                    act.wait_ge(xt, prev(b, XT, "qkv1"))
                    act.wait_ge(xp, prev(b, XP, "xlo"))
                a.activation(xh[:, :], xT32[:, :], ACT.Copy).then_inc(xa, 1)

            def exps(b, h):
                act.wait_ge(xv, n(b, XV, f"mn{h}"))
                if since(b, 1):
                    act.wait_ge(xv, prev(b, XV, f"f{h}"))
                a.activation(ex[:, h, :], mn[:, h, :], ACT.Exp).then_inc(xa, 1)

            def values(b, h, par):
                act.wait_ge(xv, n(b, XV, f"f{h}"))
                if since(b, 2):
                    act.wait_ge(xp, prev2(b, XP, f"vl{h}"))
                a.activation(v32[:, par, h, :, 0:DH],
                             p_qkv[:, 2 * C:3 * C].rearrange("p (h e) -> p h e", e=DH), ACT.Copy).then_inc(xa, 1)

            def stack_high(b, h, par):
                q2 = feat[:, h, 0:C].rearrange("p (c o) -> p c o", o=1).to_broadcast([P, C, 2])
                k2 = feat[:, h, C:2 * C].rearrange("p (c o) -> p c o", o=1).to_broadcast([P, C, 2])
                if since(b, 2):
                    act.wait_ge(xt, prev2(b, XT, f"tr{h}"))
                    act.wait_ge(yt, prev2(b, YT, "state"))
                a.activation(stack[:, par, h, 0, :, :, 0], q2, ACT.Copy).then_inc(xa, 1)
                a.activation(stack[:, par, h, 1, :, 0, :], k2, ACT.Copy).then_inc(xa, 1)

            def v_high(b, h, par):
                act.wait_ge(xa, n(b, XA, f"v{h}"))
                if since(b, 2):
                    act.wait_ge(yt, prev2(b, YT, "ctx"))
                a.activation(vh[:, par, h, :, :], v32[:, par, h, :, :], ACT.Copy).then_inc(xa, 1)

            def evac_t(b, h, par):
                act.wait_ge(xt, n(b, XT, f"tr{h}"))
                if since(b, 2):
                    act.wait_ge(yt, prev2(b, YT, "ctx"))
                a.activation(qkT[:, par, h, :, :, :].rearrange("p q j t -> p (q j) t"), p_tr, ACT.Copy)\
                    .then_inc(xa, 1)

            act.wait_ge(setup_p, 1)
            x_high(0)
            exps(0, 0)
            values(0, 0, 0)
            stack_high(0, 0, 0)
            v_high(0, 0, 0)
            exps(0, 1)
            values(0, 1, 0)
            evac_t(0, 0, 0)
            stack_high(0, 1, 0)
            v_high(0, 1, 0)
            evac_t(0, 1, 0)

            def slot(b, par):
                do_x, do_y, do_w, do_z = stages(b)
                o = 1 - par
                bx, bw, bz = b + 1, b - 1, b - 2

                if do_x:
                    x_high(bx)
                if do_z:
                    act.wait_ge(wv, n(bz, WV, "x11"))
                    if since(bz, 1):
                        act.wait_ge(zt, prev(bz, ZT, "d1"))
                        act.wait_ge(zp, prev(bz, ZP, "x1l"))
                    a.activation(x1h[:, :, :], x1[:, par, :, :], ACT.Copy).then_inc(za, 1)
                    act.wait_ge(zt, n(bz, ZT, "x1t"))
                    if since(bz, 1):
                        act.wait_ge(zt, prev(bz, ZT, "rt"))
                    a.activation(x1T[:, :, :].rearrange("p h t -> p (h t)"), p_z[0][:, 0:2 * P], ACT.Copy)\
                        .then_inc(za, 1)
                if do_w:
                    act.wait_ge(wt, n(bw, WT, "ct"))
                    if since(bw, 1):
                        act.wait_ge(wt, prev(bw, WT, "proj"))
                    a.activation(cT[:, :, :].rearrange("p h t -> p (h t)"), p_y[:, 0:2 * P], ACT.Copy)\
                        .then_inc(wa, 1)
                if do_y:
                    act.wait_ge(yv, n(b, YV, "s32"))
                    if since(b, 1):
                        act.wait_ge(yt, prev(b, YT, "ctx"))
                    a.activation(sh[:, :, :], s32[:, :, :], ACT.Copy).then_inc(ya, 1)
                def scores_high(h, r):
                    if not do_y:
                        return
                    act.wait_ge(yv, n(b, YV, f"am{h}{r}"))
                    if h:
                        act.wait_ge(yt, n(b, YT, f"ctx0{r}"))
                    elif since(b, 1):
                        act.wait_ge(yt, prev(b, YT, f"ctx1{r}"))
                    a.activation(am_hl[:, 0, r, :, :], am32[:, r, :, :], ACT.Copy).then_inc(ya, 1)

                scores_high(0, 0)
                if do_x:
                    exps(bx, 0)
                scores_high(0, 1)
                if do_x:
                    values(bx, 0, o)
                    stack_high(bx, 0, o)
                if do_z:
                    act.wait_ge(zv, n(bz, ZV, "nm"))
                    if since(bz, 1):
                        act.wait_ge(zv, prev(bz, ZV, "pr"))
                    for h in range(2):
                        a.activation(el[:, h, :], p_z[0][:, h * E:(h + 1) * E], ACT.Exp, bias=nm[:, h:h + 1],
                                     accum_out=es[:, h:h + 1]).then_inc(za, 1)
                scores_high(0, 2)
                if do_x:
                    v_high(bx, 0, o)
                scores_high(0, 3)
                if do_x:
                    exps(bx, 1)
                scores_high(1, 0)
                if do_x:
                    values(bx, 1, o)
                    evac_t(bx, 0, o)
                scores_high(1, 1)
                if do_x:
                    stack_high(bx, 1, o)
                    v_high(bx, 1, o)
                scores_high(1, 2)
                scores_high(1, 3)
                if do_x:
                    evac_t(bx, 1, o)
                if do_z:
                    for part, xd in ((0, xdh), (1, xdl)):
                        for q in range(2):
                            act.wait_ge(zt, n(bz, ZT, f"d{2 * part + q}"))
                            a.activation(xd[:, 4 * q:4 * q + 4, bass.ds(bz * CAP, CAP)],
                                         p_z[q][:, 0:HALF].rearrange("p (e c) -> p e c", c=CAP), ACT.Copy)\
                                .then_inc(za, 1)

            slots_a(act, slot)

            def chunk(nb, cpar, first):
                def high(k):
                    rows = P if k < 3 else FT
                    act.wait_ge(gate_v, nb * FK + (k + 1))
                    a.activation(gh[0:rows, cpar, k, :], g32[0:rows, k, :], ACT.Copy).then_inc(gh_a, 1)

                for k in range(FK):
                    rows = P if k < 3 else FT
                    act.wait_ge(up_t, nb * FK + (k + 1))
                    if not (first and k < 2):
                        act.wait_ge(gate_v, nb * FK + (k - 1))
                    h1 = bank[2 * (k % 2)][:, :] if k < 3 else bank[2][FT:P, :]
                    a.activation(sil[0:rows, k % 2, :], h1, ACT.Silu).then_inc(silu_a, 1)
                    if k == 0 and not (isinstance(nb, int) and nb < 2):
                        act.wait_ge(down_t, nb - 1)
                    if k > 0:
                        high(k - 1)
                high(FK - 1)

            for nb in range(2 * NCH):
                chunk(nb, nb % 2, nb == 0)
            with act.Fori(1, E // 2) as i:
                for q in range(2 * NCH):
                    chunk(i * (2 * NCH) + q, q % 2, False)

        @block.tensor
        def _(pe):
            t = nc.tensor

            def qkv(b, h):
                if h == 0:
                    pe.wait_ge(xp, n(b, XP, "xlo"))
                    pe.wait_ge(xa, n(b, XA, "xhi"))
                if h:
                    pe.wait_ge(xv, n(b, XV, "f0"))
                    pe.wait_ge(xa, n(b, XA, "v0"))
                elif since(b, 1):
                    pe.wait_ge(xv, prev(b, XV, "f1"))
                    pe.wait_ge(xa, prev(b, XA, "v1"))
                sl_ = slice(h * P, (h + 1) * P)
                o_ = p_qkv[:, 0:3 * C]
                t.matmul(o_, xh[:, sl_], wqh[:, :], start=True, stop=False)
                t.matmul(o_, xh[:, sl_], wql[:, :], start=False, stop=False)
                t.matmul(o_, xl[:, sl_], wqh[:, :], start=False, stop=False)
                t.matmul(o_, onesb[0:96, :], bias3[:, 0:3 * C], start=False, stop=True).then_inc(xt, 1)

            def transposes(b, h, par):
                pe.wait_ge(xa, n(b, XA, f"kh{h}"))
                pe.wait_ge(xp, n(b, XP, f"kl{h}"))
                if h or since(b, 1):
                    pe.wait_ge(xa, n(b, XA, "T0") if h else prev(b, XA, "T1"))
                for qk in range(2):
                    for j in range(J):
                        src = stack[:, par, h, qk, 32 * j:32 * j + 32, :, :].rearrange("p c a d -> p (c a d)")
                        ins = t.transpose(p_tr[:, qk * J + j, :], src, identb[:, :])
                ins.then_inc(xt, 1)

            pe.wait_ge(setup_p, 1)
            pe.wait_ge(setup_v, NSETV)
            qkv(0, 0)
            qkv(0, 1)
            transposes(0, 0, 0)
            transposes(0, 1, 0)

            def slot(b, par):
                do_x, do_y, do_w, do_z = stages(b)
                o = 1 - par
                bx, bw, bz = b + 1, b - 1, b - 2

                def x1_t():
                    pe.wait_ge(wv, n(bz, WV, "x11"))
                    if since(bz, 1):
                        pe.wait_ge(zv, prev(bz, ZV, "ax0"))
                    for h in range(2):
                        ins = t.transpose(p_z[0][:, h * P:(h + 1) * P], x1[:, par, h, :], ident[:, :])
                    ins.then_inc(zt, 1)

                def router():
                    pe.wait_ge(za, n(bz, ZA, "x1T"))
                    for h in range(2):
                        ins = t.matmul(p_z[0][:, h * E:(h + 1) * E], x1T[:, h, :], gt32[:, :],
                                       start=True, stop=True)
                    ins.then_inc(zt, 1)

                def positions():
                    pe.wait_ge(zv, n(bz, ZV, "M"))
                    po = p_z[0][:, 32:32 + 2 * E]
                    t.matmul(po[:, 0:E], trib[:, :], mb[:, 0, :], start=True, stop=True)
                    t.matmul(po[:, E:2 * E], onesb[:, :], mb[:, 0, :], start=True, stop=False)
                    t.matmul(po[:, E:2 * E], trib[:, :], mb[:, 1, :], start=False, stop=True).then_inc(zt, 1)

                def ctx_t():
                    pe.wait_ge(yv, n(bw, YV, "cn"))
                    if since(bw, 1):
                        pe.wait_ge(wv, prev(bw, WV, "res"))
                        pe.wait_ge(wa, prev(bw, WA, "cT"))
                    for h in range(2):
                        ins = t.transpose(p_y[:, h * P:(h + 1) * P], cn[:, h, :], ident[:, :])
                    ins.then_inc(wt, 1)

                def proj():
                    pe.wait_ge(wa, n(bw, WA, "cT"))
                    for h in range(2):
                        o_ = p_y[:, (2 + h) * C:(3 + h) * C]
                        t.matmul(o_, cT[:, h, :], wo32[:, :], start=True, stop=False)
                        ins = t.matmul(o_, onesb[0:96, :], bias3[:, 3 * C:4 * C], start=False, stop=True)
                    ins.then_inc(wt, 1)

                def state():
                    pe.wait_ge(xa, n(b, XA, "vh0"))
                    pe.wait_ge(xp, n(b, XP, "vl0"))
                    if since(b, 1):
                        pe.wait_ge(yv, prev(b, YV, "cn"))
                    for j in range(J):
                        for part, vv in ((0, vh), (1, vl)):
                            ins = t.matmul(
                                p_state[:, j * R * DV:(j + 1) * R * DV],
                                stack[:, par, 0, 1, 32 * j:32 * j + 32, :, :].rearrange("p c a d -> p (c a d)"),
                                vv[:, par, 0, j * R:(j + 1) * R, :].rearrange("p r e -> p (r e)"),
                                start=(part == 0), stop=(part == 1))
                    ins.then_inc(yt, 1)

                def scores(h, r):
                    if r == 0:
                        pe.wait_ge(xa, n(b, XA, f"T{h}"))
                    if h or r > 1:
                        pe.wait_ge(yv, n(b, YV, f"am{h}{r - 2}" if r > 1 else f"am0{r + 2}"))
                    elif since(b, 1):
                        pe.wait_ge(yv, prev(b, YV, f"am1{r + 2}"))
                    for j in range(J):
                        ins = t.matmul(p_sc[r % 2][:, j * P:(j + 1) * P], qkT[32 * r:32 * r + 32, par, h, 1, j, :],
                                       qkT[32 * r:32 * r + 32, par, h, 0, j, :], start=True, stop=True)
                    ins.then_inc(yt, 1)

                def context(h, r):
                    pe.wait_ge(ya, n(b, YA, f"hi{h}{r}"))
                    if r % 2:
                        pe.wait_ge(yp, n(b, YP, f"lo{h}{r}"))
                    else:
                        pe.wait_ge(yv, n(b, YV, f"lo{h}{r}"))
                    if r == 0:
                        pe.wait_ge(xa, n(b, XA, f"vh{h}"))
                        pe.wait_ge(xp, n(b, XP, f"vl{h}"))
                    for j in range(J):
                        hd = j * R + r
                        o_ = p_ctx[:, h, hd * DV:(hd + 1) * DV]
                        first = h == 0 and r == 0 and j == 0
                        hi, lo = am_hl[:, 0, r, j, :], am_hl[:, 1, r, j, :]
                        t.matmul(o_, hi, vh[:, par, h, hd, :], start=first, stop=False, skip_group_check=True)
                        t.matmul(o_, hi, vl[:, par, h, hd, :], start=False, stop=False, skip_group_check=True)
                        ins = t.matmul(o_, lo, vh[:, par, h, hd, :], start=False, stop=(h == 0),
                                       skip_group_check=True)
                    ins.then_inc(yt, 1)

                def context_state():
                    pe.wait_ge(ya, n(b, YA, "shi"))
                    pe.wait_ge(yp, n(b, YP, "slo"))
                    for part, s in ((0, sh), (1, sl)):
                        for j in range(J):
                            ins = t.matmul(p_ctx[:, 1, j * R * DV:(j + 1) * R * DV], qkT[:, par, 1, 0, j, :],
                                           s[:, j, :], start=False, stop=(part == 1), skip_group_check=True)
                    ins.then_inc(yt, 1)

                def dispatch(i):
                    part, q = i // 2, i % 2
                    if i == 0:
                        pe.wait_ge(zv, n(bz, ZV, "D1"))
                        pe.wait_ge(zp, n(bz, ZP, "x1l"))
                    if i == 1 and since(bz, 1):
                        pe.wait_ge(zv, prev(bz, ZV, "ax1"))
                    if part:
                        pe.wait_ge(za, n(bz, ZA, f"xh{q}" if part == 1 else f"xl{q}"))
                    if part == 2:
                        pe.wait_ge(zp, n(bz, ZP, "pl"))
                    m = C if part < 2 else NAUX
                    src = (x1h, x1l, aux)[part]
                    for h in range(2):
                        ins = t.matmul(p_z[q][0:m, 0:HALF], src[:, h, :],
                                       onehot[:, h, 4 * q:4 * q + 4, :].rearrange("p e c -> p (e c)"),
                                       start=(h == 0), stop=(h == 1))
                    ins.then_inc(zt, 1)

                if do_z:
                    x1_t()
                if do_w:
                    ctx_t()
                if do_y:
                    state()
                    scores(0, 0)
                    scores(0, 1)
                if do_x:
                    qkv(bx, 0)
                if do_z:
                    router()
                if do_w:
                    proj()
                if do_y:
                    scores(0, 2)
                    scores(0, 3)
                if do_x:
                    qkv(bx, 1)
                if do_y:
                    context(0, 0)
                    scores(1, 0)
                    context(0, 1)
                    scores(1, 1)
                if do_x:
                    transposes(bx, 0, o)
                if do_y:
                    context(0, 2)
                    scores(1, 2)
                    context(0, 3)
                    scores(1, 3)
                if do_z:
                    positions()
                if do_y:
                    context(1, 0)
                    context(1, 1)
                if do_x:
                    transposes(bx, 1, o)
                if do_y:
                    context(1, 2)
                    context(1, 3)
                    context_state()
                if do_z:
                    for i in range(6):
                        dispatch(i)

            slots_a(pe, slot)

            pe.wait_ge(za, n(B - 1, ZA, "xl1"))
            pe.wait_ge(zv, n(B - 1, ZV, "ax1"))
            pe.wait_ge(wv, n(B - 1, WV, "x11"))

            def info(e, par, first):
                pe.wait_ge(rows_loaded, e * 16 + 16)
                if not first:
                    pe.wait_ge(info_v, e * 5)
                for s in range(NT):
                    ins = t.matmul(p_y[:, 3 * s:3 * s + 3], rows_in[:, par, s * P:(s + 1) * P], sel[0:NAUX, :],
                                   start=True, stop=True)
                ins.then_inc(info_t, 1)

            def up(e, nb, par, c, first):
                for k in range(FK):
                    pair = ((2 * (k % 2), k * P), (2 * (k % 2) + 1, (3 + k) * P)) if k < 3 else ((2, 6 * P),)
                    if not (first and k < 2):
                        pe.wait_ge(gate_v, nb * FK + (k - 1))
                    for bk, w0 in pair:
                        o_ = bank[bk][:, :]
                        xs = bass.ds(c * CH, CH)
                        rh = xdh[:, bass.ds(e, 1), xs].rearrange("p o s -> p (o s)")
                        rl = xdl[:, bass.ds(e, 1), xs].rearrange("p o s -> p (o s)")
                        t.matmul(o_, wh[:, par, w0:w0 + P], rh, start=True, stop=False)
                        t.matmul(o_, wh[:, par, w0:w0 + P], rl, start=False, stop=False)
                        ins = t.matmul(o_, wl[:, par, w0:w0 + P], rh, start=False, stop=True)
                    ins.then_inc(up_t, 1)

            def down(nb, par, cpar, first):
                pe.wait_ge(gl_v, nb * FK + FK)
                if not first:
                    pe.wait_ge(eo_v, nb - 1)
                for s in range(SUB):
                    o_ = bank[4 + cpar][:, s * C:(s + 1) * C]
                    ss = slice(s * P, (s + 1) * P)
                    for k in range(FK):
                        rows = P if k < 3 else FT
                        w = slice(2 * F + k * C, 2 * F + (k + 1) * C)
                        t.matmul(o_, gh[0:rows, cpar, k, ss], wh[0:rows, par, w], start=(k == 0), stop=False)
                        t.matmul(o_, gh[0:rows, cpar, k, ss], wl[0:rows, par, w], start=False, stop=False)
                        ins = t.matmul(o_, gl[0:rows, cpar, k, ss], wh[0:rows, par, w], start=False,
                                       stop=(k == FK - 1))
                ins.then_inc(down_t, 1)

            def experts(i, first):
                for q in range(2 * NCH):
                    par, c, cpar = q // NCH, q % NCH, q % 2
                    nb = i * (2 * NCH) + q
                    if c == 0:
                        pe.wait_ge(w_split_l, i * 2 + par + 1)
                    up(i * 2 + par, nb, par, c, first and q == 0)
                    if c == 0:
                        info(i * 2 + par, par, first and par == 0)
                    if q or not first:
                        pq = (q - 1) % (2 * NCH)
                        down(nb - 1, pq // NCH, pq % 2, first and pq < 2)

            experts(0, True)
            with pe.Fori(1, E // 2) as i:
                experts(i, False)
            down(E * NCH - 1, 1, 1, False)



def kernel(**inputs):
    import numpy as np

    import concourse.bacc as bacc
    from concourse import mybir
    from concourse.bass_utils import run_bass_kernel_spmd

    fp32 = mybir.dt.float32
    x = np.asarray(inputs["L0_attn_x"])
    nb, t, c = x.shape
    x2 = np.ascontiguousarray(x.reshape(nb * t, c))
    arrays = {
        "x": x2,
        "x_t": np.ascontiguousarray(x2.T),
        "wqkv_t": np.ascontiguousarray(np.asarray(inputs["L0_attn_w_qkv"]).T),
        "bqkv": np.ascontiguousarray(np.asarray(inputs["L0_attn_b_qkv"]).reshape(1, -1)),
        "wout_t": np.ascontiguousarray(np.asarray(inputs["L0_attn_w_out"]).T),
        "bout": np.ascontiguousarray(np.asarray(inputs["L0_attn_b_out"]).reshape(1, -1)),
        "gate_t": np.ascontiguousarray(np.asarray(inputs["L0_ffn_gate_w"]).T),
        "w1": np.ascontiguousarray(np.asarray(inputs["L0_ffn_w1"])),
        "w2": np.ascontiguousarray(np.asarray(inputs["L0_ffn_w2"])),
        "w3": np.ascontiguousarray(np.asarray(inputs["L0_ffn_w3"])),
    }
    nc = bacc.Bacc("TRN2", target_bir_lowering=False, num_devices=1)
    aps = [nc.dram_tensor(k, a.shape, fp32, kind="ExternalInput").ap() for k, a in arrays.items()]
    e = arrays["w1"].shape[0]
    cap = int(t * 2 / e * 1.25)
    acc = nc.dram_tensor("acc", (nb * t + nb * cap, c), fp32, kind="Internal").ap()
    slot_rows = nc.dram_tensor("slot_rows", (e, 3 * e + 2, nb * cap), mybir.dt.bfloat16, kind="Internal").ap()
    out = nc.dram_tensor("out", (nb * t, c), fp32, kind="ExternalOutput").ap()
    build(nc, *aps, acc, slot_rows, out)
    r = run_bass_kernel_spmd(nc, [arrays], core_ids=[0])
    return np.asarray(r.results[0]["out"]).reshape(nb, t, c)
```

```python
def build(nc, x, xt_in, wqkv, bqkv, wout, bout, gate, w1, w2, w3, acc, slot_rows, out):
    from contextlib import ExitStack

    import concourse.bass as bass
    from concourse import mybir

    fp32 = mybir.dt.float32
    bf16 = mybir.dt.bfloat16
    u32 = mybir.dt.uint32
    ACT = mybir.ActivationFunctionType
    ALU = mybir.AluOpType

    TOK, C = x.shape
    P = 128
    T = 256
    B = TOK // T
    H = 16
    DH = C // H
    DV = DH + 1
    J = 4
    R = H // J
    E, _, F = w1.shape
    K_TOP = 2
    CAP = int(T * K_TOP / E * 1.25)
    SLOTS = B * CAP
    FK = 4
    FT = F - 3 * P
    CH = 512
    NCH = SLOTS // CH
    SUB = CH // P
    NT = SLOTS // P
    NAUX = 3 * E + 2
    HALF = E // 2 * CAP
    EPS_ATT = 1e-6
    EPS_LN = 1e-5
    ROWS_C = 8
    NC_CH = TOK // (P * ROWS_C)

    XT = ["qkv0", "qkv1", "tr0", "tr1"]
    XA = ["xhi", "ex0", "qh0", "kh0", "v0", "ex1", "qh1", "kh1", "vh0", "T0", "v1", "vh1", "T1"]
    XV = ["f0", "f1"]
    XP = ["xlo", "ql0", "kl0", "ql1", "kl1", "vl0", "vl1"]
    YT = ["sc00", "sc01", "sc02", "sc03", "state", "sc10", "ctx00", "sc11", "ctx01", "sc12", "sc13",
          "ctx03", "ctx02", "ctx10", "ctx11", "ctx13", "ctx12", "ctx"]
    YA = ["hi00", "hi01", "hi03", "shi", "hi02", "hi10", "hi11", "hi13", "hi12"]
    YV = ["am00", "am01", "am02", "am03", "lo00", "s32", "am10", "am11", "lo10", "am13", "am12", "den",
          "rec", "cn"]
    YP = ["lo01", "lo03", "slo", "lo02", "lo11", "lo13", "lo12"]
    WT = ["ct", "proj"]
    WA = ["cT", "x10", "x11"]
    WV = ["res", "bn0", "bn1", "ag0", "ag1", "nmean", "ve"]
    WP = ["rstd", "nmr"]
    ZT = ["x1t", "rt", "pos"]
    ZA = ["x1T", "el0", "el1", "x1h"]
    ZV = ["mx0", "mx1", "nm", "rs", "pr", "tp0", "tp1", "ti0", "ti1", "tif", "m0", "m1", "M", "val", "dpa",
          "dp", "D0", "D1"]
    ZP = ["ph", "r1", "pm", "pl", "x1l"]
    DT = ["i0", "i1", "h0", "h1", "l0", "l1"]
    DA = ["h0", "h1", "l0", "l1"]
    DI = ["i0", "i1"]

    def n(b, steps, step):
        return b * len(steps) + (steps.index(step) + 1)

    def prev(b, steps, step):
        return b * len(steps) + (steps.index(step) + 1 - len(steps))

    def prev2(b, steps, step):
        return b * len(steps) + (steps.index(step) + 1 - 2 * len(steps))

    ctx = ExitStack()
    with ctx:
        def sb(name, shape, dt=fp32):
            return ctx.enter_context(nc.sbuf_tensor(name, shape, dt))

        def sem(name):
            return ctx.enter_context(nc.semaphore(name))

        ident = sb("ident", [P, P])
        identb = sb("identb", [P, P], bf16)
        tri = sb("tri", [P, P])
        trib = sb("trib", [P, P], bf16)
        onesb = sb("onesb", [P, P], bf16)
        head_mask = sb("head_mask", [P, J, R, DV])
        iota_c = sb("iota_c", [P, CAP], bf16)
        iota_e = sb("iota_e", [P, E])
        aux_mask = sb("aux_mask", [32, E, CAP])
        sel = sb("sel", [32, 3], bf16)
        minus_one = sb("minus_one", [P, 1])
        half_pow = sb("half_pow", [P, ROWS_C])
        slot_base = sb("slot_base", [P, NT])
        spare_row = sb("spare_row", [P, NT])
        zrow = sb("zrow", [P, C])
        wq32 = sb("wq32", [P, 3 * C])
        wqh = sb("wqh", [P, 3 * C], bf16)
        wql = sb("wql", [P, 3 * C], bf16)
        wo32 = sb("wo32", [P, C])
        gt32 = sb("gt32", [P, E])
        bias32 = sb("bias32", [1, 4 * C])
        bias_m = sb("bias_m", [1, 4 * C], bf16)
        bias3 = sb("bias3", [P, 4 * C], bf16)
        xT32 = sb("xT32", [P, T])
        x32 = sb("x32", [P, 2, 2, C])
        xh = sb("xh", [P, T], bf16)
        xl = sb("xl", [P, T], bf16)
        ex = sb("ex", [P, 2, 2 * C])
        feat = sb("feat", [P, 2, 2 * C])
        stack = sb("stack", [P, 2, 2, 2, C, 2, 2], bf16)
        qkT = sb("qkT", [P, 2, 2, 2, J, P], bf16)
        v32 = sb("v32", [P, 2, 2, H, DV])
        vh = sb("vh", [P, 2, 2, H, DV], bf16)
        vl = sb("vl", [P, 2, 2, H, DV], bf16)
        s32 = sb("s32", [P, J, R * DV])
        sh = sb("sh", [P, J, R * DV], bf16)
        sl = sb("sl", [P, J, R * DV], bf16)
        am = sb("am", [P, 2, R, J, P])
        den = sb("den", [P, 2 * H])
        rec = sb("rec", [P, 2 * H])
        cn = sb("cn", [P, 2, C])
        cT = sb("cT", [P, 2, P])
        r32 = sb("r32", [P, 2, C])
        bn = sb("bn", [P, 2, 6])
        mv = sb("mv", [P, 2, 2])
        ve = sb("ve", [P, 2])
        rstd = sb("rstd", [P, 2])
        nmean = sb("nmean", [P, 2])
        nmr = sb("nmr", [P, 2])
        x1 = sb("x1", [P, 2, 2, C])
        x1h = sb("x1h", [P, 2, 2, C], bf16)
        x1l = sb("x1l", [P, 2, 2, C], bf16)
        x1T = sb("x1T", [P, 2, P])
        mx = sb("mx", [P, 2, 8])
        nm = sb("nm", [P, 2])
        el = sb("el", [P, 2, E])
        es = sb("es", [P, 2])
        rs = sb("rs", [P, 2])
        pr = sb("pr", [P, 2, E])
        tp = sb("tp", [P, 2, 8])
        ti = sb("ti", [P, 2, 8], u32)
        tif = sb("tif", [P, 2, K_TOP])
        m0 = sb("m0", [P, 2, E])
        m1 = sb("m1", [P, 2, E])
        mb = sb("mb", [P, 2, E], bf16)
        val = sb("val", [P, 2, E])
        dpa = sb("dpa", [P, 2, E])
        dp = sb("dp", [P, 2, E], bf16)
        onehot = sb("onehot", [P, 2, E, CAP], bf16)
        aux = sb("aux", [P, 2, 2, NAUX], bf16)
        pres = sb("pres", [P, 2, E])
        rows_out = sb("rows_out", [NAUX, E, CAP], bf16)
        xdh = sb("xdh", [P, E, SLOTS], bf16)
        xdl = sb("xdl", [P, E, SLOTS], bf16)
        wst = sb("wst", [P, 2 * F + FK * C])
        wh = sb("wh", [P, 2, 2 * F + FK * C], bf16)
        wl = sb("wl", [P, 2, 2 * F + FK * C], bf16)
        rows_in = sb("rows_in", [NAUX, 2, SLOTS], bf16)
        idx_a = sb("idx_a", [P, NT])
        idx = sb("idx", [P, 2, NT], u32)
        prob = sb("prob", [P, 2, NT])
        sil = sb("sil", [P, 2, CH])
        gh = sb("gh", [P, 2, FK, CH], bf16)
        am32 = am[:, 0, :, :, :]
        am_hl = am[:, 1, :, :, :].rearrange("p r j t -> p (r j t)").bitcast(bf16)\
            .rearrange("p (q r j t) -> p q r j t", q=2, r=R, j=J)
        g32 = am[:, 0, :, :, :].rearrange("p r j t -> p r (j t)")
        gl = am[:, 1, :, :, :].rearrange("p r j t -> p (r j t)").bitcast(bf16)\
            .rearrange("p (q k s) -> p q k s", q=2, k=FK)
        eo = sb("eo", [P, 2, SUB, C])
        cx = xdh[:, :, :].rearrange("p e s -> p (e s)").bitcast(fp32)
        cst = sb("cst", [P, 2, ROWS_C, 6])
        cmv = sb("cmv", [P, 2, ROWS_C, 2])
        cve = sb("cve", [P, 2, ROWS_C])
        crs = sb("crs", [P, 2, ROWS_C])
        cnm = sb("cnm", [P, 2, ROWS_C])
        cnmr = sb("cnmr", [P, 2, ROWS_C])

        bank = [ctx.enter_context(nc.psum_tensor(f"bank{i}", [P, 512], fp32)) for i in range(8)]
        p_qkv = bank[0]
        p_tr = bank[2][:, :].bitcast(bf16).rearrange("p (s t) -> p s t", s=8)
        p_sc = [bank[3], bank[4]]
        p_ctx = bank[5][:, 0:2 * H * DV].rearrange("p (h q) -> p h q", h=2)
        p_state = bank[5][:, 2 * H * DV:3 * H * DV]
        p_y = bank[6]
        p_z = bank[7]
        p_d = bank[1]

        UP = ((bank[0], bank[1]), (bank[2], bank[3]), (bank[6], bank[7]), (bank[0],))
        DOWN = (bank[4], bank[5])
        p_info = bank[2]

        const_ready = sem("const_ready")
        wa_loaded = sem("wa_loaded")
        setup_v = sem("setup_v")
        setup_p = sem("setup_p")
        passed_v = sem("passed_v")
        passed_p = sem("passed_p")
        passed_s = sem("passed_s")
        xt_loaded = sem("xt_loaded")
        x_loaded = sem("x_loaded")
        xt, xa, xv, xp = (sem(s) for s in ("xt", "xa", "xv", "xp"))
        yt, ya, yv, yp = (sem(s) for s in ("yt", "ya", "yv", "yp"))
        wt, wa, wv, wp = (sem(s) for s in ("wt", "wa", "wv", "wp"))
        zt, za, zv, zp = (sem(s) for s in ("zt", "za", "zv", "zp"))
        dt, da, dv = (sem(s) for s in ("dt", "da", "dv"))
        acc_stored = sem("acc_stored")
        spare_stored = sem("spare_stored")
        rows_stored = sem("rows_stored")
        w_loaded = sem("w_loaded")
        rows_loaded = sem("rows_loaded")
        w_split_h = sem("w_split_h")
        w_split_l = sem("w_split_l")
        info_t = sem("info_t")
        info_v = sem("info_v")
        up_t = sem("up_t")
        silu_a = sem("silu_a")
        gate_v = sem("gate_v")
        gh_a = sem("gh_a")
        gl_v = sem("gl_v")
        down_t = sem("down_t")
        eo_v = sem("eo_v")
        added = [sem("added0"), sem("added1")]
        c_loaded = [sem("c_loaded0"), sem("c_loaded1")]
        c_v = sem("c_v")
        c_p = sem("c_p")
        c_a = sem("c_a")
        c_stored = sem("c_stored")

        NSETV = 9
        block = ctx.enter_context(nc.Block())

        def since(b, first):
            return not (isinstance(b, int) and b < first)

        def low_of(h, r):
            return (yv, YV) if f"lo{h}{r}" in YV else (yp, YP)

        def stages(b):
            if not isinstance(b, int):
                return True, True, True, True, True
            return b + 1 < B, b < B, 1 <= b <= B, 2 <= b <= B + 1, 3 <= b

        def slots_a(engine, slot, ahead=1):
            pairs = (B - ahead - 4) // 2
            for b in range(4):
                slot(b, b % 2)
            with engine.Fori(0, pairs) as i:
                slot(i * 2 + 4, 0)
                slot(i * 2 + 5, 1)
            for b in range(4 + 2 * pairs, B + 3):
                slot(b, b % 2)

        @block.sync
        def _(sp):
            sp.dma_start(wq32[:, :], wqkv).then_inc(wa_loaded, 16)
            sp.dma_start(wo32[:, :], wout).then_inc(wa_loaded, 16)
            sp.dma_start(gt32[:, :], gate).then_inc(wa_loaded, 16)
            sp.dma_start(bias32[:, 0:3 * C], bqkv).then_inc(wa_loaded, 16)
            sp.dma_start(bias32[:, 3 * C:4 * C], bout).then_inc(wa_loaded, 16)

            def load_xt(b):
                if since(b, 1):
                    sp.wait_ge(xt_loaded, b * 16)
                    sp.wait_ge(xa, prev(b, XA, "xhi"))
                    sp.wait_ge(xp, prev(b, XP, "xlo"))
                    sp.sem_inc(passed_s, 1)
                sp.dma_start(xT32[:, :], xt_in[:, bass.ds(b * T, T)]).then_inc(xt_loaded, 16)

            load_xt(0)
            load_xt(1)

            def load_expert(e, par, first=False):
                if not first:
                    sp.wait_ge(w_split_l, e)
                    sp.wait_ge(w_split_h, e)
                for col, src, lo, hi in ((0, w1, 0, 3 * P), (3 * P, w3, 0, 3 * P), (6 * P, w3, 3 * P, F),
                                         (6 * P + FT, w1, 3 * P, F)):
                    s = src[bass.ds(e, 1), :, lo:hi].rearrange("o m f -> m (o f)")
                    sp.dma_start(wst[:, col:col + hi - lo], s).then_inc(w_loaded, 16)
                s = w2[bass.ds(e, 1), 0:3 * P, :].rearrange("o (k p) m -> p (o k) m", p=P)
                sp.dma_start(wst[:, 2 * F:2 * F + 3 * C].rearrange("p (k m) -> p k m", k=3), s)\
                    .then_inc(w_loaded, 16)
                s = w2[bass.ds(e, 1), 3 * P:F, :].rearrange("o f m -> f (o m)")
                for lo in (0, FT):
                    sp.dma_start(wst[lo:lo + FT, 2 * F + 3 * C:], s).then_inc(w_loaded, 16)

            def slot(b, par):
                do_x, do_y, do_w, do_z, do_d = stages(b)
                bw, bd = b - 1, b - 3
                if isinstance(b, int) and b == 2:
                    sp.wait_ge(setup_p, 3)
                    sp.dma_start(acc[TOK:TOK + SLOTS, :].rearrange("(s p) c -> p s c", p=P),
                                 zrow[:, :].rearrange("p (o c) -> p o c", o=1).to_broadcast([P, NT, C]))\
                        .then_inc(spare_stored, 16)
                    load_expert(0, 0, True)
                if not isinstance(b, int) or b + 2 < B:
                    load_xt(b + 2)
                if do_y:
                    if since(b, 2):
                        sp.wait_ge(wv, prev2(b, WV, "res"))
                        sp.sem_inc(passed_s, 1)
                        sp.wait_ge(x_loaded, b * 16)
                    elif b == 1:
                        sp.wait_ge(x_loaded, 16)
                    sp.sem_inc(passed_s, 1)
                    sp.dma_start(x32[:, par, :, :], x[bass.ds(b * T, T), :].rearrange("(h p) c -> p h c", h=2))\
                        .then_inc(x_loaded, 16)
                if do_d:
                    sp.wait_ge(dv, n(bd, DI, "i1"))
                    sp.sem_inc(passed_s, 1)
                    if since(bd, 1):
                        sp.wait_ge(rows_stored, bd * 16)
                    sp.sem_inc(passed_s, 1)
                    sp.dma_start(slot_rows[:, :, bass.ds(bd * CAP, CAP)].rearrange("e a c -> a e c"),
                                 rows_out[:, :, :]).then_inc(rows_stored, 16)
                if do_w:
                    sp.wait_ge(wa, n(bw, WA, "x11"))
                    sp.sem_inc(passed_s, 1)
                    if since(bw, 1):
                        sp.wait_ge(acc_stored, bw * 16)
                    sp.sem_inc(passed_s, 1)
                    sp.dma_start(acc[bass.ds(bw * T, T), :].rearrange("(h p) c -> p h c", h=2),
                                 x1[:, 1 - par, :, :]).then_inc(acc_stored, 16)

            slots_a(sp, slot, ahead=2)

            def load_rows(e, par):
                sp.dma_start(rows_in[:, par, :], slot_rows[bass.ds(e, 1), :, :].rearrange("o a s -> a (o s)"))\
                    .then_inc(rows_loaded, 16)

            sp.wait_ge(rows_stored, 16 * B)
            load_rows(0, 0)

            def next_expert(e, par):
                load_expert(e + 1, 1 - par)
                sp.wait_ge(rows_loaded, e * 16 + 16)
                if since(e, 1):
                    sp.wait_ge(info_t, e)
                load_rows(e + 1, 1 - par)

            next_expert(0, 0)
            next_expert(1, 1)
            with sp.Fori(1, E // 2 - 1) as i:
                next_expert(i * 2, 0)
                next_expert(i * 2 + 1, 1)
            next_expert(E - 2, 0)

            for q in range(2):
                sp.wait_ge(added[q], E * NCH // 2 * SUB * 16)
            sp.wait_ge(spare_stored, 16)

            def rows_of(t, k):
                return t[bass.ds(k * P * ROWS_C, P * ROWS_C), :].rearrange("(p r) c -> p (r c)", p=P)

            def load_c(k):
                if k > 1:
                    sp.wait_ge(c_loaded[k % 2], k // 2 * 16)
                sp.dma_start(cx[:, k * ROWS_C * C:(k + 1) * ROWS_C * C], rows_of(acc, k))\
                    .then_inc(c_loaded[k % 2], 16)

            ahead = 4
            for k in range(ahead):
                load_c(k)
            for k in range(NC_CH):
                if k + ahead < NC_CH:
                    load_c(k + ahead)
                sp.wait_ge(c_a, k + 1)
                sp.dma_start(rows_of(out, k), cx[:, k * ROWS_C * C:(k + 1) * ROWS_C * C]).then_inc(c_stored, 16)
            sp.wait_ge(acc_stored, 16 * B)
            sp.wait_ge(c_stored, NC_CH * 16)

        @block.gpsimd
        def _(pool):
            g = nc.gpsimd
            made = [0]

            def link(ins):
                made[0] += 1
                ins.then_inc(const_ready, 1)
                pool.wait_ge(const_ready, made[0])

            link(g.memset(ident[:, :], 0.0))
            link(g.affine_select(out=ident[:, :], in_=ident[:, :], compare_op=ALU.not_equal, fill=1.0, base=0,
                                 pattern=[[-1, P]], channel_multiplier=1))
            link(g.tensor_copy(identb[:, :], ident[:, :]))
            link(g.memset(v32[:, :, :, :, :], 1.0))
            link(g.memset(minus_one[:, :], -1.0))
            g.memset(onesb[:, :], 1.0).then_inc(setup_p, 1)
            link(g.memset(tri[:, :], 1.0))
            link(g.affine_select(out=tri[:, :], in_=tri[:, :], compare_op=ALU.is_ge, fill=0.0, base=0,
                                 pattern=[[1, P]], channel_multiplier=-1))
            link(g.tensor_copy(trib[:, :], tri[:, :]))
            link(g.memset(head_mask[:, :, :, :], 1.0))
            link(g.affine_select(out=head_mask[:, :, :, :], in_=head_mask[:, :, :, :], compare_op=ALU.is_ge,
                                 fill=0.0, base=0, pattern=[[0, J], [-32, R], [0, DV]], channel_multiplier=1))
            link(g.affine_select(out=head_mask[:, :, :, :], in_=head_mask[:, :, :, :], compare_op=ALU.is_ge,
                                 fill=0.0, base=31, pattern=[[0, J], [32, R], [0, DV]], channel_multiplier=-1))
            g.memset(half_pow[:, :], -0.5).then_inc(setup_p, 1)

            def late_constants():
                link(g.iota(iota_c[:, :], [[1, CAP]], base=0, channel_multiplier=0,
                            allow_small_or_imprecise_dtypes=True))
                link(g.iota(iota_e[:, :], [[1, E]], base=0, channel_multiplier=0,
                            allow_small_or_imprecise_dtypes=True))
                link(g.memset(aux_mask[:, :, :], 0.0))
                for part in range(3):
                    link(g.affine_select(out=aux_mask[:, :, :], in_=aux_mask[:, :, :], compare_op=ALU.not_equal,
                                         fill=1.0, base=-part * E, pattern=[[-1, E], [0, CAP]],
                                         channel_multiplier=1))
                link(g.affine_select(out=aux_mask[:, :, :], in_=aux_mask[:, :, :], compare_op=ALU.is_ge,
                                     fill=1.0, base=3 * E - 1, pattern=[[0, E], [0, CAP]], channel_multiplier=-1))
                link(g.memset(sel[:, :], 0.0))
                link(g.affine_select(out=sel[:, 0:2], in_=sel[:, 0:2], compare_op=ALU.not_equal, fill=1.0,
                                     base=-3 * E, pattern=[[-1, 2]], channel_multiplier=1))
                link(g.affine_select(out=sel[:, 2:3], in_=sel[:, 2:3], compare_op=ALU.is_ge, fill=1.0,
                                     base=-3 * E, pattern=[[0, 1]], channel_multiplier=1))
                link(g.memset(aux[:, :, :, 3 * E + 1:3 * E + 2], 1.0))
                for q in range(2):
                    link(g.iota(aux[:, q, :, 3 * E:3 * E + 1], [[P, 2], [0, 1]], base=0, channel_multiplier=1,
                                allow_small_or_imprecise_dtypes=True))
                link(g.iota(spare_row[:, :], [[P, NT]], base=TOK, channel_multiplier=1,
                            allow_small_or_imprecise_dtypes=True))
                g.memset(zrow[:, :], 0.0).then_inc(setup_p, 1)

            def x_low(b):
                pool.wait_ge(xa, n(b, XA, "xhi"))
                if since(b, 1):
                    pool.wait_ge(xt, prev(b, XT, "qkv1"))
                g.tensor_tensor(xl[:, :], xT32[:, :], xh[:, :], ALU.subtract).then_inc(xp, 1)

            def stack_low(b, h, par):
                q2 = feat[:, h, 0:C].rearrange("p (c o) -> p c o", o=1).to_broadcast([P, C, 2])
                k2 = feat[:, h, C:2 * C].rearrange("p (c o) -> p c o", o=1).to_broadcast([P, C, 2])
                sq, sk = stack[:, par, h, 0, :, :, :], stack[:, par, h, 1, :, :, :]
                if since(b, 2):
                    pool.wait_ge(xt, prev2(b, XT, f"tr{h}"))
                    pool.wait_ge(yt, prev2(b, YT, "state"))
                pool.wait_ge(xa, n(b, XA, f"qh{h}"))
                g.tensor_tensor(sq[:, :, :, 1], q2, sq[:, :, :, 0], ALU.subtract).then_inc(xp, 1)
                pool.wait_ge(xa, n(b, XA, f"kh{h}"))
                g.tensor_tensor(sk[:, :, 1, :], k2, sk[:, :, 0, :], ALU.subtract).then_inc(xp, 1)

            def v_low(b, h, par):
                pool.wait_ge(xa, n(b, XA, f"vh{h}"))
                if since(b, 2):
                    pool.wait_ge(yt, prev2(b, YT, "ctx"))
                g.tensor_tensor(vl[:, par, h, :, :], v32[:, par, h, :, :], vh[:, par, h, :, :], ALU.subtract)\
                    .then_inc(xp, 1)

            def split_weights(e, par):
                pool.wait_ge(w_loaded, e * 112 + 112)
                if not (isinstance(e, int) and e < 2):
                    pool.wait_ge(down_t, e * NCH - NCH)
                pool.sem_inc(passed_p, 1)
                g.tensor_copy(wh[:, par, :], wst[:, :]).then_inc(w_split_h, 1)
                pool.wait_ge(w_split_h, e + 1)
                g.tensor_tensor(wl[:, par, :], wst[:, :], wh[:, par, :], ALU.subtract).then_inc(w_split_l, 1)

            x_low(0)
            late_constants()
            stack_low(0, 0, 0)
            stack_low(0, 1, 0)
            v_low(0, 0, 0)
            v_low(0, 1, 0)

            def slot(b, par):
                do_x, do_y, do_w, do_z, do_d = stages(b)
                o = 1 - par
                bx, bw, bz = b + 1, b - 1, b - 2

                def state_low():
                    pool.wait_ge(ya, n(b, YA, "shi"))
                    if since(b, 1):
                        pool.wait_ge(yt, prev(b, YT, "ctx"))
                    g.tensor_tensor(sl[:, :, :], s32[:, :, :], sh[:, :, :], ALU.subtract).then_inc(yp, 1)

                def scores_low(h, r):
                    pool.wait_ge(ya, n(b, YA, f"hi{h}{r}"))
                    if h:
                        pool.wait_ge(yt, n(b, YT, f"ctx0{r}"))
                    elif since(b, 1):
                        pool.wait_ge(yt, prev(b, YT, f"ctx1{r}"))
                    g.tensor_tensor(am_hl[:, 1, r, :, :], am32[:, r, :, :], am_hl[:, 0, r, :, :], ALU.subtract)\
                        .then_inc(yp, 1)

                def rstd_pow():
                    pool.wait_ge(wv, n(bw, WV, "ve"))
                    if since(bw, 1):
                        pool.wait_ge(wa, prev(bw, WA, "x11"))
                    g.tensor_tensor(rstd[:, :], ve[:, :], half_pow[:, 0:2], ALU.pow).then_inc(wp, 1)
                    pool.wait_ge(wp, n(bw, WP, "rstd"))
                    g.tensor_tensor(nmr[:, :], nmean[:, :], rstd[:, :], ALU.mult).then_inc(wp, 1)

                def prob_parts():
                    pool.wait_ge(zv, n(bz, ZV, "pr"))
                    if since(bz, 2):
                        pool.wait_ge(dt, prev2(bz, DT, "i1"))
                    pool.sem_inc(passed_p, 1)
                    parts = aux[:, par, :, :]
                    g.tensor_copy(parts[:, :, 0:E], pr[:, :, :]).then_inc(zp, 1)
                    pool.wait_ge(zp, n(bz, ZP, "ph"))
                    g.tensor_tensor(pres[:, :, :], pr[:, :, :], parts[:, :, 0:E], ALU.subtract).then_inc(zp, 1)
                    pool.wait_ge(zp, n(bz, ZP, "r1"))
                    pool.sem_inc(passed_p, 1)
                    g.tensor_copy(parts[:, :, E:2 * E], pres[:, :, :]).then_inc(zp, 1)
                    pool.wait_ge(zp, n(bz, ZP, "pm"))
                    g.tensor_tensor(parts[:, :, 2 * E:3 * E], pres[:, :, :], parts[:, :, E:2 * E], ALU.subtract)\
                        .then_inc(zp, 1)

                def x1_low():
                    pool.wait_ge(za, n(bz, ZA, "x1h"))
                    if since(bz, 2):
                        pool.wait_ge(dt, prev2(bz, DT, "l1"))
                    g.tensor_tensor(x1l[:, par, :, :], x1[:, par, :, :], x1h[:, par, :, :], ALU.subtract)\
                        .then_inc(zp, 1)

                if do_y:
                    scores_low(0, 1)
                    scores_low(0, 3)
                if do_x:
                    x_low(bx)
                if do_y:
                    state_low()
                if do_z:
                    prob_parts()
                if do_y:
                    scores_low(0, 2)
                    scores_low(1, 1)
                if do_x:
                    stack_low(bx, 0, o)
                if do_y:
                    scores_low(1, 3)
                    scores_low(1, 2)
                if do_x:
                    stack_low(bx, 1, o)
                if do_w:
                    rstd_pow()
                if do_x:
                    v_low(bx, 0, o)
                    v_low(bx, 1, o)
                if do_z:
                    x1_low()

                if isinstance(b, int) and b == B - 1:
                    split_weights(0, 0)

            slots_a(pool, slot)

            def add_rows(nb, c, par, cpar):
                pool.wait_ge(eo_v, nb + 1)
                pool.sem_inc(passed_p, 1)
                for s in range(SUB):
                    g.indirect_dma_start(
                        out=acc, out_offset=bass.IndirectOffsetOnAxis(
                            ap=idx[:, par, c * SUB + s:c * SUB + s + 1], axis=0),
                        in_=eo[:, cpar, s, :], in_offset=None, compute_op=ALU.add).then_inc(added[cpar], 16)

            link(g.memset(slot_base[:, :], 0.0))
            for b in range(1, B):
                t0, t1 = max(0, (b * CAP) // P), NT
                v = slot_base[:, t0:t1]
                ins = g.affine_select(out=v, in_=v, compare_op=ALU.is_ge, fill=float(T * b),
                                      base=b * CAP - 1 - P * t0, pattern=[[-P, t1 - t0]], channel_multiplier=-1)
                if b < B - 1:
                    link(ins)
            ins.then_inc(setup_p, 1)
            pool.wait_ge(acc_stored, 16 * B)
            pool.wait_ge(spare_stored, 16)

            def experts(i, first, last):
                for q in range(2 * NCH):
                    par, c = q // NCH, q % NCH
                    nb = i * (2 * NCH) + q
                    if c == 0:
                        if par or not first:
                            pool.wait_ge(added[0], (i * NCH + (NCH // 2 + 1 if par else 0)) * SUB * 16)
                            pool.wait_ge(added[1], (i * NCH + (NCH // 2 if par else 0)) * SUB * 16)
                    add_rows(nb, c, par, q % 2)
                    if c == 0 and not (last and par == 1):
                        split_weights(i * 2 + par + 1, 1 - par)

            experts(0, True, False)
            with pool.Fori(1, E // 2 - 1) as i:
                experts(i, False, False)
            experts(E // 2 - 1, False, True)

            def chunk_c(k, par, first):
                pool.wait_ge(c_v, k * 4 + 4)
                if not first:
                    pool.wait_ge(c_a, k - 1)
                g.tensor_tensor(crs[:, par, :], cve[:, par, :], half_pow[:, :], ALU.pow).then_inc(c_p, 1)
                pool.wait_ge(c_p, k * 2 + 1)
                g.tensor_tensor(cnmr[:, par, :], cnm[:, par, :], crs[:, par, :], ALU.mult).then_inc(c_p, 1)

            chunk_c(0, 0, True)
            chunk_c(1, 1, True)
            with pool.Fori(1, NC_CH // 2) as i:
                chunk_c(i * 2, 0, False)
                chunk_c(i * 2 + 1, 1, False)

        @block.vector
        def _(dve):
            v = nc.vector
            made = [0]

            def link(ins):
                made[0] += 1
                ins.then_inc(setup_v, 1)
                dve.wait_ge(setup_v, made[0])

            link(v.memset(bias3[:, :], 0.0))
            dve.wait_ge(wa_loaded, 5 * 16)
            v.tensor_copy(wqh[:, :], wq32[:, :]).then_inc(setup_v, 1)
            made[0] += 1
            link(v.tensor_scalar(bias32[:, 0:2 * C], bias32[:, 0:2 * C], 1.0, None, ALU.add))
            v.tensor_tensor(wql[:, :], wq32[:, :], wqh[:, :], ALU.subtract).then_inc(setup_v, 1)
            made[0] += 1
            link(v.tensor_copy(bias3[0:1, :], bias32[:, :]))
            link(v.tensor_tensor(bias32[:, :], bias32[:, :], bias3[0:1, :], ALU.subtract))
            link(v.tensor_copy(bias_m[:, :], bias32[:, :]))
            v.tensor_copy(bias3[32:33, :], bias_m[:, :]).then_inc(setup_v, 1)
            made[0] += 1
            link(v.tensor_tensor(bias3[64:65, :], bias32[:, :], bias_m[:, :], ALU.subtract))
            assert made[0] == NSETV
            dve.wait_ge(setup_p, 2)

            def feats(b, h):
                dve.wait_ge(xa, n(b, XA, f"ex{h}"))
                if since(b, 1):
                    dve.wait_ge(xp, prev(b, XP, f"kl{h}"))
                v.scalar_tensor_tensor(out=feat[:, h, :], in0=ex[:, h, :], scalar=1.0, in1=p_qkv[:, 0:2 * C],
                                       op0=ALU.min, op1=ALU.max).then_inc(xv, 1)

            feats(0, 0)
            feats(0, 1)

            def slot(b, par):
                do_x, do_y, do_w, do_z, do_d = stages(b)
                o = 1 - par
                bx, bw, bz, bd = b + 1, b - 1, b - 2, b - 3

                def mask(h, r):
                    dve.wait_ge(yt, n(b, YT, f"sc{h}{r}"))
                    low, steps = low_of(1 - h, r)
                    if h:
                        dve.wait_ge(low, n(b, steps, f"lo0{r}"))
                    elif since(b, 1):
                        dve.wait_ge(low, prev(b, steps, f"lo1{r}"))
                    m = tri[:, :].rearrange("p (o t) -> p o t", o=1).to_broadcast([P, J, P])
                    v.tensor_tensor(am32[:, r, :, :], p_sc[r % 2][:, :].rearrange("p (j t) -> p j t", j=J), m,
                                    ALU.mult).then_inc(yv, 1)

                def scores_low(h, r):
                    dve.wait_ge(ya, n(b, YA, f"hi{h}{r}"))
                    if h:
                        dve.wait_ge(yt, n(b, YT, f"ctx0{r}"))
                    elif since(b, 1):
                        dve.wait_ge(yt, prev(b, YT, f"ctx1{r}"))
                    v.tensor_tensor(am_hl[:, 1, r, :, :], am32[:, r, :, :], am_hl[:, 0, r, :, :], ALU.subtract)\
                        .then_inc(yv, 1)

                def state():
                    dve.wait_ge(yt, n(b, YT, "state"))
                    if since(b, 1):
                        dve.wait_ge(yp, prev(b, YP, "slo"))
                    v.tensor_tensor(s32[:, :, :], p_state.rearrange("p (j q) -> p j q", j=J),
                                    head_mask[:, :, :, :].rearrange("p j r e -> p j (r e)"), ALU.mult)\
                        .then_inc(yv, 1)

                def normalize():
                    c4 = p_ctx.rearrange("p h (g e) -> p (h g) e", e=DV)
                    dve.wait_ge(yt, n(b, YT, "ctx"))
                    if since(b, 1):
                        dve.wait_ge(yv, prev(b, YV, "cn"))
                    v.tensor_scalar(den[:, :], c4[:, :, DH], EPS_ATT, None, ALU.add).then_inc(yv, 1)
                    dve.wait_ge(yv, n(b, YV, "den"))
                    v.reciprocal(rec[:, :], den[:, :]).then_inc(yv, 1)
                    dve.wait_ge(yv, n(b, YV, "rec"))
                    if since(b, 1):
                        dve.wait_ge(wt, prev(b, WT, "ct"))
                    v.tensor_tensor(cn[:, :, :].rearrange("p h (g e) -> p (h g) e", e=DH), c4[:, :, 0:DH],
                                    rec[:, :].rearrange("p (g o) -> p g o", o=1).to_broadcast([P, 2 * H, DH]),
                                    ALU.mult).then_inc(yv, 1)

                def residual():
                    dve.wait_ge(wt, n(bw, WT, "proj"))
                    dve.wait_ge(x_loaded, bw * 16 + 16)
                    if since(bw, 1):
                        dve.wait_ge(wa, prev(bw, WA, "x11"))
                    v.tensor_tensor(r32[:, :, :], p_y[:, 2 * C:4 * C].rearrange("p (h c) -> p h c", h=2),
                                    x32[:, o, :, :], ALU.add).then_inc(wv, 1)

                def statistics():
                    dve.wait_ge(wv, n(bw, WV, "res"))
                    for h in range(2):
                        v.bn_stats(bn[:, h, :], r32[:, h, :]).then_inc(wv, 1)
                    dve.wait_ge(wv, n(bw, WV, "bn1"))
                    for h in range(2):
                        dve.sem_inc(passed_v, 1)
                        v.bn_aggr(mv[:, h, :], bn[:, h, :]).then_inc(wv, 1)

                def variance():
                    dve.wait_ge(wv, n(bw, WV, "ag1"))
                    if since(bw, 1):
                        dve.wait_ge(wp, prev(bw, WP, "nmr"))
                    v.tensor_scalar(nmean[:, :], mv[:, :, 0], -1.0, None, ALU.mult).then_inc(wv, 1)
                    v.tensor_scalar(ve[:, :], mv[:, :, 1], EPS_LN, None, ALU.add).then_inc(wv, 1)

                lg = p_z[:, 0:2 * E].rearrange("p (h e) -> p h e", h=2)
                pos = p_z[:, 32:32 + 2 * E].rearrange("p (h e) -> p h e", h=2)

                def logits_max():
                    dve.wait_ge(zt, n(bz, ZT, "rt"))
                    if since(bz, 1):
                        dve.wait_ge(zv, prev(bz, ZV, "nm"))
                    for h in range(2):
                        dve.sem_inc(passed_v, 1)
                        v.max(mx[:, h, :], lg[:, h, :]).then_inc(zv, 1)
                    dve.wait_ge(zv, n(bz, ZV, "mx1"))
                    if since(bz, 1):
                        dve.wait_ge(za, prev(bz, ZA, "el1"))
                    v.tensor_scalar(nm[:, :], mx[:, :, 0], -1.0, None, ALU.mult).then_inc(zv, 1)

                def probabilities():
                    dve.wait_ge(za, n(bz, ZA, "el1"))
                    v.reciprocal(rs[:, :], es[:, :]).then_inc(zv, 1)
                    dve.wait_ge(zv, n(bz, ZV, "rs"))
                    if since(bz, 1):
                        dve.wait_ge(zp, prev(bz, ZP, "r1"))
                    v.tensor_tensor(pr[:, :, :], el[:, :, :],
                                    rs[:, :].rearrange("p (h o) -> p h o", o=1).to_broadcast([P, 2, E]),
                                    ALU.mult).then_inc(zv, 1)

                def top():
                    dve.wait_ge(zv, n(bz, ZV, "pr"))
                    for h in range(2):
                        dve.sem_inc(passed_v, 1)
                        v.max(tp[:, h, :], pr[:, h, :]).then_inc(zv, 1)
                    dve.wait_ge(zv, n(bz, ZV, "tp1"))
                    for h in range(2):
                        dve.sem_inc(passed_v, 1)
                        v.max_index(ti[:, h, :], tp[:, h, :], pr[:, h, :]).then_inc(zv, 1)

                def top_index():
                    dve.wait_ge(zv, n(bz, ZV, "ti1"))
                    v.tensor_copy(tif[:, :, :], ti[:, :, 0:K_TOP]).then_inc(zv, 1)

                def chosen():
                    if isinstance(bz, int) and bz == 0:
                        dve.wait_ge(setup_p, 3)
                    dve.wait_ge(zv, n(bz, ZV, "tif"))
                    ie = iota_e[:, :].rearrange("p (o e) -> p o e", o=1).to_broadcast([P, 2, E])
                    for k, m in ((0, m0), (1, m1)):
                        v.tensor_tensor(m[:, :, :], ie, tif[:, :, k:k + 1].to_broadcast([P, 2, E]),
                                        ALU.is_equal).then_inc(zv, 1)

                def chosen_both():
                    dve.wait_ge(zv, n(bz, ZV, "m1"))
                    if since(bz, 1):
                        dve.wait_ge(zt, prev(bz, ZT, "pos"))
                    v.tensor_tensor(mb[:, :, :], m0[:, :, :], m1[:, :, :], ALU.add).then_inc(zv, 1)

                def within_capacity():
                    dve.wait_ge(zt, n(bz, ZT, "pos"))
                    v.scalar_tensor_tensor(out=val[:, :, :], in0=pos, scalar=CAP + 0.5, in1=mb[:, :, :],
                                           op0=ALU.is_le, op1=ALU.mult).then_inc(zv, 1)
                    dve.wait_ge(zv, n(bz, ZV, "val"))
                    v.tensor_tensor(dpa[:, :, :], pos, val[:, :, :], ALU.mult).then_inc(zv, 1)

                def slot_number():
                    dve.wait_ge(zv, n(bz, ZV, "dpa"))
                    v.tensor_scalar(dp[:, :, :], dpa[:, :, :], -1.0, None, ALU.add).then_inc(zv, 1)

                def one_hot():
                    dve.wait_ge(zv, n(bz, ZV, "dp"))
                    if since(bz, 1):
                        dve.wait_ge(dt, prev(bz, DT, "l1"))
                    for h in range(2):
                        v.tensor_tensor(onehot[:, h, :, :],
                                        iota_c[:, :].rearrange("p (o c) -> p o c", o=1).to_broadcast([P, E, CAP]),
                                        dp[:, h, :].rearrange("p (e o) -> p e o", o=1).to_broadcast([P, E, CAP]),
                                        ALU.is_equal).then_inc(zv, 1)

                def slot_info(q):
                    if isinstance(bd, int) and bd == 0:
                        dve.wait_ge(setup_p, 3)
                    dve.wait_ge(dt, n(bd, DT, f"i{q}"))
                    if since(bd, 1):
                        dve.wait_ge(rows_stored, bd * 16)
                    v.tensor_tensor(rows_out[:, 4 * q:4 * q + 4, :],
                                    p_d[0:NAUX, 0:HALF].rearrange("p (e c) -> p e c", c=CAP),
                                    aux_mask[0:NAUX, 4 * q:4 * q + 4, :], ALU.mult).then_inc(dv, 1)

                if do_y:
                    mask(0, 0)
                    mask(0, 1)
                if do_d:
                    slot_info(0)
                if do_y:
                    mask(0, 2)
                    mask(0, 3)
                    scores_low(0, 0)
                    state()
                    mask(1, 0)
                if do_z:
                    logits_max()
                if do_d:
                    slot_info(1)
                if do_y:
                    mask(1, 1)
                if do_z:
                    probabilities()
                    top()
                    top_index()
                    chosen()
                if do_y:
                    scores_low(1, 0)
                if do_x:
                    feats(bx, 0)
                if do_y:
                    mask(1, 3)
                if do_z:
                    chosen_both()
                if do_y:
                    mask(1, 2)
                if do_w:
                    residual()
                if do_z:
                    within_capacity()
                if do_w:
                    statistics()
                if do_z:
                    slot_number()
                if do_x:
                    feats(bx, 1)
                if do_w:
                    variance()
                if do_z:
                    one_hot()
                if do_y:
                    normalize()

            slots_a(dve, slot)

            def info(e, par):
                dve.wait_ge(info_t, e + 1)
                p3 = p_info[:, 0:3 * NT].rearrange("p (t q) -> p t q", q=3)
                v.tensor_tensor(idx_a[:, :], p3[:, :, 0], slot_base[:, :], ALU.add).then_inc(info_v, 1)
                dve.wait_ge(info_v, e * 5 + 1)
                v.tensor_tensor(idx_a[:, :], idx_a[:, :], spare_row[:, :], ALU.subtract).then_inc(info_v, 1)
                dve.wait_ge(info_v, e * 5 + 2)
                v.tensor_tensor(idx_a[:, :], p3[:, :, 1], idx_a[:, :], ALU.mult).then_inc(info_v, 1)
                dve.wait_ge(info_v, e * 5 + 3)
                v.tensor_tensor(idx[:, par, :], idx_a[:, :], spare_row[:, :], ALU.add).then_inc(info_v, 1)
                v.tensor_copy(prob[:, par, :], p3[:, :, 2]).then_inc(info_v, 1)

            def gate_chunk(nb, cpar, first, early):
                for k in range(FK):
                    rows = P if k < 3 else FT
                    dve.wait_ge(silu_a, nb * FK + (k + 1))
                    if not first:
                        dve.wait_ge(gl_v, nb * FK + (k + 1 - FK))
                    h3 = UP[k][1][:, :] if k < 3 else UP[k][0][0:FT, :]
                    v.tensor_tensor(g32[0:rows, k, :], sil[0:rows, k % 2, :], h3, ALU.mult).then_inc(gate_v, 1)
                    if k:
                        low_part(nb, k - 1, cpar, early)

            def low_part(nb, k, cpar, early):
                rows = P if k < 3 else FT
                dve.wait_ge(gh_a, nb * FK + (k + 1))
                if k == 0 and not early:
                    dve.wait_ge(down_t, nb - 1)
                low = gl[:, cpar, k, :] if k < 3 else gh[FT:2 * FT, cpar, k, :]
                v.tensor_tensor(low, g32[0:rows, k, :], gh[0:rows, cpar, k, :], ALU.subtract).then_inc(gl_v, 1)

            def scale_rows(nb, e, c, par, cpar, nadds):
                dve.wait_ge(down_t, nb + 1)
                if nadds is not None:
                    dve.wait_ge(added[cpar], nadds)
                dve.wait_ge(info_v, e * 5 + 5)
                v.tensor_tensor(eo[:, cpar, :, :], DOWN[cpar][:, :].rearrange("p (s m) -> p s m", s=SUB),
                                prob[:, par, c * SUB:(c + 1) * SUB].rearrange("p (s o) -> p s o", o=1)
                                .to_broadcast([P, SUB, C]), ALU.mult).then_inc(eo_v, 1)

            def experts(i, first):
                for q in range(2 * NCH):
                    par, c, cpar = q // NCH, q % NCH, q % 2
                    nb = i * (2 * NCH) + q
                    gate_chunk(nb, cpar, first and q == 0, first and q < 2)
                    if c == 0:
                        if first and par == 0:
                            dve.wait_ge(setup_p, 4)
                        if not first:
                            back = (0, 0) if par else (NCH // 2, NCH // 2 + 1)
                            dve.wait_ge(added[0], (i * NCH - back[0]) * SUB * 16)
                            dve.wait_ge(added[1], (i * NCH - back[1]) * SUB * 16)
                        info(i * 2 + par, par)
                    if q or not first:
                        pq = (q - 1) % (2 * NCH)
                        cnt = None if first and pq < 2 else (i * NCH + (q - 1) // 2) * SUB * 16
                        scale_rows(nb - 1, i * 2 + (q - 1) // NCH, pq % NCH, pq // NCH, pq % 2, cnt)
                    low_part(nb, FK - 1, cpar, first and q < 2)

            experts(0, True)
            with dve.Fori(1, E // 2) as i:
                experts(i, False)
            scale_rows(E * NCH - 1, E - 1, NCH - 1, 1, 1, (E // 2 * NCH - 1) * SUB * 16)

            def chunk_c(k, par, i, first):
                dve.wait_ge(c_loaded[par], i * 16 + 16)
                for r in range(ROWS_C):
                    if not first and r == 0:
                        dve.sem_inc(passed_v, 1)
                    ins = v.bn_stats(cst[:, par, r, :], cx[:, bass.ds((k * ROWS_C + r) * C, C)])
                ins.then_inc(c_v, 1)
                dve.wait_ge(c_v, k * 4 + 1)
                dve.sem_inc(passed_v, 1)
                for r in range(ROWS_C):
                    ins = v.bn_aggr(cmv[:, par, r, :], cst[:, par, r, :])
                ins.then_inc(c_v, 1)
                dve.wait_ge(c_v, k * 4 + 2)
                if not first:
                    dve.wait_ge(c_p, k * 2 - 2)
                v.tensor_scalar(cnm[:, par, :], cmv[:, par, :, 0], -1.0, None, ALU.mult).then_inc(c_v, 1)
                v.tensor_scalar(cve[:, par, :], cmv[:, par, :, 1], EPS_LN, None, ALU.add).then_inc(c_v, 1)

            chunk_c(0, 0, 0, True)
            chunk_c(1, 1, 0, True)
            with dve.Fori(1, NC_CH // 2) as i:
                chunk_c(i * 2, 0, i, False)
                chunk_c(i * 2 + 1, 1, i, False)

        @block.scalar
        def _(act):
            a = nc.scalar

            def x_high(b):
                act.wait_ge(xt_loaded, b * 16 + 16)
                if since(b, 1):
                    act.wait_ge(xt, prev(b, XT, "qkv1"))
                    act.wait_ge(xp, prev(b, XP, "xlo"))
                a.activation(xh[:, :], xT32[:, :], ACT.Copy).then_inc(xa, 1)

            def exps(b, h):
                act.wait_ge(xt, n(b, XT, f"qkv{h}"))
                if since(b, 1):
                    act.wait_ge(xv, prev(b, XV, f"f{h}"))
                a.activation(ex[:, h, :], p_qkv[:, 0:2 * C], ACT.Exp, bias=minus_one[:, 0:1]).then_inc(xa, 1)

            def values(b, h, par):
                act.wait_ge(xv, n(b, XV, f"f{h}"))
                if since(b, 2):
                    act.wait_ge(xp, prev2(b, XP, f"vl{h}"))
                    act.wait_ge(yt, prev2(b, YT, "ctx"))
                a.activation(v32[:, par, h, :, 0:DH],
                             p_qkv[:, 2 * C:3 * C].rearrange("p (h e) -> p h e", e=DH), ACT.Copy).then_inc(xa, 1)

            def stack_high(b, h, par):
                q2 = feat[:, h, 0:C].rearrange("p (c o) -> p c o", o=1).to_broadcast([P, C, 2])
                k2 = feat[:, h, C:2 * C].rearrange("p (c o) -> p c o", o=1).to_broadcast([P, C, 2])
                act.wait_ge(xv, n(b, XV, f"f{h}"))
                if since(b, 2):
                    act.wait_ge(xt, prev2(b, XT, f"tr{h}"))
                    act.wait_ge(yt, prev2(b, YT, "state"))
                a.activation(stack[:, par, h, 0, :, :, 0], q2, ACT.Copy).then_inc(xa, 1)
                a.activation(stack[:, par, h, 1, :, 0, :], k2, ACT.Copy).then_inc(xa, 1)

            def v_high(b, h, par):
                act.wait_ge(xa, n(b, XA, f"v{h}"))
                if since(b, 2):
                    act.wait_ge(yt, prev2(b, YT, "ctx"))
                a.activation(vh[:, par, h, :, :], v32[:, par, h, :, :], ACT.Copy).then_inc(xa, 1)

            def evac_t(b, h, par):
                act.wait_ge(xt, n(b, XT, f"tr{h}"))
                if since(b, 2):
                    act.wait_ge(yt, prev2(b, YT, "ctx"))
                a.activation(qkT[:, par, h, :, :, :].rearrange("p q j t -> p (q j) t"), p_tr, ACT.Copy)\
                    .then_inc(xa, 1)

            act.wait_ge(setup_p, 1)
            x_high(0)
            exps(0, 0)
            stack_high(0, 0, 0)
            values(0, 0, 0)
            exps(0, 1)
            stack_high(0, 1, 0)
            v_high(0, 0, 0)
            evac_t(0, 0, 0)
            values(0, 1, 0)
            v_high(0, 1, 0)
            evac_t(0, 1, 0)

            def slot(b, par):
                do_x, do_y, do_w, do_z, do_d = stages(b)
                o = 1 - par
                bx, bw, bz, bd = b + 1, b - 1, b - 2, b - 3

                def x1_t_out():
                    act.wait_ge(zt, n(bz, ZT, "x1t"))
                    if since(bz, 1):
                        act.wait_ge(zt, prev(bz, ZT, "rt"))
                    a.activation(x1T[:, :, :].rearrange("p h t -> p (h t)"), p_z[:, 0:2 * P], ACT.Copy)\
                        .then_inc(za, 1)

                def ctx_t_out():
                    act.wait_ge(wt, n(bw, WT, "ct"))
                    if since(bw, 1):
                        act.wait_ge(wt, prev(bw, WT, "proj"))
                    a.activation(cT[:, :, :].rearrange("p h t -> p (h t)"), p_y[:, 0:2 * P], ACT.Copy)\
                        .then_inc(wa, 1)

                def scale():
                    act.wait_ge(wp, n(bw, WP, "nmr"))
                    if since(bw, 2):
                        act.wait_ge(acc_stored, bw * 16 - 16)
                        act.wait_ge(zp, prev2(bw, ZP, "x1l"))
                        act.wait_ge(zt, prev2(bw, ZT, "x1t"))
                    for h in range(2):
                        a.activation(x1[:, o, h, :], r32[:, h, :], ACT.Identity, bias=nmr[:, h:h + 1],
                                     scale=rstd[:, h:h + 1]).then_inc(wa, 1)

                def state_high():
                    act.wait_ge(yv, n(b, YV, "s32"))
                    if since(b, 1):
                        act.wait_ge(yt, prev(b, YT, "ctx"))
                    a.activation(sh[:, :, :], s32[:, :, :], ACT.Copy).then_inc(ya, 1)

                def scores_high(h, r):
                    act.wait_ge(yv, n(b, YV, f"am{h}{r}"))
                    if h:
                        act.wait_ge(yt, n(b, YT, f"ctx0{r}"))
                    elif since(b, 1):
                        act.wait_ge(yt, prev(b, YT, f"ctx1{r}"))
                    a.activation(am_hl[:, 0, r, :, :], am32[:, r, :, :], ACT.Copy).then_inc(ya, 1)

                def logits_exp():
                    act.wait_ge(zv, n(bz, ZV, "nm"))
                    if since(bz, 1):
                        act.wait_ge(zv, prev(bz, ZV, "pr"))
                    for h in range(2):
                        a.activation(el[:, h, :], p_z[:, h * E:(h + 1) * E], ACT.Exp, bias=nm[:, h:h + 1],
                                     accum_out=es[:, h:h + 1]).then_inc(za, 1)

                def x1_high():
                    act.wait_ge(wa, n(bz, WA, "x11"))
                    if since(bz, 2):
                        act.wait_ge(dt, prev2(bz, DT, "h1"))
                    a.activation(x1h[:, par, :, :], x1[:, par, :, :], ACT.Copy).then_inc(za, 1)

                def slots_out(part, q):
                    act.wait_ge(dt, n(bd, DT, f"{part}{q}"))
                    xd = xdh if part == "h" else xdl
                    a.activation(xd[:, 4 * q:4 * q + 4, bass.ds(bd * CAP, CAP)],
                                 p_d[:, 0:HALF].rearrange("p (e c) -> p e c", c=CAP), ACT.Copy).then_inc(da, 1)

                if do_y:
                    scores_high(0, 0)
                if do_z:
                    x1_t_out()
                if do_y:
                    scores_high(0, 1)
                    scores_high(0, 3)
                    state_high()
                if do_x:
                    x_high(bx)
                if do_z:
                    logits_exp()
                if do_y:
                    scores_high(0, 2)
                if do_z:
                    x1_high()
                if do_y:
                    scores_high(1, 0)
                if do_d:
                    slots_out("h", 0)
                if do_y:
                    scores_high(1, 1)
                if do_w:
                    ctx_t_out()
                if do_x:
                    exps(bx, 0)
                if do_d:
                    slots_out("h", 1)
                if do_x:
                    stack_high(bx, 0, o)
                    values(bx, 0, o)
                if do_y:
                    scores_high(1, 3)
                    scores_high(1, 2)
                if do_x:
                    exps(bx, 1)
                if do_d:
                    slots_out("l", 0)
                if do_x:
                    stack_high(bx, 1, o)
                    v_high(bx, 0, o)
                    evac_t(bx, 0, o)
                    values(bx, 1, o)
                    v_high(bx, 1, o)
                if do_d:
                    slots_out("l", 1)
                if do_w:
                    scale()
                if do_x:
                    evac_t(bx, 1, o)

            slots_a(act, slot)

            def chunk(nb, cpar, first):
                def high(k):
                    rows = P if k < 3 else FT
                    act.wait_ge(gate_v, nb * FK + (k + 1))
                    a.activation(gh[0:rows, cpar, k, :], g32[0:rows, k, :], ACT.Copy).then_inc(gh_a, 1)

                for k in range(FK):
                    rows = P if k < 3 else FT
                    act.wait_ge(up_t, nb * FK + (k + 1))
                    if not (first and k < 2):
                        act.wait_ge(gate_v, nb * FK + (k - 1))
                    h1 = UP[k][0][:, :] if k < 3 else UP[k][0][FT:P, :]
                    a.activation(sil[0:rows, k % 2, :], h1, ACT.Silu).then_inc(silu_a, 1)
                    if k == 0 and not (isinstance(nb, int) and nb < 2):
                        act.wait_ge(down_t, nb - 1)
                    if k > 0:
                        high(k - 1)
                high(FK - 1)

            for nb in range(2 * NCH):
                chunk(nb, nb % 2, nb == 0)
            with act.Fori(1, E // 2) as i:
                for q in range(2 * NCH):
                    chunk(i * (2 * NCH) + q, q % 2, False)

            def chunk_c(k, par):
                act.wait_ge(c_p, k * 2 + 2)
                for r in range(ROWS_C):
                    rows = cx[:, bass.ds((k * ROWS_C + r) * C, C)]
                    ins = a.activation(rows, rows, ACT.Identity, bias=cnmr[:, par, r:r + 1],
                                       scale=crs[:, par, r:r + 1])
                ins.then_inc(c_a, 1)

            with act.Fori(0, NC_CH // 2) as i:
                chunk_c(i * 2, 0)
                chunk_c(i * 2 + 1, 1)

        @block.tensor
        def _(pe):
            t = nc.tensor

            def qkv(b, h):
                if h == 0:
                    pe.wait_ge(xp, n(b, XP, "xlo"))
                    pe.wait_ge(xa, n(b, XA, "xhi"))
                if h:
                    pe.wait_ge(xv, n(b, XV, "f0"))
                    pe.wait_ge(xa, n(b, XA, "v0"))
                elif since(b, 1):
                    pe.wait_ge(xv, prev(b, XV, "f1"))
                    pe.wait_ge(xa, prev(b, XA, "v1"))
                sl_ = slice(h * P, (h + 1) * P)
                o_ = p_qkv[:, 0:3 * C]
                t.matmul(o_, xh[:, sl_], wqh[:, :], start=True, stop=False)
                t.matmul(o_, xh[:, sl_], wql[:, :], start=False, stop=False)
                t.matmul(o_, xl[:, sl_], wqh[:, :], start=False, stop=False)
                t.matmul(o_, onesb[:, :], bias3[:, 0:3 * C], start=False, stop=True).then_inc(xt, 1)

            def transposes(b, h, par):
                pe.wait_ge(xa, n(b, XA, f"kh{h}"))
                pe.wait_ge(xp, n(b, XP, f"kl{h}"))
                if h or since(b, 1):
                    pe.wait_ge(xa, n(b, XA, "T0") if h else prev(b, XA, "T1"))
                for qk in range(2):
                    for j in range(J):
                        src = stack[:, par, h, qk, 32 * j:32 * j + 32, :, :].rearrange("p c a d -> p (c a d)")
                        ins = t.transpose(p_tr[:, qk * J + j, :], src, identb[:, :])
                ins.then_inc(xt, 1)

            pe.wait_ge(setup_p, 1)
            pe.wait_ge(setup_v, NSETV)
            qkv(0, 0)
            qkv(0, 1)
            transposes(0, 0, 0)
            transposes(0, 1, 0)

            def slot(b, par):
                do_x, do_y, do_w, do_z, do_d = stages(b)
                o = 1 - par
                bx, bw, bz, bd = b + 1, b - 1, b - 2, b - 3

                def x1_t():
                    pe.wait_ge(wa, n(bz, WA, "x11"))
                    if since(bz, 1):
                        pe.wait_ge(za, prev(bz, ZA, "el1"))
                        pe.wait_ge(zv, prev(bz, ZV, "dpa"))
                    for h in range(2):
                        ins = t.transpose(p_z[:, h * P:(h + 1) * P], x1[:, par, h, :], ident[:, :])
                    ins.then_inc(zt, 1)

                def router():
                    pe.wait_ge(za, n(bz, ZA, "x1T"))
                    for h in range(2):
                        ins = t.matmul(p_z[:, h * E:(h + 1) * E], x1T[:, h, :], gt32[:, :],
                                       start=True, stop=True)
                    ins.then_inc(zt, 1)

                def positions():
                    if isinstance(bz, int) and bz == 0:
                        pe.wait_ge(setup_p, 3)
                    pe.wait_ge(zv, n(bz, ZV, "M"))
                    po = p_z[:, 32:32 + 2 * E]
                    t.matmul(po[:, 0:E], trib[:, :], mb[:, 0, :], start=True, stop=True)
                    t.matmul(po[:, E:2 * E], onesb[:, :], mb[:, 0, :], start=True, stop=False)
                    t.matmul(po[:, E:2 * E], trib[:, :], mb[:, 1, :], start=False, stop=True).then_inc(zt, 1)

                def ctx_t():
                    pe.wait_ge(yv, n(bw, YV, "cn"))
                    if since(bw, 1):
                        pe.wait_ge(wv, prev(bw, WV, "res"))
                        pe.wait_ge(wa, prev(bw, WA, "cT"))
                    for h in range(2):
                        ins = t.transpose(p_y[:, h * P:(h + 1) * P], cn[:, h, :], ident[:, :])
                    ins.then_inc(wt, 1)

                def proj():
                    pe.wait_ge(wa, n(bw, WA, "cT"))
                    for h in range(2):
                        o_ = p_y[:, (2 + h) * C:(3 + h) * C]
                        t.matmul(o_, cT[:, h, :], wo32[:, :], start=True, stop=False)
                        ins = t.matmul(o_, onesb[:, :], bias3[:, 3 * C:4 * C], start=False, stop=True)
                    ins.then_inc(wt, 1)

                def state():
                    pe.wait_ge(xa, n(b, XA, "vh0"))
                    pe.wait_ge(xp, n(b, XP, "vl0"))
                    if since(b, 1):
                        pe.wait_ge(yv, prev(b, YV, "cn"))
                    for j in range(J):
                        for part, vv in ((0, vh), (1, vl)):
                            ins = t.matmul(
                                p_state[:, j * R * DV:(j + 1) * R * DV],
                                stack[:, par, 0, 1, 32 * j:32 * j + 32, :, :].rearrange("p c a d -> p (c a d)"),
                                vv[:, par, 0, j * R:(j + 1) * R, :].rearrange("p r e -> p (r e)"),
                                start=(part == 0), stop=(part == 1))
                    ins.then_inc(yt, 1)

                def scores(h, r):
                    pe.wait_ge(xa, n(b, XA, f"T{h}"))
                    if h or r > 1:
                        pe.wait_ge(yv, n(b, YV, f"am{h}{r - 2}" if r > 1 else f"am0{r + 2}"))
                    elif since(b, 1):
                        pe.wait_ge(yv, prev(b, YV, f"am1{r + 2}"))
                    for j in range(J):
                        ins = t.matmul(p_sc[r % 2][:, j * P:(j + 1) * P], qkT[32 * r:32 * r + 32, par, h, 1, j, :],
                                       qkT[32 * r:32 * r + 32, par, h, 0, j, :], start=True, stop=True)
                    ins.then_inc(yt, 1)

                def context(h, r):
                    low, steps = low_of(h, r)
                    pe.wait_ge(ya, n(b, YA, f"hi{h}{r}"))
                    pe.wait_ge(low, n(b, steps, f"lo{h}{r}"))
                    pe.wait_ge(xa, n(b, XA, f"vh{h}"))
                    pe.wait_ge(xp, n(b, XP, f"vl{h}"))
                    if h == 0 and r == 0:
                        pe.wait_ge(yv, n(b, YV, "s32"))
                    for j in range(J):
                        hd = j * R + r
                        o_ = p_ctx[:, h, hd * DV:(hd + 1) * DV]
                        first = h == 0 and r == 0 and j == 0
                        hi, lo = am_hl[:, 0, r, j, :], am_hl[:, 1, r, j, :]
                        t.matmul(o_, hi, vh[:, par, h, hd, :], start=first, stop=False, skip_group_check=True)
                        t.matmul(o_, hi, vl[:, par, h, hd, :], start=False, stop=False, skip_group_check=True)
                        ins = t.matmul(o_, lo, vh[:, par, h, hd, :], start=False, stop=(h == 0),
                                       skip_group_check=True)
                    ins.then_inc(yt, 1)

                def context_state():
                    pe.wait_ge(ya, n(b, YA, "shi"))
                    pe.wait_ge(yp, n(b, YP, "slo"))
                    pe.wait_ge(xa, n(b, XA, "T1"))
                    for part, s in ((0, sh), (1, sl)):
                        for j in range(J):
                            ins = t.matmul(p_ctx[:, 1, j * R * DV:(j + 1) * R * DV], qkT[:, par, 1, 0, j, :],
                                           s[:, j, :], start=False, stop=(part == 1), skip_group_check=True)
                    ins.then_inc(yt, 1)

                def dispatch(part, q):
                    if part == "i":
                        pe.wait_ge(zv, n(bd, ZV, "D1"))
                        pe.wait_ge(zp, n(bd, ZP, "pl"))
                        if q:
                            pe.wait_ge(dv, n(bd, DI, "i0"))
                        elif since(bd, 1):
                            pe.wait_ge(da, prev(bd, DA, "l1"))
                    elif part == "h":
                        if q:
                            pe.wait_ge(da, n(bd, DA, "h0"))
                        else:
                            pe.wait_ge(dv, n(bd, DI, "i1"))
                            pe.wait_ge(za, n(bd, ZA, "x1h"))
                    else:
                        pe.wait_ge(da, n(bd, DA, "l0" if q else "h1"))
                        pe.wait_ge(zp, n(bd, ZP, "x1l"))
                    m = NAUX if part == "i" else C
                    src = {"i": aux, "h": x1h, "l": x1l}[part]
                    for h in range(2):
                        ins = t.matmul(p_d[0:m, 0:HALF], src[:, o, h, :],
                                       onehot[:, h, 4 * q:4 * q + 4, :].rearrange("p e c -> p (e c)"),
                                       start=(h == 0), stop=(h == 1))
                    ins.then_inc(dt, 1)

                if do_y:
                    scores(0, 0)
                    scores(0, 1)
                if do_d:
                    dispatch("i", 0)
                if do_w:
                    ctx_t()
                if do_y:
                    scores(0, 2)
                if do_z:
                    x1_t()
                if do_y:
                    scores(0, 3)
                    state()
                if do_d:
                    dispatch("i", 1)
                if do_y:
                    scores(1, 0)
                if do_z:
                    router()
                if do_y:
                    context(0, 0)
                    scores(1, 1)
                    context(0, 1)
                    scores(1, 2)
                if do_d:
                    dispatch("h", 0)
                if do_y:
                    scores(1, 3)
                if do_x:
                    qkv(bx, 0)
                if do_d:
                    dispatch("h", 1)
                if do_w:
                    proj()
                if do_y:
                    context(0, 3)
                    context(0, 2)
                if do_z:
                    positions()
                if do_x:
                    qkv(bx, 1)
                if do_y:
                    context(1, 0)
                if do_d:
                    dispatch("l", 0)
                if do_y:
                    context(1, 1)
                if do_d:
                    dispatch("l", 1)
                if do_x:
                    transposes(bx, 0, o)
                if do_y:
                    context(1, 3)
                    context(1, 2)
                    context_state()
                if do_x:
                    transposes(bx, 1, o)

            slots_a(pe, slot)

            pe.wait_ge(da, n(B - 1, DA, "l1"))
            pe.wait_ge(dv, n(B - 1, DI, "i1"))
            pe.wait_ge(wa, n(B - 1, WA, "x11"))

            def info(e, par, nb):
                pe.wait_ge(rows_loaded, e * 16 + 16)
                pe.wait_ge(gate_v, nb * FK + 2)
                for s in range(NT):
                    ins = t.matmul(p_info[:, 3 * s:3 * s + 3], rows_in[:, par, s * P:(s + 1) * P], sel[0:NAUX, :],
                                   start=True, stop=True)
                ins.then_inc(info_t, 1)

            def up(e, nb, par, c, first):
                for k in range(FK):
                    if k == 3 or not first:
                        pe.wait_ge(gate_v, nb * FK + (0, -2, -1, 1)[k])
                    if k == 1 and c == 1:
                        pe.wait_ge(info_v, e * 5 + 5)
                    for bk, w0 in zip(UP[k], (k * P, (3 + k) * P) if k < 3 else (6 * P,)):
                        o_ = bk[:, :]
                        xs = bass.ds(c * CH, CH)
                        rh = xdh[:, bass.ds(e, 1), xs].rearrange("p o s -> p (o s)")
                        rl = xdl[:, bass.ds(e, 1), xs].rearrange("p o s -> p (o s)")
                        t.matmul(o_, wh[:, par, w0:w0 + P], rh, start=True, stop=False)
                        t.matmul(o_, wh[:, par, w0:w0 + P], rl, start=False, stop=False)
                        ins = t.matmul(o_, wl[:, par, w0:w0 + P], rh, start=False, stop=True)
                    ins.then_inc(up_t, 1)

            def down(nb, par, cpar, first):
                pe.wait_ge(gl_v, nb * FK + FK)
                if not first:
                    pe.wait_ge(eo_v, nb - 1)
                for s in range(SUB):
                    o_ = DOWN[cpar][:, s * C:(s + 1) * C]
                    ss = slice(s * P, (s + 1) * P)
                    for k in range(FK - 1):
                        w = slice(2 * F + k * C, 2 * F + (k + 1) * C)
                        t.matmul(o_, gh[:, cpar, k, ss], wh[:, par, w], start=(k == 0), stop=False)
                        t.matmul(o_, gh[:, cpar, k, ss], wl[:, par, w], start=False, stop=False)
                        t.matmul(o_, gl[:, cpar, k, ss], wh[:, par, w], start=False, stop=False)
                    w = slice(2 * F + (FK - 1) * C, 2 * F + FK * C)
                    t.matmul(o_, gh[:, cpar, FK - 1, ss], wh[:, par, w], start=False, stop=False)
                    ins = t.matmul(o_, gh[0:FT, cpar, FK - 1, ss], wl[0:FT, par, w], start=False, stop=True)
                ins.then_inc(down_t, 1)

            def experts(i, first):
                for q in range(2 * NCH):
                    par, c, cpar = q // NCH, q % NCH, q % 2
                    nb = i * (2 * NCH) + q
                    if c == 0:
                        pe.wait_ge(w_split_l, i * 2 + par + 1)
                    up(i * 2 + par, nb, par, c, first and q == 0)
                    if c == 0:
                        info(i * 2 + par, par, nb)
                    if q or not first:
                        pq = (q - 1) % (2 * NCH)
                        down(nb - 1, pq // NCH, pq % 2, first and pq < 2)

            experts(0, True)
            with pe.Fori(1, E // 2) as i:
                experts(i, False)
            down(E * NCH - 1, 1, 1, False)



def kernel(**inputs):
    import numpy as np

    import concourse.bacc as bacc
    from concourse import mybir
    from concourse.bass_utils import run_bass_kernel_spmd

    fp32 = mybir.dt.float32
    x = np.asarray(inputs["L0_attn_x"])
    nb, t, c = x.shape
    x2 = np.ascontiguousarray(x.reshape(nb * t, c))
    arrays = {
        "x": x2,
        "x_t": np.ascontiguousarray(x2.T),
        "wqkv_t": np.ascontiguousarray(np.asarray(inputs["L0_attn_w_qkv"]).T),
        "bqkv": np.ascontiguousarray(np.asarray(inputs["L0_attn_b_qkv"]).reshape(1, -1)),
        "wout_t": np.ascontiguousarray(np.asarray(inputs["L0_attn_w_out"]).T),
        "bout": np.ascontiguousarray(np.asarray(inputs["L0_attn_b_out"]).reshape(1, -1)),
        "gate_t": np.ascontiguousarray(np.asarray(inputs["L0_ffn_gate_w"]).T),
        "w1": np.ascontiguousarray(np.asarray(inputs["L0_ffn_w1"])),
        "w2": np.ascontiguousarray(np.asarray(inputs["L0_ffn_w2"])),
        "w3": np.ascontiguousarray(np.asarray(inputs["L0_ffn_w3"])),
    }
    nc = bacc.Bacc("TRN2", target_bir_lowering=False, num_devices=1)
    aps = [nc.dram_tensor(k, a.shape, fp32, kind="ExternalInput").ap() for k, a in arrays.items()]
    e = arrays["w1"].shape[0]
    cap = int(t * 2 / e * 1.25)
    acc = nc.dram_tensor("acc", (nb * t + nb * cap, c), fp32, kind="Internal").ap()
    slot_rows = nc.dram_tensor("slot_rows", (e, 3 * e + 2, nb * cap), mybir.dt.bfloat16, kind="Internal").ap()
    out = nc.dram_tensor("out", (nb * t, c), fp32, kind="ExternalOutput").ap()
    build(nc, *aps, acc, slot_rows, out)
    r = run_bass_kernel_spmd(nc, [arrays], core_ids=[0])
    return np.asarray(r.results[0]["out"]).reshape(nb, t, c)
```
